# Optimizing a Trainium2 kernel written in Bass

```python
import numpy as np
import jax
import jax.numpy as jnp

def _softmax(x, axis=-1):
    return jax.nn.softmax(x, axis=axis)

def _gelu(x):
    return jax.nn.gelu(x, approximate=True)

def _silu(x):
    return jax.nn.silu(x)

def _sigmoid(x):
    return jax.nn.sigmoid(x)

def _layernorm(x, axis=-1, eps=1e-05):
    m = jnp.mean(x, axis=axis, keepdims=True)
    v = jnp.var(x, axis=axis, keepdims=True)
    return (x - m) / jnp.sqrt(v + eps)

def _scatter_add(tgt, idx, src, axis=0):
    return tgt.at[idx].add(src)

def _segment_sum(src, seg, n):
    return jax.ops.segment_sum(src, seg, n)
kernel_name = 'mk_flamingo_gated_d2_seqx_r8_efc03c'

def setup_inputs(seed: int=0):
    np.random.seed(seed)
    _w = jnp.asarray

    def _rec_inputs():
        import jax
        import jax.numpy as jnp
        _rk = jax.random.key(seed)
        x = -0.0002928 + 1 * jax.random.normal(jax.random.fold_in(_rk, 1), (32, 128, 128), jnp.float32)
        _lenS = 128 - jax.random.randint(jax.random.fold_in(_rk, 7), (32,), 0, max(1, 128 // 4) + 1, jnp.int32)
        _lenS2 = 120 - jax.random.randint(jax.random.fold_in(_rk, 8), (32,), 0, max(1, 120 // 4) + 1, jnp.int32)
        _ctx_1024P = jax.random.normal(jax.random.fold_in(_rk, 11), (32, 16, 128), jnp.float32)
        _ctx_1024c = jax.random.dirichlet(jax.random.fold_in(_rk, 511), 0.3 * jnp.ones((16,), jnp.float32), (32, 120))
        _ctx_1024t = jnp.einsum('bsk,bkd->bsd', _ctx_1024c, _ctx_1024P)
        _ctx_1024t = _ctx_1024t * jax.lax.rsqrt(jnp.mean(jnp.square(_ctx_1024t)) + 1e-12) * 0.953939
        ctx_1024 = -1.39393e-06 + 0.999914 * (_ctx_1024t + 0.3 * jax.random.normal(jax.random.fold_in(_rk, 611), (32, 120, 128), jnp.float32))
        fside_Bx16xSxS2_0 = -3.27644e-05 + 1.00007 * jax.random.normal(jax.random.fold_in(_rk, 13), (32, 16, 128, 120), jnp.float32)
        _validS = jnp.arange(128)[None, :] < _lenS[:, None]
        _validS2 = jnp.arange(120)[None, :] < _lenS2[:, None]
        _causal = jnp.tril(jnp.ones((128, 128), dtype=bool))
        mask_Bx1xSxS2_ik1 = jnp.where(jnp.broadcast_to(_validS2[:, None, None, :], (32, 1, 128, 120)), 1, 0).astype(jnp.int32)
        _g = jax.random.normal(jax.random.fold_in(_rk, 9001), (2, 2), jnp.float32)
        _g = jnp.sign(_g) * jnp.maximum(jnp.abs(_g), 1.0) + (_g == 0) * 1.0
        g_xattn = _g[0]
        g_ffn = _g[1]
        return (x, ctx_1024, fside_Bx16xSxS2_0, mask_Bx1xSxS2_ik1, g_xattn, g_ffn)
    x, ctx_1024, fside_Bx16xSxS2_0, mask_Bx1xSxS2_ik1, g_xattn, g_ffn = _rec_inputs()

    def _L0_xattn_setup():
        import jax, jax.numpy as jnp
        import numpy as np
        DIM = 128
        NUM_HEADS = 16
        HEAD_DIM = DIM // NUM_HEADS
        SCALE = HEAD_DIM ** (-0.5)
        key = jax.random.key(seed)
        ks = jax.random.split(key, 13)
        B, L, S = (2, 256, 256)
        inp = {'query': jax.random.normal(ks[0], (B, L, DIM), jnp.float32), 'key': jax.random.normal(ks[1], (B, S, DIM), jnp.float32), 'value': jax.random.normal(ks[2], (B, S, DIM), jnp.float32), 'mask': jax.random.randint(ks[3], (B, 1, L, S), 0, 2, jnp.int32), 'attn_bias': jax.random.normal(ks[4], (B, NUM_HEADS, L, S), jnp.float32), 'Wq': jax.random.normal(ks[5], (DIM, DIM), jnp.float32) * DIM ** (-0.5), 'bq': jax.random.normal(ks[6], (DIM,), jnp.float32) * 0.02, 'Wk': jax.random.normal(ks[7], (DIM, DIM), jnp.float32) * DIM ** (-0.5), 'bk': jax.random.normal(ks[8], (DIM,), jnp.float32) * 0.02, 'Wv': jax.random.normal(ks[9], (DIM, DIM), jnp.float32) * DIM ** (-0.5), 'bv': jax.random.normal(ks[10], (DIM,), jnp.float32) * 0.02, 'Wo': jax.random.normal(ks[11], (DIM, DIM), jnp.float32) * DIM ** (-0.5), 'bo': jax.random.normal(ks[12], (DIM,), jnp.float32) * 0.02}
        return inp
    _L0_xattn_all = _L0_xattn_setup()
    _L0_xattn_in = {k: v for k, v in _L0_xattn_all.items() if k in ('Wq', 'bq', 'Wk', 'bk', 'Wv', 'bv', 'Wo', 'bo')}
    del _L0_xattn_all

    def _L0_ffn_setup():
        import jax, jax.numpy as jnp
        import numpy as np
        EPS = 1e-08

        def _ternary_linear(x, w):
            alpha = jnp.mean(jnp.abs(w))
            w_t = jnp.sign(w) * (jnp.abs(w) > 0.5 * alpha).astype(w.dtype)
            w_q = w + jax.lax.stop_gradient(w_t - w)
            d = x.shape[-1]
            rms = jnp.sqrt(jnp.sum(x * x, axis=-1, keepdims=True)) / jnp.sqrt(jnp.asarray(d, x.dtype))
            x_norm = x / (rms + EPS)
            return jnp.einsum('bsd,fd->bsf', x_norm, w_q)
        key = jax.random.key(seed)
        k1, k2, k3 = jax.random.split(key, 3)
        d_model, d_ff = (128, 512)
        B, S = (4, 512)
        x = jax.random.normal(k1, (B, S, d_model), dtype=jnp.float32)
        w_up = jax.random.normal(k2, (d_ff, d_model), dtype=jnp.float32) * 0.02
        w_down = jax.random.normal(k3, (d_model, d_ff), dtype=jnp.float32) * 0.02
        return {'x': x, 'w_up': w_up, 'w_down': w_down}
    _L0_ffn_all = _L0_ffn_setup()
    _L0_ffn_in = {k: v for k, v in _L0_ffn_all.items() if k in ('w_up', 'w_down')}
    del _L0_ffn_all

    def _L1_xattn_setup():
        import jax, jax.numpy as jnp
        import numpy as np
        HEADS = 16
        DIM_HEAD = 64
        QUERY_DIM = 128
        INNER = HEADS * DIM_HEAD
        SCALE = DIM_HEAD ** (-0.5)
        key = jax.random.key(seed)
        ks = jax.random.split(key, 6)
        B, N, M = (2, 256, 256)
        x = jax.random.normal(ks[0], (B, N, QUERY_DIM), dtype=jnp.float32)
        context = jax.random.normal(ks[1], (B, M, QUERY_DIM), dtype=jnp.float32)
        s = QUERY_DIM ** (-0.5)
        Wq = jax.random.normal(ks[2], (QUERY_DIM, INNER), dtype=jnp.float32) * s
        Wk = jax.random.normal(ks[3], (QUERY_DIM, INNER), dtype=jnp.float32) * s
        Wv = jax.random.normal(ks[4], (QUERY_DIM, INNER), dtype=jnp.float32) * s
        Wo = jax.random.normal(ks[5], (INNER, QUERY_DIM), dtype=jnp.float32) * INNER ** (-0.5)
        return {'x': x, 'context': context, 'Wq': Wq, 'Wk': Wk, 'Wv': Wv, 'Wo': Wo}
    _L1_xattn_all = _L1_xattn_setup()
    _L1_xattn_in = {k: v for k, v in _L1_xattn_all.items() if k in ('Wq', 'Wk', 'Wv', 'Wo')}
    del _L1_xattn_all

    def _L1_ffn_setup():
        import jax, jax.numpy as jnp
        import numpy as np
        D_MODEL = 128
        MLP_DIM = 512
        N_EXPERTS = 8
        B, T = (4, 128)
        key = jax.random.key(seed)
        ks = jax.random.split(key, 7)
        scale_in = (1.0 / D_MODEL) ** 0.5
        scale_out = (1.0 / MLP_DIM) ** 0.5
        bound_g = (1.0 / D_MODEL) ** 0.5
        w_gate = jax.random.uniform(ks[0], (D_MODEL, N_EXPERTS), minval=-bound_g, maxval=bound_g, dtype=jnp.float32)
        b_gate = jax.random.uniform(ks[1], (N_EXPERTS,), minval=-bound_g, maxval=bound_g, dtype=jnp.float32)
        W1 = jax.random.uniform(ks[2], (N_EXPERTS, D_MODEL, MLP_DIM), minval=-scale_in, maxval=scale_in, dtype=jnp.float32)
        b1 = jnp.zeros((N_EXPERTS, MLP_DIM), dtype=jnp.float32)
        W2 = jax.random.uniform(ks[3], (N_EXPERTS, MLP_DIM, D_MODEL), minval=-scale_out, maxval=scale_out, dtype=jnp.float32)
        b2 = jnp.zeros((N_EXPERTS, D_MODEL), dtype=jnp.float32)
        x = jax.random.normal(ks[4], (B, T, D_MODEL), dtype=jnp.float32)
        return {'x': x, 'w_gate': w_gate, 'b_gate': b_gate, 'W1': W1, 'b1': b1, 'W2': W2, 'b2': b2}
    _L1_ffn_all = _L1_ffn_setup()
    _L1_ffn_in = {k: v for k, v in _L1_ffn_all.items() if k in ('w_gate', 'b_gate', 'W1', 'b1', 'W2', 'b2')}
    del _L1_ffn_all
    return {'x': x, 'ctx_1024': ctx_1024, 'fside_Bx16xSxS2_0': fside_Bx16xSxS2_0, 'mask_Bx1xSxS2_ik1': mask_Bx1xSxS2_ik1, 'g_xattn': g_xattn, 'g_ffn': g_ffn, 'L0_xattn_Wq': _L0_xattn_in['Wq'], 'L0_xattn_bq': _L0_xattn_in['bq'], 'L0_xattn_Wk': _L0_xattn_in['Wk'], 'L0_xattn_bk': _L0_xattn_in['bk'], 'L0_xattn_Wv': _L0_xattn_in['Wv'], 'L0_xattn_bv': _L0_xattn_in['bv'], 'L0_xattn_Wo': _L0_xattn_in['Wo'], 'L0_xattn_bo': _L0_xattn_in['bo'], 'L0_ffn_w_up': _L0_ffn_in['w_up'], 'L0_ffn_w_down': _L0_ffn_in['w_down'], 'L1_xattn_Wq': _L1_xattn_in['Wq'], 'L1_xattn_Wk': _L1_xattn_in['Wk'], 'L1_xattn_Wv': _L1_xattn_in['Wv'], 'L1_xattn_Wo': _L1_xattn_in['Wo'], 'L1_ffn_w_gate': _L1_ffn_in['w_gate'], 'L1_ffn_b_gate': _L1_ffn_in['b_gate'], 'L1_ffn_W1': _L1_ffn_in['W1'], 'L1_ffn_b1': _L1_ffn_in['b1'], 'L1_ffn_W2': _L1_ffn_in['W2'], 'L1_ffn_b2': _L1_ffn_in['b2']}

def reference(x, ctx_1024, fside_Bx16xSxS2_0, mask_Bx1xSxS2_ik1, g_xattn, g_ffn, L0_xattn_Wq, L0_xattn_bq, L0_xattn_Wk, L0_xattn_bk, L0_xattn_Wv, L0_xattn_bv, L0_xattn_Wo, L0_xattn_bo, L0_ffn_w_up, L0_ffn_w_down, L1_xattn_Wq, L1_xattn_Wk, L1_xattn_Wv, L1_xattn_Wo, L1_ffn_w_gate, L1_ffn_b_gate, L1_ffn_W1, L1_ffn_b1, L1_ffn_W2, L1_ffn_b2):
    import jax
    import jax.numpy as jnp

    def _L0_xattn_ref(query, key, value, mask, attn_bias, Wq, bq, Wk, bk, Wv, bv, Wo, bo):
        import jax, jax.numpy as jnp
        import numpy as np
        DIM = 128
        NUM_HEADS = 16
        HEAD_DIM = DIM // NUM_HEADS
        SCALE = HEAD_DIM ** (-0.5)
        B, L, _ = query.shape
        S = key.shape[1]
        H, D = (NUM_HEADS, HEAD_DIM)
        q = (query @ Wq + bq).reshape(B, L, H, D).transpose(0, 2, 1, 3)
        k = (key @ Wk + bk).reshape(B, S, H, D).transpose(0, 2, 1, 3)
        v = (value @ Wv + bv).reshape(B, S, H, D).transpose(0, 2, 1, 3)
        scores = jnp.einsum('bhld,bhsd->bhls', q, k) * SCALE + attn_bias
        scores = jnp.where(mask == 0, -jnp.inf, scores)
        probs = jax.nn.softmax(scores, axis=-1)
        out = jnp.einsum('bhls,bhsd->bhld', probs, v)
        out = out.transpose(0, 2, 1, 3).reshape(B, L, DIM)
        return out @ Wo + bo

    def _L0_ffn_ref(x, w_up, w_down):
        import jax, jax.numpy as jnp
        import numpy as np
        EPS = 1e-08

        def _ternary_linear(x, w):
            alpha = jnp.mean(jnp.abs(w))
            w_t = jnp.sign(w) * (jnp.abs(w) > 0.5 * alpha).astype(w.dtype)
            w_q = w + jax.lax.stop_gradient(w_t - w)
            d = x.shape[-1]
            rms = jnp.sqrt(jnp.sum(x * x, axis=-1, keepdims=True)) / jnp.sqrt(jnp.asarray(d, x.dtype))
            x_norm = x / (rms + EPS)
            return jnp.einsum('bsd,fd->bsf', x_norm, w_q)
        h = jax.nn.gelu(_ternary_linear(x, w_up), approximate=False)
        return _ternary_linear(h, w_down)

    def _L1_xattn_ref(x, context, Wq, Wk, Wv, Wo):
        import jax, jax.numpy as jnp
        import numpy as np
        HEADS = 16
        DIM_HEAD = 64
        QUERY_DIM = 128
        INNER = HEADS * DIM_HEAD
        SCALE = DIM_HEAD ** (-0.5)
        B, N, _ = x.shape
        M = context.shape[1]
        q = (x @ Wq).reshape(B, N, HEADS, DIM_HEAD)
        k = (context @ Wk).reshape(B, M, HEADS, DIM_HEAD)
        v = (context @ Wv).reshape(B, M, HEADS, DIM_HEAD)
        sim = jnp.einsum('bihd,bjhd->bhij', q, k) * SCALE
        attn = jax.nn.softmax(sim, axis=-1)
        out = jnp.einsum('bhij,bjhd->bihd', attn, v)
        out = out.reshape(B, N, INNER)
        return out @ Wo

    def _L1_ffn_ref(x, w_gate, b_gate, W1, b1, W2, b2):
        import jax, jax.numpy as jnp
        import numpy as np
        D_MODEL = 128
        MLP_DIM = 512
        N_EXPERTS = 8
        B, T = (4, 128)
        b, t, d = x.shape
        x_flat = x.reshape(b * t, d)
        logits = x_flat @ w_gate + b_gate
        probs = jax.nn.softmax(logits, axis=-1)
        route_p = jnp.max(probs, axis=-1)
        route_idx = jnp.argmax(probs, axis=-1)
        h = jnp.einsum('nd,edm->enm', x_flat, W1) + b1[:, None, :]
        h = jax.nn.relu(h)
        y = jnp.einsum('enm,emd->end', h, W2) + b2[:, None, :]
        n = b * t
        out = y[route_idx, jnp.arange(n)] * route_p[:, None]
        return out.reshape(b, t, d)
    x = x + jnp.tanh(g_xattn[0]) * _L0_xattn_ref(_layernorm(x, axis=-1), ctx_1024, ctx_1024, mask_Bx1xSxS2_ik1, fside_Bx16xSxS2_0, L0_xattn_Wq, L0_xattn_bq, L0_xattn_Wk, L0_xattn_bk, L0_xattn_Wv, L0_xattn_bv, L0_xattn_Wo, L0_xattn_bo)
    x = x + jnp.tanh(g_ffn[0]) * _L0_ffn_ref(_layernorm(x, axis=-1), L0_ffn_w_up, L0_ffn_w_down)
    x = x + jnp.tanh(g_xattn[1]) * _L1_xattn_ref(_layernorm(x, axis=-1), ctx_1024, L1_xattn_Wq, L1_xattn_Wk, L1_xattn_Wv, L1_xattn_Wo)
    x = x + jnp.tanh(g_ffn[1]) * _L1_ffn_ref(_layernorm(x, axis=-1), L1_ffn_w_gate, L1_ffn_b_gate, L1_ffn_W1, L1_ffn_b1, L1_ffn_W2, L1_ffn_b2)
    return x

_drawn_inputs = setup_inputs


def setup_inputs(seed=0):
    import zlib

    import numpy as np

    out = dict(_drawn_inputs(seed))
    spreads = {'g_ffn': (-1.0, 0.6), 'L1_ffn_b1': (0.0, 0.8), 'L1_ffn_b2': (0.0, 0.8)}
    factors = {'L0_xattn_bq': 8.0,
     'L0_xattn_bk': 8.0,
     'L0_xattn_bv': 3.255,
     'L0_xattn_bo': 4.73,
     'L1_xattn_Wq': 4.081,
     'L1_xattn_Wk': 4.025,
     'L1_ffn_w_gate': 8.0,
     'L1_ffn_b_gate': 8.0,
     'L1_ffn_W1': 8.0,
     'L1_ffn_W2': 8.0}
    for name, (base, spread) in spreads.items():
        noise = np.random.default_rng([zlib.crc32(name.encode()), seed]).standard_normal(out[name].shape)
        drawn = base * np.exp(spread * noise) if base else spread * noise
        out[name] = jnp.asarray(drawn.astype(out[name].dtype))
    for name, factor in factors.items():
        out[name] = (out[name] * factor).astype(out[name].dtype)
    return out
```

```python
from contextlib import ExitStack

import concourse.bass as bass
from concourse import mybir

F32 = mybir.dt.float32
BF16 = mybir.dt.bfloat16
I32 = mybir.dt.int32
ALU = mybir.AluOpType
ACT = mybir.ActivationFunctionType
AX_X = mybir.AxisListType.X

H = 16
HB = 4
NB = H // HB
LN_EPS = 1e-5
RMS_EPS = 1e-8
MASKED = -1.0e30


def at_least(eng, sem, value):
    if not isinstance(value, int) or value > 0:
        eng.wait_ge(sem, value)


def skewed(eng, n, body):
    body(0, 0, 0, True, False)
    body(1, 0, 1, True, True)
    with eng.Fori(1, n // 2 - 1) as pair:
        body(pair * 2, pair, 0, True, True)
        body(pair * 2 + 1, pair, 1, True, True)
    body(n - 2, n // 2 - 1, 0, True, True)
    body(n - 1, n // 2 - 1, 1, True, True)
    body(n, n // 2, 0, False, True)


def skewed_slots(eng, n, body):
    body(0, 0, 0, 0, True, False)
    body(1, 0, 1, 1, True, True)
    turns = (n - 3) // 4
    with eng.Fori(0, turns) as turn:
        for k in range(2, 6):
            body(turn * 4 + k, turn + k // 4, k % 4, k % 2, True, True)
    for it in range(2 + 4 * turns, n):
        body(it, it // 4, it % 4, it % 2, True, True)
    body(n, n // 4, n % 4, n % 2, False, True)


def build(nc, x, ctx_in, bias, mask, g_xattn, g_ffn, Wq0, bq0, Wk0, bk0, Wv0, bv0, Wo0, bo0, w_up, w_down,
          Wq1, Wk1, Wv1, Wo1, w_gate, b_gate, W1, b1, W2, b2, out):
    B, L, D = x.shape
    S = ctx_in.shape[1]
    HD0 = Wq0.shape[1] // H
    HD1 = Wq1.shape[1] // H
    F = w_up.shape[0]
    FC = F // 128
    assert L == 128 and D == 128 and S <= 128 and B % 2 == 0 and HD0 <= 32 and HD1 == 64
    SCALE0 = HD0 ** -0.5
    SCALE1 = HD1 ** -0.5
    V0W = HD0 + 1
    V1W = HD1 + 1
    C1 = H * HD1 // 128
    E, _, M = W1.shape
    MC = M // 128
    NT = B * L
    BLOCKS = NT // 128 + E - 1
    GATE, TOKEN, REC = 2 * D, 2 * D + 1, 2 * D + 2

    stack = ExitStack()
    with stack:
        def sb(name, shape, dt=F32):
            return stack.enter_context(nc.sbuf_tensor(name, shape, dt))

        def sem(name):
            return stack.enter_context(nc.semaphore(name))

        bank = [stack.enter_context(nc.psum_tensor(f"bank{i}", [128, 512], F32)) for i in range(8)]

        ident = sb("ident", [128, 128])
        ident_bf = sb("ident_bf", [128, 128], BF16)
        ones = sb("ones", [128, 128])
        gates = sb("gates", [128, 4])
        tg = sb("tg", [128, 4])
        wq0_raw = sb("wq0_raw", [D, H * HD0])
        wk0_raw = sb("wk0_raw", [D, H * HD0])
        wq0_pad = sb("wq0_pad", [D, HB, NB, 32])
        wk0_pad = sb("wk0_pad", [D, HB, NB, 32])
        bq0_col = sb("bq0_col", [128, HB])
        bk0_col = sb("bk0_col", [128, HB])
        wv0 = sb("wv0", [D, H * HD0])
        bv0_row = sb("bv0_row", [1, H * HD0])
        wo0 = sb("wo0", [H * HD0, D])
        bo0_row = sb("bo0_row", [1, D])
        up_raw = sb("up_raw", [128, FC, D])
        down_raw = sb("down_raw", [D, F])
        tern_a = sb("tern_a", [128, FC * D])
        tern_b = sb("tern_b", [128, FC * D])
        absum = sb("absum", [128, 2])
        thr = sb("thr", [128, 4])
        upT = sb("upT", [D, F])
        downT = sb("downT", [128, FC, D])
        w2_t = sb("w2_t", [128, E * MC * D])
        wq1_raw = w2_t[:, 0:H * HD1]
        wk1_raw = w2_t[:, H * HD1:2 * H * HD1]
        wq1T = w2_t[:, 2 * H * HD1:3 * H * HD1].rearrange("p (c d) -> p c d", c=C1)
        wk1T = w2_t[:, 3 * H * HD1:4 * H * HD1].rearrange("p (c d) -> p c d", c=C1)
        qk1 = sb("qk1", [D, H, D])
        wv1 = sb("wv1", [D, H * HD1])
        wo1 = sb("wo1", [128, C1, D])

        rec = sb("rec", [L, B, REC])
        xs = rec[:, :, D:2 * D]

        ctx_tok = sb("ctx_tok", [S, 2, D])
        mask_i = sb("mask_i", [L, 2, S], I32)
        mask_b = sb("mask_b", [L, 2, S], BF16)
        w1_t = sb("w1_t", [128, E * M])
        bias_t = w1_t[:, 0:2 * H * S].rearrange("l (p h s) -> l p h s", p=2, h=H)
        stats = sb("stats", [128, 6])
        mv = sb("mv", [128, 2, 2])
        rstd = sb("rstd", [128, 2])
        rms = sb("rms", [128, 6])
        powers = sb("powers", [128, 6])
        settle = sb("settle", [128, 1])
        xn = sb("xn", [L, 2, D])
        xcT = sb("xcT", [D, 2, L + S])
        proj_t = sb("proj_t", [128, H * L])
        qT = proj_t[:, 0:2 * HB * L].rearrange("p (a h l) -> p a h l", a=2, h=HB)
        kT = proj_t[:, 2 * HB * L:2 * HB * (L + S)].rearrange("p (a h s) -> p a h s", a=2, h=HB)
        tT = proj_t[:].rearrange("p (h l) -> p h l", h=H)
        v0 = sb("v0", [S, 2, H, V0W])
        b1_t = sb("b1_t", [128, E * M])
        sc = b1_t[:, 0:2 * H * S].rearrange("l (p h s) -> l p h s", p=2, h=H)
        mx = sb("mx", [L, 2, H])
        work = sb("work", [128, 4096])
        pr = work[:, 0:2 * H * S].rearrange("l (p h s) -> l p h s", p=2, h=H)
        hid = work[:, 0:2 * M].rearrange("l (p m) -> l p m", p=2)
        hidT = work[:, 2 * M:4 * M].rearrange("p (a c l) -> p a c l", a=2, c=MC)
        rows = work[:, 4 * M:4 * M + 4 * REC].rearrange("l (n c) -> l n c", n=4)
        y_out = work[:, 4 * M + 4 * REC:4 * M + 4 * REC + 4 * D].rearrange("l (n d) -> l n d", n=4)
        prT = sb("prT", [S, H, L])
        rden = sb("rden", [L, H])
        o0 = sb("o0", [L, H, HD0])
        o0T = sb("o0T", [H * HD0, L])
        gel = sb("gel", [L, 2, F])
        gel2 = sb("gel2", [L, F])
        ssq = sb("ssq", [L, 2])
        gelT = sb("gelT", [128, 2, FC, L])
        rs2 = sb("rs2", [L, 4])
        rgate = sb("rgate", [L, 2])
        v1 = sb("v1", [S, 2, H, V1W])
        o1 = sb("o1", [L, H * HD1])
        o1T = sb("o1T", [128, C1, L])

        w_gate_t = sb("w_gate_t", [D, E])
        bg_bc = sb("bg_bc", [128, E])
        b1_bc = b1_t[:].rearrange("p (e m) -> p e m", e=E)
        b2_bc = sb("b2_bc", [128, E, D])
        blank = sb("blank", [128, REC])
        experts = sb("experts", [128, B, E])
        before = sb("before", [128, 128])
        before_bf = sb("before_bf", [128, 128], BF16)
        ones_bf = sb("ones_bf", [128, 128], BF16)
        before_e = sb("before_e", [128, E, E])
        block_rows = sb("block_rows", [128, B])
        block_no = sb("block_no", [1, BLOCKS])
        logits = sb("logits", [L, B, E])
        route_a = sb("route_a", [L, B, E])
        route_b = sb("route_b", [L, B, E])
        onehot = sb("onehot", [L, B, E])
        onehot_bf = sb("onehot_bf", [L, E, B], BF16)
        pick = sb("pick", [L, 4, B])
        seq_count = sb("seq_count", [B, E], BF16)
        seq_before = sb("seq_before", [B, B, E], BF16)
        blocks_of = sb("blocks_of", [128, 4, E])
        above = sb("above", [128, E, B])
        block_cmp = sb("block_cmp", [1, BLOCKS, E])
        block_f = sb("block_f", [1, BLOCKS])
        block_e = sb("block_e", [1, BLOCKS], I32)
        place = sb("place", [L, B], I32)
        rowT = sb("rowT", [D, 2, 128])
        y2 = sb("y2", [128, 2, D])
        idle = sb("idle", [128, 1])
        sorted_rows = nc.dram_tensor("sorted_rows", [BLOCKS * 128, REC], F32, kind="Internal").ap()

        w_in = sem("w_in")
        g_in = sem("g_in")
        xc_in = [sem(f"xc_in{p}") for p in range(2)]
        mask_in = [sem(f"mask_in{p}") for p in range(2)]
        bias_in = [[sem(f"bias_in{p}{j}") for j in range(NB)] for p in range(2)]
        ctx1_in = [sem(f"ctx1_in{p}") for p in range(2)]
        late_in = sem("late_in")
        blanked = sem("blanked")
        ro = {n: sem("r_" + n) for n in (
            "stats", "rstd", "ln", "rec", "xT_pe", "xT", "l_pe", "logits", "v", "exp", "pe", "place", "blocks",
            "placed", "tables")}
        ex = {n: sem("m_" + n) for n in ("xT_pe", "xT", "up_pe", "hid", "t_pe", "hidT", "y_pe", "y2", "y", "idle")}
        rows_in = [sem(f"rows_in{n}") for n in range(4)]
        rows_out = [sem(f"rows_out{n}") for n in range(4)]
        zeroed = sem("zeroed")
        chained = sem("chained")
        consts_set = sem("consts_set")
        powers_set = sem("powers_set")
        tanh_set = sem("tanh_set")
        prep_v = sem("prep_v")
        prep_pe = sem("prep_pe")
        prep_a = sem("prep_a")
        weights_set = sem("weights_set")
        a = {n: sem("a_" + n) for n in (
            "ln", "xcT_pe", "xcT", "q_pe", "k_pe", "v_pe", "qk", "v", "s_pe", "biased", "max", "shifted", "exp",
            "mask", "stats", "rstd", "t_pe", "prT", "pv_pe", "rden", "o", "oT_pe", "oT", "y_pe", "x")}
        f = {n: sem("f_" + n) for n in (
            "ln", "xT_pe", "xT", "up_pe", "gel", "sq", "t_pe", "gelT", "stats", "rstd", "chain", "rs2", "chain2", "y_pe", "x")}
        c = {n: sem("c_" + n) for n in (
            "ln", "stats", "rstd", "xcT_pe", "xcT", "t_pe", "t", "v_pe", "v", "s_pe", "max", "shifted", "exp",
            "p_pe", "prT", "pv_pe", "rden", "o", "oT_pe", "oT", "y_pe", "x")}

        def bcast(row, n):
            return row.rearrange("(o d) -> o d", o=1).to_broadcast([n, row.shape[0]])

        block = stack.enter_context(nc.Block())

        @block.sync
        def _(sp):
            def load_seq(it, half, par):
                at_least(sp, a["xcT_pe"], it - 1)
                sp.dma_start(xs[:, bass.ds(it, 1), :].rearrange("l o d -> l (o d)"), x[bass.ds(it, 1), :, :].rearrange("o l d -> (o l) d")).then_inc(xc_in[par], 16)
                sp.dma_start(ctx_tok[:, par, :], ctx_in[bass.ds(it, 1), :, :].rearrange("o s d -> (o s) d")).then_inc(xc_in[par], 16)
                at_least(sp, a["mask"], it - 1)
                sp.dma_start(mask_i[:, par, :], mask[bass.ds(it, 1), 0, :, :].rearrange("o l s -> (o l) s")).then_inc(mask_in[par], 16)
                for j in range(NB):
                    at_least(sp, a["biased"], NB * (it - 2) + j + 1)
                    sp.dma_start(bias_t[:, par, HB * j:HB * j + HB, :],
                                 bias[bass.ds(it, 1), HB * j:HB * j + HB, :, :].rearrange("o h l s -> l (o h) s")
                                 ).then_inc(bias_in[par][j], 16)

            sp.dma_start(wq0_raw[:], Wq0).then_inc(w_in, 16)
            sp.dma_start(wk0_raw[:], Wk0).then_inc(w_in, 16)
            load_seq(0, 0, 0)
            load_seq(1, 0, 1)
            sp.dma_start(wv0[:], Wv0).then_inc(w_in, 16)
            sp.dma_start(wo0[:], Wo0).then_inc(w_in, 16)
            sp.dma_start(bv0_row[:], bv0.rearrange("(o d) -> o d", o=1)).then_inc(w_in, 16)
            sp.dma_start(bo0_row[:], bo0.rearrange("(o d) -> o d", o=1)).then_inc(w_in, 16)
            sp.dma_start(up_raw[:], w_up.rearrange("(c p) d -> p c d", p=128)).then_inc(w_in, 16)
            sp.dma_start(down_raw[:], w_down).then_inc(w_in, 16)
            sp.dma_start(wq1_raw, Wq1).then_inc(w_in, 16)
            sp.dma_start(wk1_raw, Wk1).then_inc(w_in, 16)
            sp.dma_start(wv1[:], Wv1).then_inc(w_in, 16)
            sp.dma_start(wo1[:], Wo1.rearrange("(c p) n -> p c n", p=128)).then_inc(w_in, 16)
            sp.wait_ge(ro["tables"], 2)
            sp.dma_start(sorted_rows.rearrange("(j p) c -> p j c", p=128),
                         blank[:].unsqueeze(1).to_broadcast([128, BLOCKS, REC])).then_inc(blanked, 16)
            with sp.Fori(1, B // 2) as pair:
                load_seq(pair * 2, pair, 0)
                load_seq(pair * 2 + 1, pair, 1)
            sp.dma_start(w_gate_t[:], w_gate).then_inc(late_in, 16)
            sp.dma_start(bg_bc[:], bcast(b_gate, 128)).then_inc(late_in, 16)
            sp.dma_start(b2_bc[:].rearrange("p e d -> p (e d)"), bcast(b2.rearrange("e d -> (e d)"), 128)).then_inc(late_in, 16)
            sp.wait_ge(a["biased"], NB * B)
            sp.dma_start(w1_t[:].rearrange("d (e m) -> d e m", e=E), W1.rearrange("e d m -> d e m")).then_inc(late_in, 16)
            sp.wait_ge(prep_a, 10)
            sp.dma_start(w2_t[:].rearrange("p (e c d) -> p e c d", e=E, c=MC), W2.rearrange("e (c p) d -> p e c d", p=128)
                         ).then_inc(late_in, 16)

            def load_ctx(it, par):
                at_least(sp, c["xcT_pe"], it - 1)
                sp.dma_start(ctx_tok[:, par, :], ctx_in[bass.ds(it, 1), :, :].rearrange("o s d -> (o s) d")).then_inc(ctx1_in[par], 16)

            sp.wait_ge(a["xcT_pe"], B)
            load_ctx(0, 0)
            load_ctx(1, 1)
            with sp.Fori(1, B // 2) as pair:
                load_ctx(pair * 2, 0)
                load_ctx(pair * 2 + 1, 1)
            sp.wait_ge(c["exp"], NB * B)
            sp.dma_start(b1_t[:], bcast(b1.rearrange("e m -> (e m)"), 128)).then_inc(late_in, 16)

            def load_rows(it, use, slot, par, front, back):
                if front:
                    at_least(sp, rows_out[slot], use * 16)
                    sp.wait_ge(ro["placed"], 16 * B)
                    sp.dma_start(rows[:, slot, :],
                                 sorted_rows.rearrange("(j p) c -> j p c", p=128)[bass.ds(it, 1), :, :].rearrange("o p c -> (o p) c")
                                 ).then_inc(rows_in[slot], 16)

            for it in range(4):
                load_rows(it, 0, it, it % 2, True, False)
            with sp.Fori(1, BLOCKS // 4) as turn:
                for k in range(4):
                    load_rows(turn * 4 + k, turn, k, k % 2, True, False)
            for it in range(BLOCKS // 4 * 4, BLOCKS):
                load_rows(it, it // 4, it % 4, it % 2, True, False)

        W_ALL = 16 * 12

        @block.gpsimd
        def _(pool):
            pool.memset(bq0_col[:], 0.0).then_inc(zeroed, 1)
            pool.memset(bk0_col[:], 0.0).then_inc(zeroed, 1)
            pool.wait_ge(zeroed, 2)
            bq_v = bq0.rearrange("(j g d) -> j d g", j=NB, g=HB)
            bk_v = bk0.rearrange("(j g d) -> j d g", j=NB, g=HB)
            with nc.allow_non_contiguous_dma(reason="two 512-byte vectors laid along partitions"):
                for j in range(NB):
                    pool.dma_start(bq0_col[32 * j:32 * j + HD0, :], bq_v[j]).then_inc(g_in, 16)
                    pool.dma_start(bk0_col[32 * j:32 * j + HD0, :], bk_v[j]).then_inc(g_in, 16)
            pool.dma_start(gates[:, 0:2], bcast(g_xattn, 128)).then_inc(g_in, 16)
            pool.dma_start(gates[:, 2:4], bcast(g_ffn, 128)).then_inc(g_in, 16)
            pool.memset(ones[:], 1.0).then_inc(consts_set, 1)
            pool.memset(ident[:], 1.0).then_inc(consts_set, 1)
            pool.memset(ident_bf[:], 1.0).then_inc(consts_set, 1)
            pool.wait_ge(consts_set, 3)
            pool.affine_select(out=ident[:], in_=ident[:], compare_op=ALU.is_equal, fill=0.0, base=0,
                               pattern=[[-1, 128]], channel_multiplier=1).then_inc(consts_set, 1)
            pool.affine_select(out=ident_bf[:], in_=ident_bf[:], compare_op=ALU.is_equal, fill=0.0, base=0,
                               pattern=[[-1, 128]], channel_multiplier=1).then_inc(consts_set, 1)
            for n, power in enumerate((0.5, -0.5, -1.0, LN_EPS, RMS_EPS, 1.0 / F)):
                pool.memset(powers[:, n:n + 1], power).then_inc(powers_set, 1)
            pool.wait_ge(powers_set, 6)
            pool.memset(v0[:], 1.0).then_inc(consts_set, 1)
            pool.memset(v1[:], 1.0).then_inc(consts_set, 1)
            pool.memset(blank[:, 0:TOKEN], 0.0).then_inc(ro["tables"], 1)
            pool.memset(blank[:, TOKEN:REC].bitcast(I32), 1 << 30).then_inc(ro["tables"], 1)
            pool.memset(before[:], 1.0).then_inc(ro["tables"], 1)
            pool.memset(before_e[:], 1.0).then_inc(ro["tables"], 1)
            pool.memset(ones_bf[:], 1.0).then_inc(ro["tables"], 1)
            pool.wait_ge(ro["tables"], 5)
            pool.affine_select(out=before[:], in_=before[:], compare_op=ALU.is_gt, fill=0.0, base=0,
                               pattern=[[1, 128]], channel_multiplier=-1).then_inc(ro["tables"], 1)
            pool.affine_select(out=before_e[:], in_=before_e[:], compare_op=ALU.is_gt, fill=0.0, base=0,
                               pattern=[[1, E], [-1, E]], channel_multiplier=0).then_inc(ro["tables"], 1)
            pool.iota(experts[:], pattern=[[0, B], [1, E]], base=0, channel_multiplier=0,
                      allow_small_or_imprecise_dtypes=True).then_inc(ro["tables"], 1)
            pool.iota(block_rows[:], pattern=[[128, B]], base=0, channel_multiplier=0,
                      allow_small_or_imprecise_dtypes=True).then_inc(ro["tables"], 1)
            pool.iota(block_no[:], pattern=[[1, BLOCKS]], base=0, channel_multiplier=0,
                      allow_small_or_imprecise_dtypes=True).then_inc(ro["tables"], 1)
            pool.iota(rec[:, :, TOKEN:REC].bitcast(I32), pattern=[[128, B]], base=0, channel_multiplier=1
                      ).then_inc(ro["tables"], 1)

            def inv_std(it, par, s):
                pool.wait_ge(s["stats"], 2 * it + 2)
                at_least(pool, s["ln"], it - 1)
                pool.tensor_tensor(rstd[:, par:par + 1], mv[:, par, 1:2], powers[:, 3:4], ALU.add).then_inc(s["rstd"], 1)
                pool.wait_ge(s["rstd"], 2 * it + 1)
                pool.tensor_tensor(rstd[:, par:par + 1], rstd[:, par:par + 1], powers[:, 1:2], ALU.pow
                                   ).then_inc(s["rstd"], 1)

            def shift(it, half, par, front, back):
                if not front:
                    return
                for j in range(NB):
                    if j == 2 and not (isinstance(it, int) and it == B - 1):
                        inv_std(it + 1, 1 - par, a)
                    s = sc[:, par, HB * j:HB * j + HB, :]
                    pool.wait_ge(a["max"], NB * it + j + 1)
                    pool.tensor_tensor(s, s, mx[:, par, HB * j:HB * j + HB].unsqueeze(2).to_broadcast([L, HB, S]),
                                       ALU.subtract).then_inc(a["shifted"], 1)

            inv_std(0, 0, a)
            skewed(pool, B, shift)

            def rms_scales(it, par):
                inv_std(it, par, f)
                pool.wait_ge(f["rstd"], 2 * it + 2)
                pool.tensor_tensor(rms[:, 0:1], mv[:, par, 1:2], powers[:, 0:1], ALU.pow).then_inc(f["chain"], 1)
                pool.wait_ge(f["chain"], 5 * it + 1)
                pool.tensor_tensor(rms[:, 1:2], rms[:, 0:1], rstd[:, par:par + 1], ALU.mult).then_inc(f["chain"], 1)
                pool.wait_ge(f["chain"], 5 * it + 2)
                pool.tensor_tensor(rms[:, 2:3], rms[:, 1:2], powers[:, 4:5], ALU.add).then_inc(f["chain"], 1)
                pool.wait_ge(f["chain"], 5 * it + 3)
                pool.tensor_tensor(rms[:, 3:4], rms[:, 2:3], powers[:, 2:3], ALU.pow).then_inc(f["chain"], 1)
                pool.wait_ge(f["chain"], 5 * it + 4)
                pool.tensor_tensor(rms[:, 4 + par:5 + par], rms[:, 3:4], rstd[:, par:par + 1], ALU.mult
                                   ).then_inc(f["chain"], 1)

            def ffn_scales(it, half, par, front, back):
                if front:
                    if not (isinstance(it, int) and it == B - 1):
                        rms_scales(it + 1, 1 - par)
                    pool.wait_ge(f["sq"], it + 1)
                    at_least(pool, f["x"], it - 1)
                    pool.tensor_tensor(rs2[:, 0:1], ssq[:, par:par + 1], powers[:, 5:6], ALU.mult).then_inc(f["chain2"], 1)
                    pool.wait_ge(f["chain2"], 4 * it + 1)
                    pool.tensor_tensor(rs2[:, 1:2], rs2[:, 0:1], powers[:, 0:1], ALU.pow).then_inc(f["chain2"], 1)
                    pool.wait_ge(f["chain2"], 4 * it + 2)
                    pool.tensor_tensor(rs2[:, 2:3], rs2[:, 1:2], powers[:, 4:5], ALU.add).then_inc(f["chain2"], 1)
                    pool.wait_ge(f["chain2"], 4 * it + 3)
                    pool.tensor_tensor(rs2[:, 3:4], rs2[:, 2:3], powers[:, 2:3], ALU.pow).then_inc(f["chain2"], 1)
                    pool.wait_ge(f["chain2"], 4 * it + 4)
                    pool.tensor_tensor(rgate[:, par:par + 1], rs2[:, 3:4], tg[:, 2:3], ALU.mult).then_inc(f["rs2"], 1)

            pool.wait_ge(tanh_set, 1)
            rms_scales(0, 0)
            skewed(pool, B, ffn_scales)

            def attn1_scales(it, half, par, front, back):
                if front and not (isinstance(it, int) and it == B - 1):
                    inv_std(it + 1, 1 - par, c)

            inv_std(0, 0, c)
            skewed(pool, B, attn1_scales)

            def route_scales(it, half, par, front, back):
                if front and not (isinstance(it, int) and it == B - 1):
                    inv_std(it + 1, 1 - par, ro)

            inv_std(0, 0, ro)
            skewed(pool, B, route_scales)

            pool.wait_ge(ro["place"], 1)
            pool.wait_ge(ro["rec"], B + 1)
            pool.wait_ge(blanked, 16)
            for b in range(B):
                pool.indirect_dma_start(out=sorted_rows, out_offset=bass.IndirectOffsetOnAxis(ap=place[:, b:b + 1], axis=0),
                                        in_=rec[:, b, :], in_offset=None, bounds_check=BLOCKS * 128 - 1, oob_is_err=False
                                        ).then_inc(ro["placed"], 16)

            out_rows = out.rearrange("b l d -> (b l) d")

            def store_rows(it, use, slot, par, front, back):
                if back:
                    g = it - 1
                    gslot = (slot + 3) % 4
                    pool.wait_ge(ex["y"], g + 1)
                    at_least(pool, ex["idle"], g)
                    pool.tensor_tensor(idle[:], powers[:, 0:1], powers[:, 0:1], ALU.add).then_inc(ex["idle"], 1)
                    pool.indirect_dma_start(out=out_rows,
                                            out_offset=bass.IndirectOffsetOnAxis(
                                                ap=rows[:, gslot, TOKEN:REC].bitcast(I32), axis=0),
                                            in_=y_out[:, gslot, :], in_offset=None, bounds_check=NT - 1, oob_is_err=False
                                            ).then_inc(rows_out[gslot], 16)

            skewed_slots(pool, BLOCKS, store_rows)
            for n in range(4):
                pool.wait_ge(rows_out[n], 16 * ((BLOCKS - n + 3) // 4))

        @block.tensor
        def _(pe):
            pe.wait_ge(consts_set, 7)

            def misc(it_par, pos, per_it):
                return bank[6 + (per_it * it_par + pos) % 2]

            def attn0(it, half, par, front, back):
                gpar = 1 - par
                g = it - 1

                def transpose_probs(j):
                    pe.wait_ge(a["exp"], NB * g + j + 1)
                    at_least(pe, a["prT"], NB * g + j - 1)
                    b_ = bank[4 + j % 2]
                    for n in range(HB):
                        mm = pe.transpose(b_[0:S, n * L:n * L + L], pr[:, gpar, HB * j + n, :], ident[:])
                    mm.then_inc(a["t_pe"], 1)

                def scores(j):
                    at_least(pe, a["biased"], NB * (it - 1) + j + 1)
                    if j == 0:
                        pe.wait_ge(a["mask"], it + 1)
                        pe.wait_ge(a["qk"], 2 * it + 2)
                    s = bank[j][:, 0:HB * S]
                    pe.matmul(s.rearrange("p (h s) -> p h s", h=HB), ident_bf[:],
                              mask_b[:, par, :].unsqueeze(1).to_broadcast([L, HB, S]), start=True, stop=False)
                    for n in range(HB):
                        mm = pe.matmul(bank[j][:, n * S:n * S + S], qT[32 * j:32 * j + HD0, par, n, :],
                                       kT[32 * j:32 * j + HD0, par, n, :], start=False, stop=(n == HB - 1))
                    mm.then_inc(a["s_pe"], 1)

                if front:
                    pe.wait_ge(a["ln"], it + 1)
                    pe.wait_ge(xc_in[par], half * 32 + 32)
                    at_least(pe, a["oT"], it - 1)
                    if isinstance(it, int) and it == 1:
                        pe.wait_ge(a["v"], 1)
                        pe.wait_ge(a["qk"], 2)
                    b_ = misc(par, 0, 7)
                    pe.transpose(b_[:, 0:L], xn[:, par, :], ident[:])
                    pe.transpose(b_[:, L:L + S], ctx_tok[:, par, :], ident[0:S, 0:S]).then_inc(a["xcT_pe"], 1)
                if back:
                    at_least(pe, a["pv_pe"], g)
                    transpose_probs(0)
                    transpose_probs(1)
                if front:
                    xT = xcT[:, par, 0:L]
                    cT = xcT[:, par, L:L + S]
                    pe.wait_ge(a["xcT"], it + 1)
                    at_least(pe, a["x"], it - 1)
                    b_ = misc(par, 1, 7)
                    for n in range(HB):
                        mm = pe.matmul(b_[:, n * L:n * L + L], wq0_pad[:, n, :, :].rearrange("p j r -> p (j r)"), xT,
                                       start=(n == 0), stop=(n == HB - 1), skip_group_check=True)
                    mm.then_inc(a["q_pe"], 1)
                    b_ = misc(par, 2, 7)
                    for n in range(HB):
                        mm = pe.matmul(b_[:, n * S:n * S + S], wk0_pad[:, n, :, :].rearrange("p j r -> p (j r)"), cT,
                                       start=(n == 0), stop=(n == HB - 1), skip_group_check=True)
                    mm.then_inc(a["k_pe"], 1)
                    pe.wait_ge(a["qk"], 2 * it + 1)
                    b_ = misc(par, 3, 7)
                    pe.matmul(b_[0:S, 0:H * HD0], cT, wv0[:], start=True, stop=False)
                    pe.matmul(b_[0:S, 0:H * HD0], ones[0:1, 0:S], bv0_row[:], start=False, stop=True).then_inc(a["v_pe"], 1)
                if back:
                    transpose_probs(2)
                    transpose_probs(3)
                if front:
                    scores(0)
                    scores(1)
                if back:
                    pe.wait_ge(a["prT"], NB * g + NB)
                    pe.wait_ge(a["v"], g + 1)
                    b_ = misc(par, 4, 7)
                    for h in range(H):
                        mm = pe.matmul(b_[:, h * V0W:h * V0W + V0W], prT[:, h, :], v0[:, gpar, h, :],
                                       start=(h == 0), stop=(h == H - 1), skip_group_check=True)
                    mm.then_inc(a["pv_pe"], 1)
                if front:
                    scores(2)
                    scores(3)
                if back:
                    pe.wait_ge(a["o"], g + 1)
                    if front:
                        pe.wait_ge(a["v"], it + 1)
                    at_least(pe, a["x"], g)
                    b_ = misc(par, 5, 7)
                    pe.transpose(b_[:, 0:L], o0[:].rearrange("l h d -> l (h d)"), ident[:]).then_inc(a["oT_pe"], 1)
                    pe.wait_ge(a["oT"], g + 1)
                    b_ = misc(par, 6, 7)
                    pe.matmul(b_[:, 0:D], o0T[:], wo0[:], start=True, stop=False)
                    pe.matmul(b_[:, 0:D], ones[0:1, 0:L], bo0_row[:], start=False, stop=True).then_inc(a["y_pe"], 1)

            pe.wait_ge(weights_set, 1)
            skewed(pe, B, attn0)

            pe.wait_ge(a["x"], B)
            pe.matmul(bank[0][:, 0:2], ones[:], absum[:], start=True, stop=True).then_inc(prep_pe, 1)
            pe.wait_ge(prep_v, 12)
            for n in range(FC):
                pe.transpose(bank[1][:, n * 128:n * 128 + 128], tern_a[:, n * D:n * D + D], ident[:])
            for n in range(FC):
                mm = pe.transpose(bank[2][:, n * 128:n * 128 + 128], tern_b[:, n * 128:n * 128 + 128], ident[:])
            mm.then_inc(prep_pe, 1)
            for m, w in enumerate((wq1_raw, wk1_raw)):
                for n in range(C1):
                    mm = pe.transpose(bank[3 + 2 * m + n // 4][:, n % 4 * 128:n % 4 * 128 + 128],
                                      w[:, n * 128:n * 128 + 128], ident[:])
            mm.then_inc(prep_pe, 1)
            pe.wait_ge(prep_a, 6)
            for n in range(C1):
                for r in range(2):
                    mm = pe.matmul(bank[3 + 2 * r + n // 4][:, n % 4 * 128:n % 4 * 128 + 128],
                                   wq1T[64 * r:64 * r + 64, n, :], wk1T[64 * r:64 * r + 64, n, :],
                                   start=(n % 4 == 0), stop=(n % 4 == 3), skip_group_check=True)
            mm.then_inc(prep_pe, 1)
            pe.wait_ge(prep_a, 10)

            def ffn0(it, half, par, front, back):
                gpar = 1 - par
                g = it - 1
                if front:
                    pe.wait_ge(f["ln"], it + 1)
                    at_least(pe, f["xT"], it - 1)
                    pe.transpose(bank[4 + par][:, 0:L], xn[:, par, :], ident[:]).then_inc(f["xT_pe"], 1)
                if back:
                    pe.wait_ge(f["gel"], g + 1)
                    at_least(pe, f["gelT"], g)
                    for n in range(FC):
                        mm = pe.transpose(bank[2 + gpar][:, n * 128:n * 128 + 128],
                                          gel[:, gpar, n * 128:n * 128 + 128], ident[:])
                    mm.then_inc(f["t_pe"], 1)
                if front:
                    pe.wait_ge(f["xT"], it + 1)
                    at_least(pe, f["gel"], it - 1)
                    pe.matmul(bank[par][:, 0:F], xcT[:, par, 0:L], upT[:], start=True, stop=True).then_inc(f["up_pe"], 1)
                if back:
                    pe.wait_ge(f["gelT"], g + 1)
                    at_least(pe, f["x"], g)
                    for n in range(FC):
                        mm = pe.matmul(bank[6 + gpar][:, 0:D], gelT[:, gpar, n, :], downT[:, n, :],
                                       start=(n == 0), stop=(n == FC - 1))
                    mm.then_inc(f["y_pe"], 1)

            skewed(pe, B, ffn0)

            def attn1(it, half, par, front, back):
                gpar = 1 - par
                g = it - 1
                xT = xcT[:, par, 0:L]
                cT = xcT[:, par, L:L + S]

                def transpose_probs(j):
                    pe.wait_ge(c["exp"], NB * g + j + 1)
                    at_least(pe, c["prT"], NB * g + j - 1)
                    b_ = bank[4 + j % 2]
                    for n in range(HB):
                        mm = pe.transpose(b_[0:S, n * L:n * L + L], pr[:, gpar, HB * j + n, :], ident[:])
                    mm.then_inc(c["p_pe"], 1)

                def project_t(j):
                    at_least(pe, c["t"], NB * it + j - 1)
                    for n in range(HB):
                        mm = pe.matmul(bank[j % 2][:, n * L:n * L + L], qk1[:, HB * j + n, :], xT,
                                       start=(n == 0), stop=(n == HB - 1), skip_group_check=True)
                    mm.then_inc(c["t_pe"], 1)

                def scores(j):
                    pe.wait_ge(c["t"], NB * it + j + 1)
                    at_least(pe, c["shifted"], NB * it + j - 1)
                    for n in range(HB):
                        mm = pe.matmul(bank[2 + j % 2][:, n * S:n * S + S], tT[:, HB * j + n, :], cT,
                                       start=(n == 0), stop=(n == HB - 1), skip_group_check=True)
                    mm.then_inc(c["s_pe"], 1)

                if front:
                    pe.wait_ge(c["ln"], it + 1)
                    pe.wait_ge(ctx1_in[par], half * 16 + 16)
                    at_least(pe, c["oT"], 2 * (it - 1))
                    if isinstance(it, int) and it == 1:
                        pe.wait_ge(c["v"], 2)
                    pe.transpose(bank[6][:, 0:L], xn[:, par, :], ident[:])
                    pe.transpose(bank[6][:, L:L + S], ctx_tok[:, par, :], ident[0:S, 0:S]).then_inc(c["xcT_pe"], 1)
                if back:
                    transpose_probs(0)
                    transpose_probs(1)
                if front:
                    pe.wait_ge(c["xcT"], it + 1)
                    project_t(0)
                    project_t(1)
                if back:
                    transpose_probs(2)
                    transpose_probs(3)
                if front:
                    at_least(pe, c["x"], it - 1)
                    for n in range(2):
                        b_ = bank[7 - n]
                        pe.matmul(b_[0:S, :], cT, wv1[:, n * 512:n * 512 + 512], start=True, stop=True
                                  ).then_inc(c["v_pe"], 1)
                    project_t(2)
                    scores(0)
                    project_t(3)
                    scores(1)
                if back:
                    pe.wait_ge(c["prT"], NB * g + NB)
                    for j in range(NB):
                        if j < 2:
                            if front:
                                pe.wait_ge(c["v"], 2 * it + j + 1)
                            at_least(pe, c["x"], g)
                        else:
                            pe.wait_ge(c["o"], NB * g + j - 1)
                        b_ = bank[7 - j % 2]
                        for n in range(HB):
                            h = HB * j + n
                            mm = pe.matmul(b_[:, n * V1W:n * V1W + V1W], prT[:, h, :], v1[:, gpar, h, :],
                                           start=(n == 0), stop=(n == HB - 1), skip_group_check=True)
                        mm.then_inc(c["pv_pe"], 1)
                if front:
                    scores(2)
                    scores(3)
                if back:
                    for n in range(2):
                        pe.wait_ge(c["o"], NB * g + NB - 1 + n)
                        for m in range(4):
                            mm = pe.transpose(bank[7 - n][:, m * 128:m * 128 + 128],
                                              o1[:, (4 * n + m) * 128:(4 * n + m) * 128 + 128], ident[:])
                        mm.then_inc(c["oT_pe"], 1)
                    for m in range(C1):
                        if m % 4 == 0:
                            pe.wait_ge(c["oT"], 2 * g + m // 4 + 1)
                        mm = pe.matmul(bank[7][:, 0:D], o1T[:, m, :], wo1[:, m, :], start=(m == 0), stop=(m == C1 - 1))
                    mm.then_inc(c["y_pe"], 1)

            pe.wait_ge(f["x"], B)
            skewed(pe, B, attn1)

            def route(it, half, par, front, back):
                gpar = 1 - par
                g = it - 1
                if front:
                    pe.wait_ge(ro["ln"], it + 1)
                    at_least(pe, ro["xT"], it - 1)
                    pe.transpose(bank[par][:, 0:L], xn[:, par, :], ident[:]).then_inc(ro["xT_pe"], 1)
                if back:
                    pe.wait_ge(ro["xT"], g + 1)
                    at_least(pe, ro["logits"], g)
                    pe.matmul(bank[2 + gpar][:, 0:E], xcT[:, gpar, 0:L], w_gate_t[:], start=True, stop=True
                              ).then_inc(ro["l_pe"], 1)

            pe.wait_ge(c["x"], B)
            pe.wait_ge(late_in, 16 * 6)
            skewed(pe, B, route)
            pe.wait_ge(ro["v"], 7)
            for e in range(E):
                mm = pe.matmul(bank[4][0:B, e:e + 1], onehot_bf[:, e, :], ones_bf[:, 0:1], start=(e == 0), stop=(e == E - 1),
                               skip_group_check=True)
            mm.then_inc(ro["pe"], 1)
            pe.wait_ge(ro["v"], 9)
            pe.matmul(bank[5][:, 0:B * E].rearrange("p (e b) -> p e b", e=E), before_bf[:], onehot_bf[:], start=True, stop=False)
            pe.matmul(bank[5][:, 0:B * E].rearrange("p (e b) -> p b e", e=E), ones_bf[0:B, :], seq_before[:], start=False, stop=True)
            pe.matmul(bank[6][:, 0:E], ones_bf[0:B, :], seq_count[:], start=True, stop=True).then_inc(ro["pe"], 1)

            def expert(it, use, slot, par, front, back):
                gpar = 1 - par
                g = it - 1
                if front:
                    pe.wait_ge(rows_in[slot], use * 16 + 16)
                    at_least(pe, ex["xT"], it - 1)
                    pe.transpose(bank[4 + par][:, 0:128], rows[:, slot, 0:D], ident[:]).then_inc(ex["xT_pe"], 1)
                if back:
                    pe.wait_ge(ex["hid"], g + 1)
                    at_least(pe, ex["hidT"], g)
                    for n in range(MC):
                        mm = pe.transpose(bank[2 + gpar][:, n * 128:n * 128 + 128], hid[:, gpar, n * 128:n * 128 + 128],
                                          ident[:])
                    mm.then_inc(ex["t_pe"], 1)
                if front:
                    e = pe.value_load(block_e[0:1, bass.ds(it, 1)], min_val=0, max_val=E - 1)
                    pe.wait_ge(ex["xT"], it + 1)
                    at_least(pe, ex["hid"], it - 1)
                    pe.matmul(bank[par][:, 0:M], rowT[:, par, :], w1_t[:, bass.ds(e * M, M)], start=True, stop=True
                              ).then_inc(ex["up_pe"], 1)
                if back:
                    e = pe.value_load(block_e[0:1, bass.ds(g, 1)], min_val=0, max_val=E - 1)
                    pe.wait_ge(ex["hidT"], g + 1)
                    at_least(pe, ex["y2"], g)
                    for n in range(MC):
                        mm = pe.matmul(bank[6 + gpar][:, 0:D], hidT[:, gpar, n, :], w2_t[:, bass.ds(e * (MC * D) + n * D, D)],
                                       start=(n == 0), stop=(n == MC - 1))
                    mm.then_inc(ex["y_pe"], 1)

            pe.wait_ge(ro["blocks"], 1)
            skewed_slots(pe, BLOCKS, expert)

        @block.scalar
        def _(act):
            act.wait_ge(g_in, 16 * (2 * NB + 2))
            act.activation(tg[:], gates[:], ACT.Tanh).then_inc(tanh_set, 1)

            def attn0(it, half, par, front, back):
                gpar = 1 - par
                g = it - 1

                def copy_probs(j):
                    act.wait_ge(a["t_pe"], NB * g + j + 1)
                    at_least(act, a["pv_pe"], g)
                    act.copy(prT[:, HB * j:HB * j + HB, :], bank[4 + j % 2][0:S, :].rearrange("p (h l) -> p h l", h=HB)
                             ).then_inc(a["prT"], 1)

                def exponent(j):
                    act.wait_ge(a["shifted"], NB * it + j + 1)
                    at_least(act, a["t_pe"], NB * (it - 2) + j + 1)
                    act.activation(pr[:, par, HB * j:HB * j + HB, :], sc[:, par, HB * j:HB * j + HB, :], ACT.Exp
                                   ).then_inc(a["exp"], 1)

                if front:
                    act.wait_ge(a["xcT_pe"], it + 1)
                    at_least(act, a["v_pe"], it - 1)
                    act.copy(xcT[:, par, :], bank[6 + (7 * par) % 2][:, 0:L + S]).then_inc(a["xcT"], 1)
                if back:
                    copy_probs(0)
                    copy_probs(1)
                if front:
                    act.wait_ge(a["v_pe"], it + 1)
                    at_least(act, a["pv_pe"], it - 1)
                    act.copy(v0[:, par, :, 0:HD0],
                             bank[6 + (7 * par + 3) % 2][0:S, 0:H * HD0].rearrange("s (h d) -> s h d", h=H)
                             ).then_inc(a["v"], 1)
                if back:
                    copy_probs(2)
                    copy_probs(3)
                if front:
                    exponent(0)
                    exponent(1)
                if back:
                    act.wait_ge(a["oT_pe"], g + 1)
                    at_least(act, a["y_pe"], g)
                    act.copy(o0T[:], bank[6 + (7 * par + 5) % 2][:, 0:L]).then_inc(a["oT"], 1)
                if front:
                    exponent(2)
                    exponent(3)

            skewed(act, B, attn0)

            act.wait_ge(prep_pe, 3)
            act.copy(upT[:], bank[1][:]).then_inc(prep_a, 1)
            act.copy(downT[:].rearrange("p c d -> p (c d)"), bank[2][:]).then_inc(prep_a, 1)
            for m, w in enumerate((wq1T, wk1T)):
                for n in range(2):
                    act.copy(w[:, 4 * n:4 * n + 4, :].rearrange("p c d -> p (c d)"), bank[3 + 2 * m + n][:]
                             ).then_inc(prep_a, 1)
            act.wait_ge(prep_pe, 4)
            for r in range(2):
                for n in range(2):
                    act.mul(qk1[:, 8 * n + r:8 * n + r + 7:2, :],
                            bank[3 + 2 * r + n][:].rearrange("p (h e) -> p h e", h=4), SCALE1).then_inc(prep_a, 1)

            def ffn0(it, half, par, front, back):
                gpar = 1 - par
                g = it - 1
                if front:
                    act.wait_ge(f["xT_pe"], it + 1)
                    at_least(act, f["up_pe"], it - 1)
                    act.copy(xcT[:, par, 0:L], bank[4 + par][:, 0:L]).then_inc(f["xT"], 1)
                if back:
                    act.wait_ge(f["t_pe"], g + 1)
                    at_least(act, f["y_pe"], g)
                    act.copy(gelT[:, gpar, :, :].rearrange("p c l -> p (c l)"), bank[2 + gpar][:]).then_inc(f["gelT"], 1)
                if front:
                    act.wait_ge(f["up_pe"], it + 1)
                    at_least(act, f["t_pe"], it - 1)
                    at_least(act, f["sq"], it - 1)
                    act.activation(gel[:, par, :], bank[par][:, 0:F], ACT.Gelu).then_inc(f["gel"], 1)

            skewed(act, B, ffn0)

            def attn1(it, half, par, front, back):
                gpar = 1 - par
                g = it - 1

                def copy_probs(j):
                    act.wait_ge(c["p_pe"], NB * g + j + 1)
                    at_least(act, c["pv_pe"], NB * g)
                    act.copy(prT[:, HB * j:HB * j + HB, :], bank[4 + j % 2][0:S, :].rearrange("p (h l) -> p h l", h=HB)
                             ).then_inc(c["prT"], 1)

                def exponent(j):
                    act.wait_ge(c["shifted"], NB * it + j + 1)
                    at_least(act, c["p_pe"], NB * (it - 2) + j + 1)
                    act.activation(pr[:, par, HB * j:HB * j + HB, :], sc[:, par, HB * j:HB * j + HB, :], ACT.Exp
                                   ).then_inc(c["exp"], 1)

                if front:
                    act.wait_ge(c["xcT_pe"], it + 1)
                    at_least(act, c["s_pe"], NB * (it - 1))
                    act.copy(xcT[:, par, :], bank[6][:, 0:L + S]).then_inc(c["xcT"], 1)
                if back:
                    copy_probs(0)
                    copy_probs(1)
                    copy_probs(2)
                    copy_probs(3)
                if front:
                    for n in range(2):
                        act.wait_ge(c["v_pe"], 2 * it + n + 1)
                        at_least(act, c["pv_pe"], NB * (it - 1))
                        act.copy(v1[:, par, 8 * n:8 * n + 8, 0:HD1],
                                 bank[7 - n][0:S, :].rearrange("s (h d) -> s h d", h=8)).then_inc(c["v"], 1)
                    exponent(0)
                    exponent(1)
                if front:
                    exponent(2)
                if back:
                    for n in range(2):
                        act.wait_ge(c["oT_pe"], 2 * g + n + 1)
                        at_least(act, c["y_pe"], g)
                        act.copy(o1T[:, 4 * n:4 * n + 4, :].rearrange("p c l -> p (c l)"), bank[7 - n][:]
                                 ).then_inc(c["oT"], 1)
                if front:
                    exponent(3)

            skewed(act, B, attn1)

            def route(it, half, par, front, back):
                if front:
                    act.wait_ge(ro["xT_pe"], it + 1)
                    at_least(act, ro["l_pe"], it - 1)
                    act.copy(xcT[:, par, 0:L], bank[par][:, 0:L]).then_inc(ro["xT"], 1)

            skewed(act, B, route)
            act.wait_ge(ro["v"], 2)
            act.activation(route_b[:], route_a[:], ACT.Exp).then_inc(ro["exp"], 1)

            def expert(it, use, slot, par, front, back):
                gpar = 1 - par
                g = it - 1
                if front:
                    act.wait_ge(ex["xT_pe"], it + 1)
                    at_least(act, ex["up_pe"], it - 1)
                    act.copy(rowT[:, par, :], bank[4 + par][:, 0:128]).then_inc(ex["xT"], 1)
                if back:
                    act.wait_ge(ex["t_pe"], g + 1)
                    at_least(act, ex["y_pe"], g)
                    act.activation(hidT[:, gpar, :, :].rearrange("p c l -> p (c l)"), bank[2 + gpar][:], ACT.Relu
                                   ).then_inc(ex["hidT"], 1)

            skewed_slots(act, BLOCKS, expert)

        @block.vector
        def _(dve):
            dve.memset(wq0_pad[:], 0.0).then_inc(prep_v, 1)
            dve.memset(wk0_pad[:], 0.0).then_inc(prep_v, 1)
            dve.wait_ge(prep_v, 2)
            dve.wait_ge(w_in, W_ALL)
            dve.wait_ge(tanh_set, 1)
            dve.tensor_scalar(wq0_pad[:, :, :, 0:HD0], wq0_raw[:].rearrange("p (j g d) -> p g j d", j=NB, g=HB),
                              SCALE0, None, ALU.mult).then_inc(prep_v, 1)
            dve.tensor_copy(wk0_pad[:, :, :, 0:HD0], wk0_raw[:].rearrange("p (j g d) -> p g j d", j=NB, g=HB)
                            ).then_inc(prep_v, 1)
            dve.tensor_scalar(bq0_col[:], bq0_col[:], SCALE0, None, ALU.mult).then_inc(prep_v, 1)
            dve.tensor_scalar(wo0[:], wo0[:], tg[:, 0:1], None, ALU.mult).then_inc(prep_v, 1)
            dve.tensor_scalar(bo0_row[:], bo0_row[:], tg[0:1, 0:1], None, ALU.mult).then_inc(prep_v, 1)
            dve.tensor_scalar(wo1[:], wo1[:], tg[:, 1:2], None, ALU.mult).then_inc(prep_v, 1)
            dve.wait_ge(prep_v, 8)
            for m, (w, t) in enumerate(((up_raw[:].rearrange("p c d -> p (c d)"), tern_a), (down_raw[:], tern_b))):
                dve.scalar_tensor_tensor(out=t[:], in0=w, scalar=-1.0, in1=w, op0=ALU.mult, op1=ALU.max
                                         ).then_inc(zeroed, 1)
                dve.wait_ge(zeroed, 3 + m)
                dve.reduce_sum(absum[:, m:m + 1], t[:], AX_X).then_inc(zeroed if m < 0 else prep_v, 1)
            dve.wait_ge(prep_v, 10)
            dve.sem_inc(weights_set, 1)

            def row_stats(it, par, s):
                dve.bn_stats(stats[:], xs[:, bass.ds(it, 1), :].rearrange("l o d -> l (o d)")).then_inc(s["stats"], 1)
                dve.wait_ge(s["stats"], 2 * it + 1)
                dve.memset(settle[:], 0.0)
                dve.bn_aggr(mv[:, par, :], stats[:]).then_inc(s["stats"], 1)

            def normalise(it, par, s, transposed, ready, scale):
                at_least(dve, s[transposed], it - 1)
                dve.wait_ge(s["stats"], 2 * it + 2)
                dve.wait_ge(ready[0], ready[1] * it + ready[1])
                dve.tensor_scalar(xn[:, par, :], xs[:, bass.ds(it, 1), :].rearrange("l o d -> l (o d)"),
                                  mv[:, par, 0:1], scale[:, par:par + 1], ALU.subtract, ALU.mult).then_inc(s["ln"], 1)

            def attn0(it, half, par, front, back):
                gpar = 1 - par
                g = it - 1

                last = isinstance(it, int) and it == B - 1

                def add_bias(j):
                    s = sc[:, par, HB * j:HB * j + HB, :]
                    dve.wait_ge(a["s_pe"], NB * it + j + 1)
                    dve.wait_ge(bias_in[par][j], half * 16 + 16)
                    at_least(dve, a["exp"], NB * (it - 2) + j + 1)
                    dve.tensor_tensor(s, bank[j][:, 0:HB * S].rearrange("p (h s) -> p h s", h=HB),
                                      bias_t[:, par, HB * j:HB * j + HB, :], ALU.add).then_inc(a["biased"], 1)
                    dve.wait_ge(a["biased"], NB * it + j + 1)
                    dve.reduce_max(mx[:, par, HB * j:HB * j + HB], s, AX_X).then_inc(a["max"], 1)

                if front:
                    dve.wait_ge(a["q_pe"], it + 1)
                    at_least(dve, a["s_pe"], NB * (it - 1))
                    dve.tensor_tensor(qT[:, par, :, :], bank[6 + (7 * par + 1) % 2][:].rearrange("p (g l) -> p g l", g=HB),
                                      bq0_col[:].unsqueeze(2).to_broadcast([128, HB, L]), ALU.add).then_inc(a["qk"], 1)
                    dve.wait_ge(a["k_pe"], it + 1)
                    dve.tensor_tensor(kT[:, par, :, :],
                                      bank[6 + (7 * par + 2) % 2][:, 0:HB * S].rearrange("p (g l) -> p g l", g=HB),
                                      bk0_col[:].unsqueeze(2).to_broadcast([128, HB, S]), ALU.add).then_inc(a["qk"], 1)
                    add_bias(0)
                    add_bias(1)
                    if not last:
                        dve.wait_ge(xc_in[1 - par], (half + par) * 32 + 32)
                        row_stats(it + 1, 1 - par, a)
                if back:
                    b_ = bank[6 + (7 * par + 4) % 2][:, 0:H * V0W].rearrange("l (h d) -> l h d", h=H)
                    dve.wait_ge(a["pv_pe"], g + 1)
                    at_least(dve, a["oT_pe"], g)
                    dve.reciprocal(rden[:].unsqueeze(2), b_[:, :, HD0:V0W]).then_inc(a["rden"], 1)
                    dve.wait_ge(a["rden"], g + 1)
                    dve.tensor_tensor(o0[:], b_[:, :, 0:HD0], rden[:].unsqueeze(2).to_broadcast([L, H, HD0]), ALU.mult
                                      ).then_inc(a["o"], 1)
                if front:
                    add_bias(2)
                    add_bias(3)
                if front and not last:
                    additive_mask(it + 1, half + par, 1 - par)
                    normalise(it + 1, 1 - par, a, "xcT_pe", (a["rstd"], 2), rstd)
                if back:
                    row = xs[:, bass.ds(g, 1), :].rearrange("l o d -> l (o d)")
                    dve.wait_ge(a["y_pe"], g + 1)
                    dve.tensor_tensor(row, bank[6 + (7 * par + 6) % 2][:, 0:D], row, ALU.add).then_inc(a["x"], 1)

            def additive_mask(it, half, par):
                at_least(dve, a["s_pe"], NB * (it - 1))
                dve.wait_ge(mask_in[par], half * 16 + 16)
                dve.tensor_scalar(mask_b[:, par, :], mask_i[:, par, :], 0.0, MASKED, ALU.is_equal, ALU.mult
                                  ).then_inc(a["mask"], 1)

            additive_mask(0, 0, 0)
            dve.wait_ge(xc_in[0], 32)
            row_stats(0, 0, a)
            normalise(0, 0, a, "xcT_pe", (a["rstd"], 2), rstd)
            skewed(dve, B, attn0)

            dve.wait_ge(prep_pe, 1)
            dve.tensor_scalar(thr[:, 0:2], bank[0][:, 0:2], 0.5 / (F * D), None, ALU.mult).then_inc(weights_set, 1)
            dve.tensor_scalar(thr[:, 2:4], bank[0][:, 0:2], -0.5 / (F * D), None, ALU.mult).then_inc(weights_set, 1)
            dve.wait_ge(weights_set, 3)
            for m, (w, t) in enumerate(((up_raw[:].rearrange("p c d -> p (c d)"), tern_a), (down_raw[:], tern_b))):
                dve.tensor_scalar(t[:], w, thr[:, m:m + 1], None, ALU.is_gt).then_inc(weights_set, 1)
                dve.wait_ge(weights_set, 4 + 4 * m)
                dve.tensor_scalar(gelT[:, m, :, :].rearrange("p c l -> p (c l)"), w, thr[:, 2 + m:3 + m], None, ALU.is_lt
                                  ).then_inc(weights_set, 1)
                dve.wait_ge(weights_set, 5 + 4 * m)
                dve.tensor_tensor(t[:], t[:], gelT[:, m, :, :].rearrange("p c l -> p (c l)"), ALU.subtract
                                  ).then_inc(weights_set, 1)
                dve.wait_ge(weights_set, 6 + 4 * m)
                dve.tensor_tensor(t[:], t[:], w, ALU.subtract).then_inc(weights_set, 1)
                dve.wait_ge(weights_set, 7 + 4 * m)
                dve.tensor_tensor(t[:], t[:], w, ALU.add).then_inc(prep_v, 1)

            def ffn0(it, half, par, front, back):
                gpar = 1 - par
                g = it - 1
                last = isinstance(it, int) and it == B - 1
                if front and not last:
                    row_stats(it + 1, 1 - par, f)
                if back:
                    row = xs[:, bass.ds(g, 1), :].rearrange("l o d -> l (o d)")
                    dve.wait_ge(f["rs2"], g + 1)
                    dve.wait_ge(f["y_pe"], g + 1)
                    dve.scalar_tensor_tensor(out=row, in0=bank[6 + gpar][:, 0:D], scalar=rgate[:, gpar:gpar + 1],
                                             in1=row, op0=ALU.mult, op1=ALU.add).then_inc(f["x"], 1)
                if front and not last:
                    normalise(it + 1, 1 - par, f, "xT_pe", (f["chain"], 5), rms[:, 4:6])
                if front:
                    dve.wait_ge(f["gel"], it + 1)
                    at_least(dve, f["rs2"], it - 1)
                    dve.tensor_tensor_reduce(out=gel2[:], in0=gel[:, par, :], in1=gel[:, par, :], scale=1.0, scalar=0.0,
                                             op0=ALU.mult, op1=ALU.add, accum_out=ssq[:, par:par + 1]).then_inc(f["sq"], 1)

            row_stats(0, 0, f)
            normalise(0, 0, f, "xT_pe", (f["chain"], 5), rms[:, 4:6])
            skewed(dve, B, ffn0)

            def attn1(it, half, par, front, back):
                gpar = 1 - par
                g = it - 1

                last = isinstance(it, int) and it == B - 1

                def copy_t(j):
                    dve.wait_ge(c["t_pe"], NB * it + j + 1)
                    at_least(dve, c["s_pe"], NB * (it - 1) + j + 1)
                    dve.tensor_copy(tT[:, HB * j:HB * j + HB, :].rearrange("p h l -> p (h l)"), bank[j % 2][:]
                                    ).then_inc(c["t"], 1)

                def shift(j):
                    s = bank[2 + j % 2][:, 0:HB * S].rearrange("p (h s) -> p h s", h=HB)
                    m = mx[:, par, HB * j:HB * j + HB]
                    dve.wait_ge(c["s_pe"], NB * it + j + 1)
                    dve.reduce_max(m, s, AX_X).then_inc(c["max"], 1)
                    dve.wait_ge(c["max"], NB * it + j + 1)
                    at_least(dve, c["exp"], NB * (it - 2) + j + 1)
                    dve.tensor_tensor(sc[:, par, HB * j:HB * j + HB, :], s, m.unsqueeze(2).to_broadcast([L, HB, S]),
                                      ALU.subtract).then_inc(c["shifted"], 1)

                if front:
                    if not last:
                        row_stats(it + 1, 1 - par, c)
                    for j in range(NB):
                        copy_t(j)
                    shift(0)
                    shift(1)
                if back:
                    for j in range(NB):
                        b_ = bank[7 - j % 2][:, 0:HB * V1W].rearrange("l (h d) -> l h d", h=HB)
                        r = rden[:, HB * j:HB * j + HB].unsqueeze(2)
                        dve.wait_ge(c["pv_pe"], NB * g + j + 1)
                        if j == 0:
                            at_least(dve, c["oT_pe"], 2 * g)
                        dve.reciprocal(r, b_[:, :, HD1:V1W]).then_inc(c["rden"], 1)
                        dve.wait_ge(c["rden"], NB * g + j + 1)
                        dve.tensor_tensor(o1[:, HB * j * HD1:(HB * j + HB) * HD1].rearrange("l (h d) -> l h d", h=HB),
                                          b_[:, :, 0:HD1], r.to_broadcast([L, HB, HD1]), ALU.mult).then_inc(c["o"], 1)
                if front:
                    shift(2)
                    shift(3)
                if front and not last:
                    normalise(it + 1, 1 - par, c, "xcT_pe", (c["rstd"], 2), rstd)
                if back:
                    row = xs[:, bass.ds(g, 1), :].rearrange("l o d -> l (o d)")
                    dve.wait_ge(c["y_pe"], g + 1)
                    dve.tensor_tensor(row, bank[7][:, 0:D], row, ALU.add).then_inc(c["x"], 1)

            row_stats(0, 0, c)
            normalise(0, 0, c, "xcT_pe", (c["rstd"], 2), rstd)
            skewed(dve, B, attn1)

            def route(it, half, par, front, back):
                g = it - 1
                last = isinstance(it, int) and it == B - 1
                if front and not last:
                    row_stats(it + 1, 1 - par, ro)
                if back:
                    dve.wait_ge(ro["l_pe"], g + 1)
                    dve.tensor_tensor(logits[:, bass.ds(g, 1), :].rearrange("l o e -> l (o e)"), bank[2 + 1 - par][:, 0:E], bg_bc[:],
                                      ALU.add).then_inc(ro["logits"], 1)
                if front:
                    dve.wait_ge(ro["ln"], it + 1)
                    dve.tensor_scalar(rec[:, bass.ds(it, 1), 0:D].rearrange("l o d -> l (o d)"), xn[:, par, :], 1.0, None, ALU.mult
                                      ).then_inc(ro["rec"], 1)
                if front and not last:
                    normalise(it + 1, 1 - par, ro, "xT_pe", (ro["rstd"], 2), rstd)

            row_stats(0, 0, ro)
            normalise(0, 0, ro, "xT_pe", (ro["rstd"], 2), rstd)
            skewed(dve, B, route)

            best, total, first, at = (pick[:, n, :] for n in range(4))
            dve.wait_ge(ro["logits"], B)
            dve.reduce_max(best, logits[:], AX_X).then_inc(ro["v"], 1)
            dve.wait_ge(ro["v"], 1)
            dve.tensor_tensor(route_a[:], logits[:], best.unsqueeze(2).to_broadcast([L, B, E]), ALU.subtract
                              ).then_inc(ro["v"], 1)
            dve.wait_ge(ro["exp"], 1)
            dve.reduce_sum(total, route_b[:], AX_X).then_inc(ro["v"], 1)
            dve.tensor_scalar(route_a[:], route_a[:], 0.0, float(E), ALU.is_lt, ALU.mult).then_inc(ro["v"], 1)
            dve.wait_ge(ro["v"], 4)
            dve.tensor_tensor(route_a[:], route_a[:], experts[:], ALU.add).then_inc(ro["v"], 1)
            dve.wait_ge(ro["v"], 5)
            dve.tensor_reduce(first, route_a[:], AX_X, ALU.min).then_inc(ro["v"], 1)
            dve.wait_ge(ro["v"], 6)
            dve.tensor_tensor(onehot[:], experts[:], first.unsqueeze(2).to_broadcast([L, B, E]), ALU.is_equal
                              ).then_inc(chained, 1)
            dve.wait_ge(chained, 1)
            dve.wait_ge(ro["tables"], 11)
            dve.tensor_copy(before_bf[:], before[:]).then_inc(chained, 1)
            dve.tensor_copy(onehot_bf[:], onehot[:].rearrange("l b e -> l e b")).then_inc(ro["v"], 1)
            dve.wait_ge(chained, 2)
            dve.reciprocal(at, total).then_inc(chained, 1)
            dve.wait_ge(chained, 3)
            dve.tensor_scalar(rec[:, :, GATE:TOKEN], at.unsqueeze(2), tg[:, 3:4], None, ALU.mult).then_inc(ro["rec"], 1)
            dve.wait_ge(ro["pe"], 1)
            dve.tensor_copy(seq_count[:], bank[4][0:B, 0:E]).then_inc(ro["v"], 1)
            dve.wait_ge(ro["v"], 8)
            dve.tensor_tensor(seq_before[:], before[0:B, 0:B].unsqueeze(2).to_broadcast([B, B, E]),
                              seq_count[:].unsqueeze(1).to_broadcast([B, B, E]), ALU.mult).then_inc(ro["v"], 1)
            n_blocks, start, end, base = (blocks_of[:, n, :] for n in range(4))
            dve.wait_ge(ro["pe"], 2)
            dve.tensor_tensor(above[:], bank[6][:, 0:E].unsqueeze(2).to_broadcast([128, E, B]),
                              block_rows[:].unsqueeze(1).to_broadcast([128, E, B]), ALU.is_gt).then_inc(chained, 1)
            dve.wait_ge(chained, 4)
            dve.reduce_sum(n_blocks, above[:], AX_X).then_inc(chained, 1)
            dve.wait_ge(chained, 5)
            dve.tensor_tensor(above[:, :, 0:E], before_e[:], n_blocks.unsqueeze(1).to_broadcast([128, E, E]), ALU.mult
                              ).then_inc(chained, 1)
            dve.wait_ge(chained, 6)
            dve.reduce_sum(start, above[:, :, 0:E], AX_X).then_inc(chained, 1)
            dve.wait_ge(chained, 7)
            dve.tensor_tensor(end, start, n_blocks, ALU.add).then_inc(chained, 1)
            dve.tensor_scalar(base, start, 128.0, None, ALU.mult).then_inc(chained, 1)
            dve.wait_ge(chained, 9)
            dve.tensor_tensor(route_a[:], bank[5][:, 0:B * E].rearrange("p (e b) -> p b e", e=E),
                              base.unsqueeze(1).to_broadcast([L, B, E]), ALU.add).then_inc(chained, 1)
            dve.wait_ge(chained, 10)
            dve.tensor_tensor(route_a[:], route_a[:], onehot[:], ALU.mult).then_inc(chained, 1)
            dve.wait_ge(chained, 11)
            dve.reduce_sum(best, route_a[:], AX_X).then_inc(chained, 1)
            dve.wait_ge(chained, 12)
            dve.tensor_copy(place[:], best).then_inc(ro["place"], 1)
            dve.tensor_tensor(block_cmp[:], block_no[:].unsqueeze(2).to_broadcast([1, BLOCKS, E]),
                              end[0:1, :].unsqueeze(1).to_broadcast([1, BLOCKS, E]), ALU.is_ge).then_inc(chained, 1)
            dve.wait_ge(chained, 13)
            dve.reduce_sum(block_f[:], block_cmp[:], AX_X).then_inc(chained, 1)
            dve.wait_ge(chained, 14)
            dve.tensor_scalar(block_e[:], block_f[:], float(E - 1), None, ALU.min).then_inc(ro["blocks"], 1)

            def expert(it, use, slot, par, front, back):
                gpar = 1 - par
                gslot = (slot + 3) % 4
                g = it - 1
                if front:
                    e = dve.value_load(block_e[0:1, bass.ds(it, 1)], min_val=0, max_val=E - 1)
                    dve.wait_ge(ex["up_pe"], it + 1)
                    at_least(dve, ex["t_pe"], it - 1)
                    dve.tensor_tensor(hid[:, par, :], bank[par][:, 0:M],
                                      b1_bc[:, bass.ds(e, 1), :].rearrange("p o m -> p (o m)"), ALU.add).then_inc(ex["hid"], 1)
                if back:
                    e = dve.value_load(block_e[0:1, bass.ds(g, 1)], min_val=0, max_val=E - 1)
                    dve.wait_ge(ex["y_pe"], g + 1)
                    dve.tensor_tensor(y2[:, gpar, :], bank[6 + gpar][:, 0:D],
                                      b2_bc[:, bass.ds(e, 1), :].rearrange("p o d -> p (o d)"), ALU.add).then_inc(ex["y2"], 1)
                    dve.wait_ge(ex["y2"], g + 1)
                    dve.scalar_tensor_tensor(out=y_out[:, gslot, :], in0=y2[:, gpar, :], scalar=rows[:, gslot, GATE:TOKEN],
                                             in1=rows[:, gslot, D:2 * D], op0=ALU.mult, op1=ALU.add).then_inc(ex["y"], 1)

            dve.wait_ge(ro["blocks"], 1)
            dve.wait_ge(late_in, 16 * 6)
            skewed_slots(dve, BLOCKS, expert)


_INS = ['x', 'ctx_1024', 'fside_Bx16xSxS2_0', 'mask_Bx1xSxS2_ik1', 'g_xattn', 'g_ffn', 'L0_xattn_Wq', 'L0_xattn_bq',
        'L0_xattn_Wk', 'L0_xattn_bk', 'L0_xattn_Wv', 'L0_xattn_bv', 'L0_xattn_Wo', 'L0_xattn_bo', 'L0_ffn_w_up',
        'L0_ffn_w_down', 'L1_xattn_Wq', 'L1_xattn_Wk', 'L1_xattn_Wv', 'L1_xattn_Wo', 'L1_ffn_w_gate', 'L1_ffn_b_gate',
        'L1_ffn_W1', 'L1_ffn_b1', 'L1_ffn_W2', 'L1_ffn_b2']


def kernel(**inputs):
    import numpy as np
    import concourse.bacc as bacc
    from concourse.bass_utils import run_bass_kernel_spmd

    nc = bacc.Bacc("TRN2", target_bir_lowering=False, num_devices=1)
    arrays, args = {}, []
    for name in _INS:
        arr = np.ascontiguousarray(inputs[name])
        arrays[f"in_{name}"] = arr
        args.append(nc.dram_tensor(f"in_{name}", arr.shape, mybir.dt.from_np(arr.dtype), kind="ExternalInput").ap())
    out = nc.dram_tensor("out_x", inputs["x"].shape, F32, kind="ExternalOutput").ap()
    build(nc, *args, out)
    r = run_bass_kernel_spmd(nc, [arrays], core_ids=[0])
    return r.results[0]["out_x"]
```

```python
from contextlib import ExitStack

import concourse.bass as bass
from concourse import mybir

F32 = mybir.dt.float32
F32R = mybir.dt.float32r
BF16 = mybir.dt.bfloat16
I32 = mybir.dt.int32
ALU = mybir.AluOpType
ACT = mybir.ActivationFunctionType
AX_X = mybir.AxisListType.X

H = 16
HB = 4
NB = H // HB
LN_EPS = 1e-5
RMS_EPS = 1e-8
MASKED = -1.0e30


def at_least(eng, sem, value):
    if not isinstance(value, int) or value > 0:
        eng.wait_ge(sem, value)


def live(k, n):
    return not isinstance(k, int) or 0 <= k < n


def staged(eng, n, body):
    for it in range(-1, 4):
        body(it, it // 2, it % 2)
    with eng.Fori(2, n // 2 - 1) as pair:
        body(pair * 2, pair, 0)
        body(pair * 2 + 1, pair, 1)
    for it in range(n // 2 * 2 - 2, n + 2):
        body(it, it // 2, it % 2)


def staged_slots(eng, n, body):
    for it in range(-1, 4):
        body(it, it // 4, it % 4)
    turns = (n - 1) // 4
    with eng.Fori(1, turns) as turn:
        for k in range(4):
            body(turn * 4 + k, turn, k)
    for it in range(4 * turns, n + 2):
        body(it, it // 4, it % 4)


def build(nc, x, ctx_in, bias, mask, g_xattn, g_ffn, Wq0, bq0, Wk0, bk0, Wv0, bv0, Wo0, bo0, w_up, w_down,
          Wq1, Wk1, Wv1, Wo1, w_gate, b_gate, W1, b1, W2, b2, out):
    B, L, D = x.shape
    S = ctx_in.shape[1]
    HD0 = Wq0.shape[1] // H
    HD1 = Wq1.shape[1] // H
    F = w_up.shape[0]
    FC = F // 128
    assert L == 128 and D == 128 and S <= 128 and B % 2 == 0 and HD0 <= 32 and HD1 == 64
    SCALE0 = HD0 ** -0.5
    SCALE1 = HD1 ** -0.5
    C1 = H * HD1 // 128
    E, _, M = W1.shape
    MC = M // 128
    NT = B * L
    BLOCKS = NT // 128 + E - 1
    GATE, TOKEN, REC = 2 * D, 2 * D + 1, 2 * D + 2

    stack = ExitStack()
    with stack:
        def sb(name, shape, dt=F32):
            return stack.enter_context(nc.sbuf_tensor(name, shape, dt))

        def sem(name):
            return stack.enter_context(nc.semaphore(name))

        bank = [stack.enter_context(nc.psum_tensor(f"bank{i}", [128, 512], F32)) for i in range(8)]

        ident = sb("ident", [128, 128])
        ident_bf = sb("ident_bf", [128, 128], BF16)
        ones = sb("ones", [128, 128])
        gates = sb("gates", [128, 4])
        tg = sb("tg", [128, 4])
        wq0_raw = sb("wq0_raw", [D, H * HD0])
        wk0_raw = sb("wk0_raw", [D, H * HD0])
        wq0_pad = sb("wq0_pad", [D, HB, NB, 32])
        wk0_pad = sb("wk0_pad", [D, HB, NB, 32])
        bq0_col = sb("bq0_col", [128, HB])
        bk0_col = sb("bk0_col", [128, HB])
        wv0 = sb("wv0", [D, H * HD0])
        bv0_row = sb("bv0_row", [1, H * HD0])
        wo0 = sb("wo0", [H * HD0, D])
        bo0_row = sb("bo0_row", [1, D])
        absum = sb("absum", [128, FC, 2])
        thr = sb("thr", [128, 4])
        w2_t = sb("w2_t", [128, E * MC * D])
        wq1_raw = w2_t[:, 0:H * HD1]
        wk1_raw = w2_t[:, H * HD1:2 * H * HD1]
        wq1T = w2_t[:, 2 * H * HD1:3 * H * HD1].rearrange("p (c d) -> p c d", c=C1)
        wk1T = w2_t[:, 3 * H * HD1:4 * H * HD1].rearrange("p (c d) -> p c d", c=C1)
        kq1_t = sb("kq1_t", [D, H * D])
        kq1 = kq1_t[:].rearrange("p (h d) -> p h d", h=H)
        wo1 = sb("wo1", [128, C1, D])
        vo1_hi = sb("vo1_hi", [D, H, D], F32R)
        vo1_lo = sb("vo1_lo", [D, H, D], F32R)

        rec = sb("rec", [L, B, REC])
        xs = rec[:, :, D:2 * D]
        assert B >= 6 * FC + H * HD1 // D
        up_raw, down_raw, tern_a, tern_b, upT, downT = (rec[:, n * FC:(n + 1) * FC, 0:D] for n in range(6))
        wv1_raw = rec[:, 6 * FC:6 * FC + H * HD1 // D, 0:D]

        ctx_tok = sb("ctx_tok", [S, 2, D])
        mask_i = sb("mask_i", [L, 2, S], I32)
        mask_b = sb("mask_b", [L, 2, S], BF16)
        w1_t = sb("w1_t", [128, E * M])
        bias_t = w1_t[:, 0:2 * H * S].rearrange("l (p h s) -> l p h s", p=2, h=H)
        stats = sb("stats", [128, 6])
        mv = sb("mv", [128, 2, 2])
        stats_all = sb("stats_all", [128, B, 6])
        mean_all = sb("mean_all", [128, B])
        scale_all = sb("scale_all", [128, B])
        tmp_all = sb("tmp_all", [128, 6, B])
        rstd = sb("rstd", [128, 2])
        powers = sb("powers", [128, 6])
        settle = sb("settle", [128, 1])
        xn = sb("xn", [L, 2, D])
        xcT = sb("xcT", [D, 2, L + S])
        proj_t = sb("proj_t", [128, 4 * F])
        qT = proj_t[:, 0:2 * HB * L].rearrange("p (a h l) -> p a h l", a=2, h=HB)
        kT = proj_t[:, 2 * HB * L:2 * HB * (L + S)].rearrange("p (a h s) -> p a h s", a=2, h=HB)
        gel = proj_t[:, 0:2 * F].rearrange("p (a f) -> p a f", a=2)
        gelT = proj_t[:, 2 * F:4 * F].rearrange("p (a c l) -> p a c l", a=2, c=FC)
        xcT_hi = sb("xcT_hi", [D, 2, L + S], F32R)
        xcT_lo = sb("xcT_lo", [D, 2, L + S], F32R)
        u_hi = sb("u_hi", [D, 2, H, S], F32R)
        u_lo = sb("u_lo", [D, 2, H, S], F32R)
        b1_t = sb("b1_t", [128, E * M])
        sc = b1_t[:, 0:2 * H * S].rearrange("l (p h s) -> l p h s", p=2, h=H)
        mx = sb("mx", [L, 2, H])
        work = sb("work", [128, 4096 + 128])
        v0 = work[0:S, 0:2 * H * D].rearrange("s (p h d) -> s p h d", p=2, h=H)
        w_vo = work[0:S, 0:2 * H * D].rearrange("s (p h d) -> s p h d", p=2, h=H)
        wv1T = work[:, 0:H * HD1].rearrange("p (c d) -> p c d", c=C1)
        gel2 = work[:, H * HD1:H * HD1 + F]
        hid = work[:, 0:2 * M].rearrange("l (p m) -> l p m", p=2)
        hidT = work[:, 2 * M:4 * M].rearrange("p (a c l) -> p a c l", a=2, c=MC)
        at0 = 4 * M
        rows_n = work[:, at0:at0 + 4 * D].rearrange("l (n c) -> l n c", n=4)
        rows_x = work[:, at0 + 4 * D:at0 + 4 * D + 4 * (REC - D)].rearrange("l (n c) -> l n c", n=4)
        y_out = work[:, at0 + 8 * D + 8:at0 + 12 * D + 8].rearrange("l (n d) -> l n d", n=4)
        prT = sb("prT", [S, H, L])
        den = sb("den", [L, 2, H])
        rden = sb("rden", [L, 2, H])
        o0T = sb("o0T", [H * HD0, L])
        ssq = sb("ssq", [L, 2])
        rms = sb("rms", [L, 2])
        rms_eps = sb("rms_eps", [L, 1])
        rrms = sb("rrms", [L, 1])

        w_gate_t = sb("w_gate_t", [D, E])
        bg_bc = sb("bg_bc", [128, E])
        b1_bc = b1_t[:].rearrange("p (e m) -> p e m", e=E)
        b2_bc = sb("b2_bc", [128, E, D])
        blank = sb("blank", [128, REC])
        experts = sb("experts", [128, B, E])
        before = sb("before", [128, 128])
        before_bf = sb("before_bf", [128, 128], BF16)
        ones_bf = sb("ones_bf", [128, 128], BF16)
        before_e = sb("before_e", [128, E, E])
        block_rows = sb("block_rows", [128, B])
        block_no = sb("block_no", [1, BLOCKS])
        logits, route_a, route_b, onehot = (
            kq1_t[:, n * B * E:(n + 1) * B * E].rearrange("l (b e) -> l b e", e=E) for n in range(4))
        above = kq1_t[:, 4 * B * E:5 * B * E].rearrange("p (e b) -> p e b", e=E)
        rowT = kq1_t[:, 5 * B * E:5 * B * E + 2 * D].rearrange("p (a l) -> p a l", a=2)
        y2 = kq1_t[:, 5 * B * E + 2 * D:5 * B * E + 4 * D].rearrange("p (a d) -> p a d", a=2)
        assert 5 * B * E + 4 * D <= H * D
        onehot_bf = sb("onehot_bf", [L, E, B], BF16)
        pick = sb("pick", [L, 4, B])
        seq_count = sb("seq_count", [B, E], BF16)
        seq_before = sb("seq_before", [B, B, E], BF16)
        blocks_of = sb("blocks_of", [128, 4, E])
        block_cmp = sb("block_cmp", [1, BLOCKS, E])
        block_f = sb("block_f", [1, BLOCKS])
        block_e = sb("block_e", [1, BLOCKS], I32)
        place = sb("place", [L, B], I32)
        idle = sb("idle", [128, 1])
        sorted_rows = nc.dram_tensor("sorted_rows", [BLOCKS * 128, REC], F32, kind="Internal").ap()

        wqk0_in = sem("wqk0_in")
        wvo0_in = sem("wvo0_in")
        w_in = sem("w_in")
        g_in = sem("g_in")
        xc_in = [sem(f"xc_in{p}") for p in range(2)]
        mask_in = [sem(f"mask_in{p}") for p in range(2)]
        bias_in = [[sem(f"bias_in{p}{j}") for j in range(NB)] for p in range(2)]
        ctx1_in = [sem(f"ctx1_in{p}") for p in range(2)]
        late_in = sem("late_in")
        blanked = sem("blanked")
        ro = {n: sem("r_" + n) for n in (
            "ln", "rec", "xT_pe", "xT", "l_pe", "logits", "v", "exp", "pe", "place", "blocks", "placed", "tables",
            "var", "pow", "scale")}
        ex = {n: sem("m_" + n) for n in ("xT_pe", "xT", "up_pe", "hid", "t_pe", "hidT", "y_pe", "y2", "y", "idle")}
        x_in = [sem(f"x_in{n}") for n in range(4)]
        rows_in = [sem(f"rows_in{n}") for n in range(4)]
        rows_out = [sem(f"rows_out{n}") for n in range(4)]
        zeroed = sem("zeroed")
        padded = sem("padded")
        chained = sem("chained")
        tern_set = sem("tern_set")
        consts_set = sem("consts_set")
        powers_set = sem("powers_set")
        tanh_set = sem("tanh_set")
        prep_v = sem("prep_v")
        prep_pe = sem("prep_pe")
        prep_a = sem("prep_a")
        absum_set = sem("absum_set")
        wo1_set = sem("wo1_set")
        weights_set = sem("weights_set")
        a = {n: sem("a_" + n) for n in (
            "ln", "xcT_pe", "xcT", "q_pe", "k_pe", "v_pe", "qk", "v", "s_pe", "biased", "max", "shifted", "exp",
            "mask", "stats", "rstd", "den", "rden", "normed", "t_pe", "prT", "pv_pe", "oT", "y_pe", "x", "row_stats")}
        f = {n: sem("f_" + n) for n in (
            "ln", "xT_pe", "xT", "up_pe", "gel", "sq", "rms", "eps", "rrms", "t_pe", "gelT", "y_pe", "x", "row_stats",
            "var", "pow", "scale")}
        c = {n: sem("c_" + n) for n in (
            "ln", "xcT_pe", "hi", "lo", "u_pe", "u_hi", "u", "w_pe", "w", "s_pe", "max", "shifted", "exp", "den",
            "rden", "normed", "p_pe", "prT", "y_pe", "x", "row_stats", "var", "pow", "scale")}

        v0_diag = [work[0:S, p * H * D:p * H * D + H * (D + HD0)].rearrange("s (h c) -> s h c", c=D + HD0)[:, :, 0:HD0]
                   for p in range(2)]

        def bcast(row, n):
            return row.rearrange("(o d) -> o d", o=1).to_broadcast([n, row.shape[0]])

        block = stack.enter_context(nc.Block())

        @block.sync
        def _(sp):
            def load_seq(it, half, par):
                at_least(sp, a["xcT_pe"], it - 1)
                sp.dma_start(xs[:, bass.ds(it, 1), :].rearrange("l o d -> l (o d)"), x[bass.ds(it, 1), :, :].rearrange("o l d -> (o l) d")).then_inc(xc_in[par], 16)
                sp.dma_start(ctx_tok[:, par, :], ctx_in[bass.ds(it, 1), :, :].rearrange("o s d -> (o s) d")).then_inc(xc_in[par], 16)
                at_least(sp, a["mask"], it - 1)
                sp.dma_start(mask_i[:, par, :], mask[bass.ds(it, 1), 0, :, :].rearrange("o l s -> (o l) s")).then_inc(mask_in[par], 16)
                for j in range(NB):
                    at_least(sp, a["biased"], NB * (it - 2) + j + 1)
                    sp.dma_start(bias_t[:, par, HB * j:HB * j + HB, :],
                                 bias[bass.ds(it, 1), HB * j:HB * j + HB, :, :].rearrange("o h l s -> l (o h) s")
                                 ).then_inc(bias_in[par][j], 16)

            sp.dma_start(wq0_raw[:], Wq0).then_inc(wqk0_in, 16)
            sp.dma_start(wk0_raw[:], Wk0).then_inc(wqk0_in, 16)
            load_seq(0, 0, 0)
            load_seq(1, 0, 1)
            sp.dma_start(wv0[:], Wv0).then_inc(wvo0_in, 16)
            sp.dma_start(wo0[:], Wo0).then_inc(wvo0_in, 16)
            sp.dma_start(bv0_row[:], bv0.rearrange("(o d) -> o d", o=1)).then_inc(wvo0_in, 16)
            sp.dma_start(bo0_row[:], bo0.rearrange("(o d) -> o d", o=1)).then_inc(wvo0_in, 16)
            sp.dma_start(up_raw, w_up.rearrange("(c p) d -> p c d", p=128)).then_inc(w_in, 16)
            sp.dma_start(down_raw, w_down.rearrange("d (c l) -> d c l", c=FC)).then_inc(w_in, 16)
            sp.dma_start(wq1_raw, Wq1).then_inc(w_in, 16)
            sp.dma_start(wk1_raw, Wk1).then_inc(w_in, 16)
            sp.dma_start(wv1_raw, Wv1.rearrange("d (c l) -> d c l", l=128)).then_inc(w_in, 16)
            sp.dma_start(wo1[:], Wo1.rearrange("(c p) n -> p c n", p=128)).then_inc(w_in, 16)
            sp.wait_ge(ro["tables"], 2)
            sp.dma_start(sorted_rows.rearrange("(j p) c -> p j c", p=128),
                         blank[:].unsqueeze(1).to_broadcast([128, BLOCKS, REC])).then_inc(blanked, 16)
            with sp.Fori(1, B // 2) as pair:
                load_seq(pair * 2, pair, 0)
                load_seq(pair * 2 + 1, pair, 1)
            sp.dma_start(w_gate_t[:], w_gate).then_inc(late_in, 16)
            sp.dma_start(bg_bc[:], bcast(b_gate, 128)).then_inc(late_in, 16)
            sp.dma_start(b2_bc[:].rearrange("p e d -> p (e d)"), bcast(b2.rearrange("e d -> (e d)"), 128)).then_inc(late_in, 16)
            sp.wait_ge(a["biased"], NB * B)
            sp.dma_start(w1_t[:].rearrange("d (e m) -> d e m", e=E), W1.rearrange("e d m -> d e m")).then_inc(late_in, 16)
            sp.wait_ge(prep_pe, 4)
            sp.dma_start(w2_t[:].rearrange("p (e c d) -> p e c d", e=E, c=MC), W2.rearrange("e (c p) d -> p e c d", p=128)
                         ).then_inc(late_in, 16)

            def load_ctx(it, par):
                at_least(sp, c["xcT_pe"], it - 1)
                sp.dma_start(ctx_tok[:, par, :], ctx_in[bass.ds(it, 1), :, :].rearrange("o s d -> (o s) d")).then_inc(ctx1_in[par], 16)

            sp.wait_ge(a["xcT_pe"], B)
            load_ctx(0, 0)
            load_ctx(1, 1)
            with sp.Fori(1, B // 2) as pair:
                load_ctx(pair * 2, 0)
                load_ctx(pair * 2 + 1, 1)
            sp.wait_ge(c["p_pe"], NB * B)
            sp.dma_start(b1_t[:], bcast(b1.rearrange("e m -> (e m)"), 128)).then_inc(late_in, 16)

            sorted_blocks = sorted_rows.rearrange("(j p) c -> j p c", p=128)

            def load_rows(it, use, slot):
                at_least(sp, ex["xT_pe"], it - 3)
                sp.wait_ge(ro["placed"], 16 * B)
                sp.dma_start(rows_n[:, slot, :], sorted_blocks[bass.ds(it, 1), :, 0:D].rearrange("o p c -> (o p) c")
                             ).then_inc(rows_in[slot], 16)
                at_least(sp, rows_out[slot], use * 16)
                sp.wait_ge(ro["placed"], 16 * B)
                sp.dma_start(rows_x[:, slot, :], sorted_blocks[bass.ds(it, 1), :, D:REC].rearrange("o p c -> (o p) c")
                             ).then_inc(x_in[slot], 16)

            for it in range(4):
                load_rows(it, 0, it)
            with sp.Fori(1, BLOCKS // 4) as turn:
                for k in range(4):
                    load_rows(turn * 4 + k, turn, k)
            for it in range(BLOCKS // 4 * 4, BLOCKS):
                load_rows(it, it // 4, it % 4)

        W_ALL = 16 * 6

        @block.gpsimd
        def _(pool):
            pool.memset(bq0_col[:], 0.0).then_inc(zeroed, 1)
            pool.memset(bk0_col[:], 0.0).then_inc(zeroed, 1)
            pool.wait_ge(zeroed, 2)
            bq_v = bq0.rearrange("(j g d) -> j d g", j=NB, g=HB)
            bk_v = bk0.rearrange("(j g d) -> j d g", j=NB, g=HB)
            with nc.allow_non_contiguous_dma(reason="two 512-byte vectors laid along partitions"):
                for j in range(NB):
                    pool.dma_start(bq0_col[32 * j:32 * j + HD0, :], bq_v[j]).then_inc(g_in, 16)
                    pool.dma_start(bk0_col[32 * j:32 * j + HD0, :], bk_v[j]).then_inc(g_in, 16)
            pool.dma_start(gates[:, 0:2], bcast(g_xattn, 128)).then_inc(g_in, 16)
            pool.dma_start(gates[:, 2:4], bcast(g_ffn, 128)).then_inc(g_in, 16)
            pool.memset(ones[:], 1.0).then_inc(consts_set, 1)
            pool.memset(ident[:], 1.0).then_inc(consts_set, 1)
            pool.memset(ident_bf[:], 1.0).then_inc(consts_set, 1)
            pool.wait_ge(consts_set, 3)
            pool.affine_select(out=ident[:], in_=ident[:], compare_op=ALU.is_equal, fill=0.0, base=0,
                               pattern=[[-1, 128]], channel_multiplier=1).then_inc(consts_set, 1)
            pool.affine_select(out=ident_bf[:], in_=ident_bf[:], compare_op=ALU.is_equal, fill=0.0, base=0,
                               pattern=[[-1, 128]], channel_multiplier=1).then_inc(consts_set, 1)
            for n, power in enumerate((0.5, -0.5, -1.0, LN_EPS, RMS_EPS, 1.0 / F)):
                pool.memset(powers[:, n:n + 1], power).then_inc(powers_set, 1)
            pool.wait_ge(powers_set, 6)
            pool.memset(work[0:S, :], 0.0).then_inc(consts_set, 1)
            pool.memset(blank[:, 0:TOKEN], 0.0).then_inc(ro["tables"], 1)
            pool.memset(blank[:, TOKEN:REC].bitcast(I32), 1 << 30).then_inc(ro["tables"], 1)
            pool.memset(before[:], 1.0).then_inc(ro["tables"], 1)
            pool.memset(before_e[:], 1.0).then_inc(ro["tables"], 1)
            pool.memset(ones_bf[:], 1.0).then_inc(ro["tables"], 1)
            pool.wait_ge(ro["tables"], 5)
            pool.affine_select(out=before[:], in_=before[:], compare_op=ALU.is_gt, fill=0.0, base=0,
                               pattern=[[1, 128]], channel_multiplier=-1).then_inc(ro["tables"], 1)
            pool.affine_select(out=before_e[:], in_=before_e[:], compare_op=ALU.is_gt, fill=0.0, base=0,
                               pattern=[[1, E], [-1, E]], channel_multiplier=0).then_inc(ro["tables"], 1)
            pool.iota(experts[:], pattern=[[0, B], [1, E]], base=0, channel_multiplier=0,
                      allow_small_or_imprecise_dtypes=True).then_inc(ro["tables"], 1)
            pool.iota(block_rows[:], pattern=[[128, B]], base=0, channel_multiplier=0,
                      allow_small_or_imprecise_dtypes=True).then_inc(ro["tables"], 1)
            pool.iota(block_no[:], pattern=[[1, BLOCKS]], base=0, channel_multiplier=0,
                      allow_small_or_imprecise_dtypes=True).then_inc(ro["tables"], 1)
            pool.iota(rec[:, :, TOKEN:REC].bitcast(I32), pattern=[[128, B]], base=0, channel_multiplier=1
                      ).then_inc(ro["tables"], 1)

            def inv_std(it, par, s):
                pool.wait_ge(s["stats"], 2 * it + 2)
                at_least(pool, s["ln"], it - 1)
                pool.tensor_tensor(rstd[:, par:par + 1], mv[:, par, 1:2], powers[:, 3:4], ALU.add).then_inc(s["rstd"], 1)
                pool.wait_ge(s["rstd"], 2 * it + 1)
                pool.tensor_tensor(rstd[:, par:par + 1], rstd[:, par:par + 1], powers[:, 1:2], ALU.pow
                                   ).then_inc(s["rstd"], 1)

            def attn0(it, half, par):
                if live(it, B):
                    for j in range(NB):
                        s = sc[:, par, HB * j:HB * j + HB, :]
                        pool.wait_ge(a["max"], NB * it + j + 1)
                        pool.tensor_tensor(s, s, mx[:, par, HB * j:HB * j + HB].unsqueeze(2).to_broadcast([L, HB, S]),
                                           ALU.subtract).then_inc(a["shifted"], 1)
                        if j == 1 and live(it + 2, B):
                            inv_std(it + 2, par, a)
                    for j in range(NB):
                        scale_probs(it, par, j, a)
                elif live(it + 2, B):
                    inv_std(it + 2, par, a)

            def scale_probs(it, par, j, s):
                p = sc[:, par, HB * j:HB * j + HB, :]
                pool.wait_ge(s["rden"], NB * it + j + 1)
                pool.tensor_tensor(p, p, rden[:, par, HB * j:HB * j + HB].unsqueeze(2).to_broadcast([L, HB, S]),
                                   ALU.mult).then_inc(s["normed"], 1)

            inv_std(0, 0, a)
            staged(pool, B, attn0)

            def powers_of_var(s, with_root):
                pool.wait_ge(s["var"], 7)
                pool.tensor_tensor(tmp_all[:, 4, :], tmp_all[:, 3, :], powers[:, 1:2].to_broadcast([128, B]), ALU.pow
                                   ).then_inc(s["pow"], 1)
                if with_root:
                    pool.tensor_tensor(tmp_all[:, 5, :], tmp_all[:, 2, :], powers[:, 0:1].to_broadcast([128, B]), ALU.pow
                                       ).then_inc(s["pow"], 1)

            powers_of_var(f, True)

            def ffn_rms(it, half, par):
                if live(it - 1, B):
                    pool.wait_ge(f["sq"], it)
                    at_least(pool, f["eps"], it - 2)
                    pool.tensor_tensor(rms[:, 1 - par:2 - par], ssq[:, 1 - par:2 - par], powers[:, 0:1], ALU.pow
                                       ).then_inc(f["rms"], 1)

            staged(pool, B, ffn_rms)
            powers_of_var(c, False)

            def attn1(it, half, par):
                if live(it, B):
                    for j in range(NB):
                        scale_probs(it, par, j, c)

            staged(pool, B, attn1)
            powers_of_var(ro, False)

            pool.wait_ge(ro["place"], 1)
            pool.wait_ge(ro["rec"], B + 1)
            pool.wait_ge(blanked, 16)
            for b in range(B):
                pool.indirect_dma_start(out=sorted_rows, out_offset=bass.IndirectOffsetOnAxis(ap=place[:, b:b + 1], axis=0),
                                        in_=rec[:, b, :], in_offset=None, bounds_check=BLOCKS * 128 - 1, oob_is_err=False
                                        ).then_inc(ro["placed"], 16)

            out_rows = out.rearrange("b l d -> (b l) d")

            def store_rows(it, use, slot):
                old = it - 2
                oslot = (slot + 2) % 4
                if live(old, BLOCKS):
                    pool.wait_ge(ex["y"], old + 1)
                    at_least(pool, ex["idle"], old)
                    pool.tensor_tensor(idle[:], powers[:, 0:1], powers[:, 0:1], ALU.add).then_inc(ex["idle"], 1)
                    pool.indirect_dma_start(out=out_rows,
                                            out_offset=bass.IndirectOffsetOnAxis(
                                                ap=rows_x[:, oslot, TOKEN - D:REC - D].bitcast(I32), axis=0),
                                            in_=y_out[:, oslot, :], in_offset=None, bounds_check=NT - 1, oob_is_err=False
                                            ).then_inc(rows_out[oslot], 16)

            staged_slots(pool, BLOCKS, store_rows)
            for n in range(4):
                pool.wait_ge(rows_out[n], 16 * ((BLOCKS - n + 3) // 4))

        @block.tensor
        def _(pe):
            pe.wait_ge(consts_set, 6)

            def attn0(it, half, par):
                nxt, prv, old = it + 1, it - 1, it - 2
                npar = 1 - par

                def transpose_probs(j):
                    pe.wait_ge(a["normed"], NB * prv + j + 1)
                    at_least(pe, a["prT"], NB * prv + j - 1)
                    for n in range(HB):
                        mm = pe.transpose(bank[4 + j % 2][0:S, n * L:n * L + L], sc[:, npar, HB * j + n, :], ident[:])
                    mm.then_inc(a["t_pe"], 1)

                def scores(j):
                    at_least(pe, a["biased"], NB * prv + j + 1)
                    if j == 0:
                        pe.wait_ge(a["mask"], it + 1)
                        pe.wait_ge(a["qk"], 2 * it + 2)
                    pe.matmul(bank[j][:, 0:HB * S].rearrange("p (h s) -> p h s", h=HB), ident_bf[:],
                              mask_b[:, par, :].unsqueeze(1).to_broadcast([L, HB, S]), start=True, stop=False)
                    for n in range(HB):
                        mm = pe.matmul(bank[j][:, n * S:n * S + S], qT[32 * j:32 * j + HD0, par, n, :],
                                       kT[32 * j:32 * j + HD0, par, n, :], start=False, stop=(n == HB - 1))
                    mm.then_inc(a["s_pe"], 1)

                if live(it, B):
                    scores(0)
                    scores(1)
                if live(old, B):
                    pe.wait_ge(a["oT"], old + 1)
                    pe.matmul(bank[6][:, 0:D], o0T[:], wo0[:], start=True, stop=False)
                    pe.matmul(bank[6][:, 0:D], ones[0:1, 0:L], bo0_row[:], start=False, stop=True).then_inc(a["y_pe"], 1)
                if live(it, B):
                    scores(2)
                    scores(3)
                if live(prv, B):
                    transpose_probs(0)
                    transpose_probs(1)
                if live(nxt, B):
                    pe.wait_ge(a["ln"], nxt + 1)
                    pe.wait_ge(xc_in[npar], (half + par) * 32 + 32)
                    at_least(pe, a["v"], nxt)
                    pe.transpose(bank[7][:, 0:L], xn[:, npar, :], ident[:])
                    pe.transpose(bank[7][:, L:L + S], ctx_tok[:, npar, :], ident[0:S, 0:S]).then_inc(a["xcT_pe"], 1)
                if live(prv, B):
                    transpose_probs(2)
                    transpose_probs(3)
                xT = xcT[:, npar, 0:L]
                cT = xcT[:, npar, L:L + S]
                at_least(pe, a["x"], old + 1 if live(old, B) else 0)
                if live(nxt, B):
                    pe.wait_ge(a["xcT"], nxt + 1)
                    for n in range(HB):
                        mm = pe.matmul(bank[6][:, n * L:n * L + L], wq0_pad[:, n, :, :].rearrange("p j r -> p (j r)"), xT,
                                       start=(n == 0), stop=(n == HB - 1), skip_group_check=True)
                    mm.then_inc(a["q_pe"], 1)
                    for n in range(HB):
                        mm = pe.matmul(bank[7][:, n * S:n * S + S], wk0_pad[:, n, :, :].rearrange("p j r -> p (j r)"), cT,
                                       start=(n == 0), stop=(n == HB - 1), skip_group_check=True)
                    mm.then_inc(a["k_pe"], 1)
                if live(prv, B):
                    pe.wait_ge(a["prT"], NB * prv + NB)
                    pe.wait_ge(a["v"], prv + 1)
                    if live(nxt, B):
                        pe.wait_ge(a["qk"], 2 * nxt + 1)
                    for h in range(H):
                        mm = pe.matmul(bank[6][:, 0:L], v0[:, npar, h, :], prT[:, h, :], start=(h == 0), stop=(h == H - 1))
                    mm.then_inc(a["pv_pe"], 1)
                if live(nxt, B):
                    pe.wait_ge(a["qk"], 2 * nxt + 2)
                    pe.matmul(bank[7][0:S, 0:H * HD0], cT, wv0[:], start=True, stop=False)
                    pe.matmul(bank[7][0:S, 0:H * HD0], ones[0:1, 0:S], bv0_row[:], start=False, stop=True
                              ).then_inc(a["v_pe"], 1)

            pe.wait_ge(wvo0_in, 64)
            pe.wait_ge(weights_set, 1)
            staged(pe, B, attn0)

            pe.wait_ge(a["x"], B)
            pe.wait_ge(w_in, W_ALL)
            wq1_chunks, wk1_chunks = (w.rearrange("d (c l) -> d c l", l=128) for w in (wq1_raw, wk1_raw))
            for w, b_ in ((wq1_chunks, 1), (wk1_chunks, 3), (wv1_raw, 5)):
                for n in range(C1):
                    mm = pe.transpose(bank[b_ + n // 4][:, n % 4 * 128:n % 4 * 128 + 128], w[:, n, :], ident[:])
            mm.then_inc(prep_pe, 1)
            pe.wait_ge(absum_set, 2)
            for n in range(FC):
                mm = pe.matmul(bank[0][:, 0:2], ones[:], absum[:, n, :], start=(n == 0), stop=(n == FC - 1))
            mm.then_inc(prep_pe, 1)
            pe.wait_ge(prep_v, 2)
            pe.wait_ge(prep_a, 2)
            for n in range(FC):
                pe.transpose(bank[1][:, n * 128:n * 128 + 128], tern_a[:, n, :], ident[:])
            for n in range(FC):
                mm = pe.transpose(bank[2][:, n * 128:n * 128 + 128], tern_b[:, n, :], ident[:])
            mm.then_inc(prep_pe, 1)
            pe.wait_ge(prep_a, 6)
            for n in range(C1):
                for r in range(2):
                    mm = pe.matmul(bank[3 + 2 * r + n // 4][:, n % 4 * 128:n % 4 * 128 + 128],
                                   wk1T[64 * r:64 * r + 64, n, :], wq1T[64 * r:64 * r + 64, n, :],
                                   start=(n % 4 == 0), stop=(n % 4 == 3), skip_group_check=True)
            mm.then_inc(prep_pe, 1)
            pe.wait_ge(prep_a, 8)
            pe.wait_ge(weights_set, 3)
            pe.wait_ge(wo1_set, 1)
            for n in range(C1):
                for r in range(2):
                    mm = pe.matmul(bank[(1 + n // 4, (7, 0)[n // 4])[r]][:, n % 4 * 128:n % 4 * 128 + 128],
                                   wv1T[64 * r:64 * r + 64, n, :], wo1[64 * r:64 * r + 64, n, :],
                                   start=(n % 4 == 0), stop=(n % 4 == 3), skip_group_check=True)
            mm.then_inc(prep_pe, 1)
            pe.wait_ge(prep_a, 16)
            pe.wait_ge(prep_v, 6)

            def ffn0(it, half, par):
                nxt, prv, old = it + 1, it - 1, it - 2
                npar = 1 - par
                if live(it, B):
                    pe.wait_ge(f["xT"], it + 1)
                    at_least(pe, f["gel"], it - 1)
                    pe.matmul(bank[par][:, 0:F].rearrange("l (c f) -> l c f", c=FC), xcT[:, par, 0:L], upT, start=True, stop=True).then_inc(f["up_pe"], 1)
                if live(nxt, B):
                    pe.wait_ge(f["ln"], nxt + 1)
                    at_least(pe, f["xT"], nxt - 1)
                    pe.transpose(bank[4 + npar][:, 0:L], xn[:, npar, :], ident[:]).then_inc(f["xT_pe"], 1)
                if live(old, B):
                    pe.wait_ge(f["gelT"], old + 1)
                    at_least(pe, f["x"], old - 1)
                    for n in range(FC):
                        mm = pe.matmul(bank[6 + par][:, 0:D], gelT[:, par, n, :], downT[:, n, :],
                                       start=(n == 0), stop=(n == FC - 1))
                    mm.then_inc(f["y_pe"], 1)
                if live(prv, B):
                    pe.wait_ge(f["gel"], prv + 1)
                    at_least(pe, f["gelT"], prv - 1)
                    for n in range(FC):
                        mm = pe.transpose(bank[2 + npar][:, n * 128:n * 128 + 128],
                                          gel[:, npar, n * 128:n * 128 + 128], ident[:])
                    mm.then_inc(f["t_pe"], 1)

            staged(pe, B, ffn0)

            def attn1(it, half, par):
                nxt, prv = it + 1, it - 1
                npar = 1 - par
                cT = xcT[:, npar, L:L + S]

                def transpose_probs(j):
                    pe.wait_ge(c["normed"], NB * prv + j + 1)
                    at_least(pe, c["prT"], NB * prv + j - 1)
                    for n in range(HB):
                        mm = pe.transpose(bank[2 + j % 2][0:S, n * L:n * L + L], sc[:, npar, HB * j + n, :], ident[:])
                    mm.then_inc(c["p_pe"], 1)

                def scores(j):
                    pe.wait_ge(c["u"], NB * it + j + 1)
                    at_least(pe, c["shifted"], NB * it + j - 1)
                    hi, lo = xcT_hi[:, par, 0:L], xcT_lo[:, par, 0:L]
                    uh = u_hi[:, par, HB * j:HB * j + HB, :].rearrange("p h s -> p (h s)")
                    ul = u_lo[:, par, HB * j:HB * j + HB, :].rearrange("p h s -> p (h s)")
                    b_ = bank[j % 2][:, 0:HB * S]
                    pe.matmul(b_, hi, uh, start=True, stop=False)
                    pe.matmul(b_, hi, ul, start=False, stop=False)
                    pe.matmul(b_, lo, uh, start=False, stop=True).then_inc(c["s_pe"], 1)

                def project_u(j):
                    if j < 2:
                        at_least(pe, c["w"], NB * it + j + 3 if live(it, B) else 0)
                    else:
                        pe.wait_ge(c["u"], NB * nxt + j - 1)
                    for n in range(HB):
                        mm = pe.matmul(bank[4 + j % 2][:, n * S:n * S + S], kq1[:, HB * j + n, :], cT,
                                       start=(n == 0), stop=(n == HB - 1), skip_group_check=True)
                    mm.then_inc(c["u_pe"], 1)

                def project_w(j):
                    if j < 2:
                        pe.wait_ge(c["u"], NB * nxt + j + 3)
                    else:
                        pe.wait_ge(c["w"], NB * nxt + j - 1)
                    hi, lo = xcT_hi[:, npar, L:L + S], xcT_lo[:, npar, L:L + S]
                    vh = vo1_hi[:, HB * j:HB * j + HB, :].rearrange("p h n -> p (h n)")
                    vl = vo1_lo[:, HB * j:HB * j + HB, :].rearrange("p h n -> p (h n)")
                    b_ = bank[4 + j % 2][0:S, :]
                    pe.matmul(b_, hi, vh, start=True, stop=False)
                    pe.matmul(b_, hi, vl, start=False, stop=False)
                    pe.matmul(b_, lo, vh, start=False, stop=True).then_inc(c["w_pe"], 1)

                if live(it, B):
                    scores(0)
                    scores(1)
                if live(prv, B):
                    transpose_probs(0)
                    transpose_probs(1)
                if live(it, B):
                    scores(2)
                if live(nxt, B):
                    pe.wait_ge(c["ln"], nxt + 1)
                    pe.wait_ge(ctx1_in[npar], (half + par) * 16 + 16)
                    at_least(pe, c["hi"], 2 * nxt)
                    at_least(pe, c["lo"], nxt)
                    pe.transpose(bank[6][:, 0:L], xn[:, npar, :], ident[:])
                    pe.transpose(bank[6][:, L:L + S], ctx_tok[:, npar, :], ident[0:S, 0:S]).then_inc(c["xcT_pe"], 1)
                if live(it, B):
                    scores(3)
                if live(prv, B):
                    transpose_probs(2)
                    transpose_probs(3)
                if live(nxt, B):
                    pe.wait_ge(c["hi"], 2 * nxt + 2)
                    for j in range(NB):
                        project_u(j)
                if live(prv, B):
                    pe.wait_ge(c["prT"], NB * prv + NB)
                    pe.wait_ge(c["w"], NB * prv + NB)
                    at_least(pe, c["x"], prv)
                    for h in range(H):
                        mm = pe.matmul(bank[7][:, 0:D], prT[:, h, :], w_vo[:, npar, h, :], start=(h == 0), stop=(h == H - 1))
                    mm.then_inc(c["y_pe"], 1)
                if live(nxt, B):
                    pe.wait_ge(c["lo"], nxt + 1)
                    for j in range(NB):
                        project_w(j)

            pe.wait_ge(f["x"], B)
            staged(pe, B, attn1)

            def route(it, half, par):
                nxt = it + 1
                npar = 1 - par
                if live(nxt, B):
                    pe.wait_ge(ro["ln"], nxt + 1)
                    at_least(pe, ro["xT"], nxt - 1)
                    pe.transpose(bank[npar][:, 0:L], xn[:, npar, :], ident[:]).then_inc(ro["xT_pe"], 1)
                if live(it, B):
                    pe.wait_ge(ro["xT"], it + 1)
                    at_least(pe, ro["logits"], it - 1)
                    pe.matmul(bank[2 + par][:, 0:E], xcT[:, par, 0:L], w_gate_t[:], start=True, stop=True
                              ).then_inc(ro["l_pe"], 1)

            pe.wait_ge(c["x"], B)
            pe.wait_ge(late_in, 16 * 6)
            staged(pe, B, route)
            pe.wait_ge(ro["v"], 7)
            for e in range(E):
                mm = pe.matmul(bank[4][0:B, e:e + 1], onehot_bf[:, e, :], ones_bf[:, 0:1], start=(e == 0), stop=(e == E - 1),
                               skip_group_check=True)
            mm.then_inc(ro["pe"], 1)
            pe.wait_ge(ro["v"], 9)
            pe.matmul(bank[5][:, 0:B * E].rearrange("p (e b) -> p e b", e=E), before_bf[:], onehot_bf[:], start=True, stop=False)
            pe.matmul(bank[5][:, 0:B * E].rearrange("p (e b) -> p b e", e=E), ones_bf[0:B, :], seq_before[:], start=False, stop=True)
            pe.matmul(bank[6][:, 0:E], ones_bf[0:B, :], seq_count[:], start=True, stop=True).then_inc(ro["pe"], 1)

            def expert(it, use, slot):
                nxt, prv, old = it + 1, it - 1, it - 2
                par = slot % 2
                npar = 1 - par
                nslot = (slot + 1) % 4
                if live(it, BLOCKS):
                    e = pe.value_load(block_e[0:1, bass.ds(it, 1)], min_val=0, max_val=E - 1)
                    pe.wait_ge(ex["xT"], it + 1)
                    at_least(pe, ex["hid"], it - 1)
                    pe.matmul(bank[par][:, 0:M], rowT[:, par, :], w1_t[:, bass.ds(e * M, M)], start=True, stop=True
                              ).then_inc(ex["up_pe"], 1)
                if live(nxt, BLOCKS):
                    pe.wait_ge(rows_in[nslot], (use + (slot + 1) // 4) * 16 + 16)
                    at_least(pe, ex["xT"], nxt - 1)
                    pe.transpose(bank[4 + npar][:, 0:128], rows_n[:, nslot, :], ident[:]).then_inc(ex["xT_pe"], 1)
                if live(old, BLOCKS):
                    e = pe.value_load(block_e[0:1, bass.ds(old, 1)], min_val=0, max_val=E - 1)
                    pe.wait_ge(ex["hidT"], old + 1)
                    at_least(pe, ex["y2"], old - 1)
                    for n in range(MC):
                        mm = pe.matmul(bank[6 + par][:, 0:D], hidT[:, par, n, :], w2_t[:, bass.ds(e * (MC * D) + n * D, D)],
                                       start=(n == 0), stop=(n == MC - 1))
                    mm.then_inc(ex["y_pe"], 1)
                if live(prv, BLOCKS):
                    pe.wait_ge(ex["hid"], prv + 1)
                    at_least(pe, ex["hidT"], prv - 1)
                    for n in range(MC):
                        mm = pe.transpose(bank[2 + npar][:, n * 128:n * 128 + 128], hid[:, npar, n * 128:n * 128 + 128],
                                          ident[:])
                    mm.then_inc(ex["t_pe"], 1)

            pe.wait_ge(ro["blocks"], 1)
            staged_slots(pe, BLOCKS, expert)

        @block.scalar
        def _(act):
            act.wait_ge(g_in, 16 * (2 * NB + 2))
            act.activation(tg[:], gates[:], ACT.Tanh).then_inc(tanh_set, 1)

            def attn0(it, half, par):
                nxt, prv = it + 1, it - 1
                npar = 1 - par

                def copy_probs(j):
                    act.wait_ge(a["t_pe"], NB * prv + j + 1)
                    at_least(act, a["pv_pe"], prv)
                    act.copy(prT[:, HB * j:HB * j + HB, :].rearrange("p h l -> p (h l)"), bank[4 + j % 2][0:S, :]
                             ).then_inc(a["prT"], 1)

                def exponent(j):
                    p = sc[:, par, HB * j:HB * j + HB, :]
                    act.wait_ge(a["shifted"], NB * it + j + 1)
                    act.activation(p, p, ACT.Exp).then_inc(a["exp"], 1)

                if live(it, B):
                    exponent(0)
                if live(prv, B):
                    copy_probs(0)
                    copy_probs(1)
                if live(nxt, B):
                    act.wait_ge(a["xcT_pe"], nxt + 1)
                    at_least(act, a["v_pe"], nxt - 1)
                    act.copy(xcT[:, npar, :], bank[7][:, 0:L + S]).then_inc(a["xcT"], 1)
                if live(it, B):
                    exponent(1)
                if live(prv, B):
                    copy_probs(2)
                if live(it, B):
                    exponent(2)
                if live(prv, B):
                    copy_probs(3)
                if live(it, B):
                    exponent(3)
                if live(prv, B):
                    act.wait_ge(a["pv_pe"], prv + 1)
                    at_least(act, a["y_pe"], prv)
                    act.copy(o0T[:], bank[6][:, 0:L]).then_inc(a["oT"], 1)
                if live(nxt, B):
                    act.wait_ge(a["v_pe"], nxt + 1)
                    at_least(act, a["pv_pe"], nxt - 1)
                    act.copy(v0_diag[npar], bank[7][0:S, 0:H * HD0].rearrange("s (h d) -> s h d", h=H)
                             ).then_inc(a["v"], 1)

            staged(act, B, attn0)

            act.wait_ge(prep_pe, 1)
            for w, b_ in ((wq1T, 1), (wk1T, 3), (wv1T, 5)):
                for n in range(2):
                    act.copy(w[:, 4 * n:4 * n + 4, :].rearrange("p c d -> p (c d)"), bank[b_ + n][:]).then_inc(prep_a, 1)
            act.wait_ge(prep_pe, 3)
            act.copy(upT, bank[1][:].rearrange("p (c d) -> p c d", c=FC)).then_inc(prep_a, 1)
            act.mul(downT, bank[2][:].rearrange("p (c d) -> p c d", c=FC), tg[:, 2:3]).then_inc(prep_a, 1)
            act.wait_ge(prep_pe, 4)
            for r in range(2):
                for n in range(2):
                    act.mul(kq1[:, 8 * n + r:8 * n + r + 7:2, :],
                            bank[3 + 2 * r + n][:].rearrange("p (h e) -> p h e", h=4), SCALE1).then_inc(prep_a, 1)
            act.wait_ge(prep_pe, 5)
            for r in range(2):
                for n in range(2):
                    act.copy(vo1_hi[:, 8 * n + r:8 * n + r + 7:2, :],
                             bank[(1 + n, (7, 0)[n])[r]][:].rearrange("p (h e) -> p h e", h=4)).then_inc(prep_a, 1)

            def ffn0(it, half, par):
                nxt, prv = it + 1, it - 1
                npar = 1 - par
                if live(nxt, B):
                    act.wait_ge(f["xT_pe"], nxt + 1)
                    at_least(act, f["up_pe"], nxt - 1)
                    act.copy(xcT[:, npar, 0:L], bank[4 + npar][:, 0:L]).then_inc(f["xT"], 1)
                if live(it, B):
                    act.wait_ge(f["up_pe"], it + 1)
                    at_least(act, f["t_pe"], it - 1)
                    at_least(act, f["sq"], it - 1)
                    act.activation(gel[:, par, :], bank[par][:, 0:F], ACT.Gelu).then_inc(f["gel"], 1)
                if live(prv, B):
                    act.wait_ge(f["t_pe"], prv + 1)
                    at_least(act, f["y_pe"], prv - 1)
                    act.copy(gelT[:, npar, :, :].rearrange("p c l -> p (c l)"), bank[2 + npar][:]).then_inc(f["gelT"], 1)

            staged(act, B, ffn0)

            def attn1(it, half, par):
                nxt, prv = it + 1, it - 1
                npar = 1 - par

                def copy_probs(j):
                    act.wait_ge(c["p_pe"], NB * prv + j + 1)
                    at_least(act, c["y_pe"], prv)
                    act.copy(prT[:, HB * j:HB * j + HB, :].rearrange("p h l -> p (h l)"), bank[2 + j % 2][0:S, :]
                             ).then_inc(c["prT"], 1)

                def exponent(j):
                    p = sc[:, par, HB * j:HB * j + HB, :]
                    act.wait_ge(c["shifted"], NB * it + j + 1)
                    act.activation(p, p, ACT.Exp).then_inc(c["exp"], 1)

                def high_u(j):
                    act.wait_ge(c["u_pe"], NB * nxt + j + 1)
                    at_least(act, c["s_pe"], NB * (nxt - 2) + j + 1)
                    act.copy(u_hi[:, npar, HB * j:HB * j + HB, :].rearrange("p h s -> p (h s)"),
                             bank[4 + j % 2][:, 0:HB * S]).then_inc(c["u_hi"], 1)

                if live(it, B):
                    exponent(0)
                if live(prv, B):
                    copy_probs(0)
                if live(it, B):
                    exponent(1)
                if live(prv, B):
                    copy_probs(1)
                if live(nxt, B):
                    act.wait_ge(c["xcT_pe"], nxt + 1)
                    at_least(act, c["w_pe"], NB * (nxt - 1))
                    act.copy(xcT_hi[:, npar, :], bank[6][:, 0:L + S]).then_inc(c["hi"], 1)
                    act.copy(xcT[:, npar, L:L + S], bank[6][:, L:L + S]).then_inc(c["hi"], 1)
                if live(it, B):
                    exponent(2)
                if live(prv, B):
                    copy_probs(2)
                    copy_probs(3)
                if live(it, B):
                    exponent(3)
                if live(nxt, B):
                    for j in range(NB):
                        high_u(j)
                    for j in range(NB):
                        act.wait_ge(c["w_pe"], NB * nxt + j + 1)
                        at_least(act, c["y_pe"], nxt - 1)
                        act.copy(w_vo[:, npar, HB * j:HB * j + HB, :].rearrange("p h n -> p (h n)"), bank[4 + j % 2][0:S, :]
                                 ).then_inc(c["w"], 1)

            staged(act, B, attn1)

            def route(it, half, par):
                nxt = it + 1
                npar = 1 - par
                if live(nxt, B):
                    act.wait_ge(ro["xT_pe"], nxt + 1)
                    at_least(act, ro["l_pe"], nxt - 1)
                    act.copy(xcT[:, npar, 0:L], bank[npar][:, 0:L]).then_inc(ro["xT"], 1)

            staged(act, B, route)
            act.wait_ge(ro["v"], 2)
            act.activation(route_b[:], route_a[:], ACT.Exp).then_inc(ro["exp"], 1)

            def expert(it, use, slot):
                nxt, prv = it + 1, it - 1
                par = slot % 2
                npar = 1 - par
                if live(nxt, BLOCKS):
                    act.wait_ge(ex["xT_pe"], nxt + 1)
                    at_least(act, ex["up_pe"], nxt - 1)
                    act.copy(rowT[:, npar, :], bank[4 + npar][:, 0:128]).then_inc(ex["xT"], 1)
                if live(prv, BLOCKS):
                    act.wait_ge(ex["t_pe"], prv + 1)
                    at_least(act, ex["y_pe"], prv - 1)
                    act.activation(hidT[:, npar, :, :].rearrange("p c l -> p (c l)"), bank[2 + npar][:], ACT.Relu
                                   ).then_inc(ex["hidT"], 1)

            staged_slots(act, BLOCKS, expert)

        @block.vector
        def _(dve):
            dve.memset(wq0_pad[:], 0.0).then_inc(padded, 1)
            dve.memset(wk0_pad[:], 0.0).then_inc(padded, 1)
            dve.wait_ge(padded, 2)
            dve.wait_ge(wqk0_in, 32)
            dve.tensor_scalar(wq0_pad[:, :, :, 0:HD0], wq0_raw[:].rearrange("p (j g d) -> p g j d", j=NB, g=HB),
                              SCALE0, None, ALU.mult).then_inc(chained, 1)
            dve.tensor_copy(wk0_pad[:, :, :, 0:HD0], wk0_raw[:].rearrange("p (j g d) -> p g j d", j=NB, g=HB)
                            ).then_inc(chained, 1)
            dve.wait_ge(g_in, 16 * (2 * NB + 2))
            dve.tensor_scalar(bq0_col[:], bq0_col[:], SCALE0, None, ALU.mult).then_inc(chained, 1)
            dve.wait_ge(tanh_set, 1)
            dve.wait_ge(wvo0_in, 64)
            dve.tensor_scalar(wo0[:], wo0[:], tg[:, 0:1], None, ALU.mult).then_inc(chained, 1)
            dve.tensor_scalar(bo0_row[:], bo0_row[:], tg[0:1, 0:1], None, ALU.mult).then_inc(chained, 1)
            dve.wait_ge(chained, 5)
            dve.sem_inc(weights_set, 1)

            def all_scales(s, rows_done, with_rms):
                me, mo, ve, vo = (stats_all[:, :, n] for n in (1, 4, 2, 5))
                t = [tmp_all[:, n, :] for n in range(6)]
                dve.wait_ge(rows_done, B)
                dve.tensor_tensor(t[0], me, mo, ALU.add).then_inc(s["var"], 1)
                dve.tensor_tensor(t[1], me, mo, ALU.subtract).then_inc(s["var"], 1)
                dve.tensor_tensor(t[2], ve, vo, ALU.add).then_inc(s["var"], 1)
                dve.wait_ge(s["var"], 3)
                dve.tensor_scalar(mean_all[:], t[0], 0.5, None, ALU.mult).then_inc(s["var"], 1)
                dve.scalar_tensor_tensor(out=t[1], in0=t[1], scalar=0.25, in1=t[1], op0=ALU.mult, op1=ALU.mult
                                         ).then_inc(s["var"], 1)
                dve.wait_ge(s["var"], 5)
                dve.scalar_tensor_tensor(out=t[2], in0=t[2], scalar=1.0 / D, in1=t[1], op0=ALU.mult, op1=ALU.add
                                         ).then_inc(s["var"], 1)
                dve.wait_ge(s["var"], 6)
                dve.tensor_scalar(t[3], t[2], LN_EPS, None, ALU.add).then_inc(s["var"], 1)
                if not with_rms:
                    dve.wait_ge(s["pow"], 1)
                    dve.tensor_copy(scale_all[:], t[4]).then_inc(s["scale"], 1)
                else:
                    dve.wait_ge(s["pow"], 2)
                    dve.tensor_tensor(t[0], t[5], t[4], ALU.mult).then_inc(s["scale"], 1)
                    dve.wait_ge(s["scale"], 1)
                    dve.tensor_scalar(t[1], t[0], RMS_EPS, None, ALU.add).then_inc(s["scale"], 1)
                    dve.wait_ge(s["scale"], 2)
                    dve.reciprocal(t[0], t[1]).then_inc(s["scale"], 1)
                    dve.wait_ge(s["scale"], 3)
                    dve.tensor_tensor(scale_all[:], t[0], t[4], ALU.mult).then_inc(s["scale"], 1)

            def seq_rows(k):
                return xs[:, bass.ds(k, 1), :].rearrange("l o d -> l (o d)")

            def normalise_all(k, par, s, transposed):
                at_least(dve, s[transposed], k - 1)
                dve.wait_ge(s["scale"], 4 if s is f else 1)
                dve.tensor_scalar(xn[:, par, :], seq_rows(k), mean_all[:, bass.ds(k, 1)], scale_all[:, bass.ds(k, 1)],
                                  ALU.subtract, ALU.mult).then_inc(s["ln"], 1)

            def stats_of(k, s):
                dve.wait_ge(s["x"], k + 1)
                dve.bn_stats(stats_all[:, bass.ds(k, 1), :].rearrange("l o n -> l (o n)"), seq_rows(k)
                             ).then_inc(s["row_stats"], 1)

            def denominators(it, par, j, s):
                cols = slice(HB * j, HB * j + HB)
                dve.wait_ge(s["exp"], NB * it + j + 1)
                dve.reduce_sum(den[:, par, cols], sc[:, par, cols, :], AX_X).then_inc(s["den"], 1)

            def reciprocals(it, par, j, s):
                cols = slice(HB * j, HB * j + HB)
                dve.wait_ge(s["den"], NB * it + j + 1)
                dve.reciprocal(rden[:, par, cols], den[:, par, cols]).then_inc(s["rden"], 1)

            def row_stats(it, par, s):
                dve.bn_stats(stats[:], xs[:, bass.ds(it, 1), :].rearrange("l o d -> l (o d)")).then_inc(s["stats"], 1)
                dve.wait_ge(s["stats"], 2 * it + 1)
                dve.memset(settle[:], 0.0)
                dve.bn_aggr(mv[:, par, :], stats[:]).then_inc(s["stats"], 1)

            def normalise(it, par, s, transposed, ready, scale):
                at_least(dve, s[transposed], it - 1)
                dve.wait_ge(s["stats"], 2 * it + 2)
                dve.wait_ge(ready[0], ready[1] * it + ready[1])
                dve.tensor_scalar(xn[:, par, :], xs[:, bass.ds(it, 1), :].rearrange("l o d -> l (o d)"),
                                  mv[:, par, 0:1], scale[:, par:par + 1], ALU.subtract, ALU.mult).then_inc(s["ln"], 1)

            def attn0(it, half, par):
                nxt, far, old = it + 1, it + 2, it - 2
                npar = 1 - par

                def add_bias(j):
                    s = sc[:, par, HB * j:HB * j + HB, :]
                    dve.wait_ge(bias_in[par][j], half * 16 + 16)
                    at_least(dve, a["t_pe"], NB * (it - 2) + j + 1)
                    dve.wait_ge(a["s_pe"], NB * it + j + 1)
                    dve.tensor_tensor(s, bank[j][:, 0:HB * S].rearrange("p (h s) -> p h s", h=HB),
                                      bias_t[:, par, HB * j:HB * j + HB, :], ALU.add).then_inc(a["biased"], 1)
                    dve.wait_ge(a["biased"], NB * it + j + 1)
                    dve.reduce_max(mx[:, par, HB * j:HB * j + HB], s, AX_X).then_inc(a["max"], 1)

                if live(it, B):
                    add_bias(0)
                    add_bias(1)
                if live(old, B):
                    dve.wait_ge(a["y_pe"], old + 1)
                    dve.tensor_tensor(seq_rows(old), bank[6][:, 0:D], seq_rows(old), ALU.add).then_inc(a["x"], 1)
                if live(far, B):
                    dve.wait_ge(xc_in[par], half * 32 + 64)
                    row_stats(far, par, a)
                if live(it, B):
                    add_bias(2)
                    add_bias(3)
                if live(old, B):
                    stats_of(old, a)
                if live(it, B):
                    denominators(it, par, 0, a)
                    denominators(it, par, 1, a)
                    reciprocals(it, par, 0, a)
                    reciprocals(it, par, 1, a)
                if live(nxt, B):
                    at_least(dve, a["s_pe"], NB * (nxt - 1))
                    dve.wait_ge(a["q_pe"], nxt + 1)
                    dve.tensor_tensor(qT[:, npar, :, :], bank[6][:].rearrange("p (g l) -> p g l", g=HB),
                                      bq0_col[:].unsqueeze(2).to_broadcast([128, HB, L]), ALU.add).then_inc(a["qk"], 1)
                    dve.wait_ge(a["k_pe"], nxt + 1)
                    dve.tensor_tensor(kT[:, npar, :, :], bank[7][:, 0:HB * S].rearrange("p (g l) -> p g l", g=HB),
                                      bk0_col[:].unsqueeze(2).to_broadcast([128, HB, S]), ALU.add).then_inc(a["qk"], 1)
                if live(it, B):
                    denominators(it, par, 2, a)
                    denominators(it, par, 3, a)
                    reciprocals(it, par, 2, a)
                    reciprocals(it, par, 3, a)
                if live(nxt, B):
                    additive_mask(nxt, half + par, npar)
                if live(far, B):
                    normalise(far, par, a, "xcT_pe", (a["rstd"], 2), rstd)

            def additive_mask(it, half, par):
                at_least(dve, a["s_pe"], NB * (it - 1))
                dve.wait_ge(mask_in[par], half * 16 + 16)
                dve.tensor_scalar(mask_b[:, par, :], mask_i[:, par, :], 0.0, MASKED, ALU.is_equal, ALU.mult
                                  ).then_inc(a["mask"], 1)

            dve.wait_ge(xc_in[0], 32)
            row_stats(0, 0, a)
            normalise(0, 0, a, "xcT_pe", (a["rstd"], 2), rstd)
            staged(dve, B, attn0)

            dve.wait_ge(w_in, W_ALL)
            for m, (w, t) in enumerate(((up_raw, tern_a), (down_raw, tern_b))):
                dve.scalar_tensor_tensor(out=t, in0=w, scalar=-1.0, in1=w, op0=ALU.mult, op1=ALU.max
                                         ).then_inc(padded, 1)
                dve.wait_ge(padded, 3 + m)
                dve.reduce_sum(absum[:, :, m], t, AX_X).then_inc(absum_set, 1)
            dve.tensor_scalar(wo1[:], wo1[:], tg[:, 1:2], None, ALU.mult).then_inc(wo1_set, 1)
            dve.wait_ge(prep_pe, 2)
            dve.tensor_scalar(thr[:, 0:2], bank[0][:, 0:2], 0.5 / (F * D), None, ALU.mult).then_inc(weights_set, 1)
            dve.tensor_scalar(thr[:, 2:4], bank[0][:, 0:2], -0.5 / (F * D), None, ALU.mult).then_inc(weights_set, 1)
            dve.wait_ge(weights_set, 3)
            for m, (w, t) in enumerate(((up_raw, tern_a), (down_raw, tern_b))):
                below = gelT[:, m, :, :]
                dve.tensor_scalar(t, w, thr[:, m:m + 1], None, ALU.is_gt).then_inc(tern_set, 1)
                dve.tensor_scalar(below, w, thr[:, 2 + m:3 + m], None, ALU.is_lt).then_inc(tern_set, 1)
                dve.wait_ge(tern_set, 2 + 4 * m)
                dve.tensor_tensor(t, t, below, ALU.subtract).then_inc(tern_set, 1)
                dve.wait_ge(tern_set, 3 + 4 * m)
                dve.tensor_tensor(t, t, w, ALU.subtract).then_inc(tern_set, 1)
                dve.wait_ge(tern_set, 4 + 4 * m)
                dve.tensor_tensor(t, t, w, ALU.add).then_inc(prep_v, 1)
            for k, (r, n) in enumerate(((0, 0), (0, 1), (1, 0), (1, 1))):
                dve.wait_ge(prep_a, 13 + k)
                cols = slice(8 * n + r, 8 * n + r + 7, 2)
                dve.tensor_tensor(vo1_lo[:, cols, :], bank[(1 + n, (7, 0)[n])[r]][:].rearrange("p (h e) -> p h e", h=4),
                                  vo1_hi[:, cols, :].bitcast(F32), ALU.subtract).then_inc(prep_v, 1)

            all_scales(f, a["row_stats"], True)

            def ffn0(it, half, par):
                far, prv, old = it + 2, it - 1, it - 2
                npar = 1 - par
                if live(far, B):
                    normalise_all(far, par, f, "xT_pe")
                if live(old, B):
                    dve.wait_ge(f["rms"], old + 1)
                    at_least(dve, f["rrms"], old)
                    dve.tensor_scalar(rms_eps[:], rms[:, par:par + 1], RMS_EPS, None, ALU.add).then_inc(f["eps"], 1)
                    dve.wait_ge(f["eps"], old + 1)
                    at_least(dve, f["x"], old)
                    dve.reciprocal(rrms[:], rms_eps[:]).then_inc(f["rrms"], 1)
                if live(prv, B):
                    dve.wait_ge(f["gel"], prv + 1)
                    at_least(dve, f["rms"], prv - 1)
                    dve.tensor_tensor_reduce(out=gel2[:], in0=gel[:, npar, :], in1=gel[:, npar, :], scale=1.0 / F, scalar=0.0,
                                             op0=ALU.mult, op1=ALU.add, accum_out=ssq[:, npar:npar + 1]).then_inc(f["sq"], 1)
                if live(old, B):
                    dve.wait_ge(f["rrms"], old + 1)
                    dve.wait_ge(f["y_pe"], old + 1)
                    dve.scalar_tensor_tensor(out=seq_rows(old), in0=bank[6 + par][:, 0:D], scalar=rrms[:],
                                             in1=seq_rows(old), op0=ALU.mult, op1=ALU.add).then_inc(f["x"], 1)
                    stats_of(old, f)

            normalise_all(0, 0, f, "xT_pe")
            staged(dve, B, ffn0)

            all_scales(c, f["row_stats"], False)

            def attn1(it, half, par):
                nxt, far, prv = it + 1, it + 2, it - 1
                npar = 1 - par

                def shift(j):
                    s = bank[j % 2][:, 0:HB * S].rearrange("p (h s) -> p h s", h=HB)
                    m = mx[:, par, HB * j:HB * j + HB]
                    dve.wait_ge(c["s_pe"], NB * it + j + 1)
                    dve.reduce_max(m, s, AX_X).then_inc(c["max"], 1)
                    at_least(dve, c["p_pe"], NB * (it - 2) + j + 1)
                    dve.wait_ge(c["max"], NB * it + j + 1)
                    dve.tensor_tensor(sc[:, par, HB * j:HB * j + HB, :], s, m.unsqueeze(2).to_broadcast([L, HB, S]),
                                      ALU.subtract).then_inc(c["shifted"], 1)

                def low_u(j):
                    cols = slice(HB * j, HB * j + HB)
                    dve.wait_ge(c["u_hi"], NB * nxt + j + 1)
                    dve.tensor_tensor(u_lo[:, npar, cols, :].rearrange("p h s -> p (h s)"), bank[4 + j % 2][:, 0:HB * S],
                                      u_hi[:, npar, cols, :].rearrange("p h s -> p (h s)").bitcast(F32), ALU.subtract
                                      ).then_inc(c["u"], 1)

                if live(it, B):
                    shift(0)
                    shift(1)
                    shift(2)
                if live(nxt, B):
                    dve.wait_ge(c["hi"], 2 * nxt + 2)
                    dve.tensor_tensor(xcT_lo[:, npar, :], bank[6][:, 0:L + S], xcT_hi[:, npar, :].bitcast(F32),
                                      ALU.subtract).then_inc(c["lo"], 1)
                if live(it, B):
                    shift(3)
                for j in range(NB):
                    if live(it, B):
                        denominators(it, par, j, c)
                    if live(nxt, B):
                        low_u(j)
                    if live(it, B):
                        reciprocals(it, par, j, c)
                if live(far, B):
                    normalise_all(far, par, c, "xcT_pe")
                if live(prv, B):
                    dve.wait_ge(c["y_pe"], prv + 1)
                    dve.tensor_tensor(seq_rows(prv), bank[7][:, 0:D], seq_rows(prv), ALU.add).then_inc(c["x"], 1)
                    stats_of(prv, c)

            normalise_all(0, 0, c, "xcT_pe")
            staged(dve, B, attn1)

            all_scales(ro, c["row_stats"], False)

            def route(it, half, par):
                far = it + 2
                if live(far, B):
                    normalise_all(far, par, ro, "xT_pe")
                    dve.tensor_scalar(rec[:, bass.ds(far, 1), 0:D].rearrange("l o d -> l (o d)"), seq_rows(far),
                                      mean_all[:, bass.ds(far, 1)], scale_all[:, bass.ds(far, 1)],
                                      ALU.subtract, ALU.mult).then_inc(ro["rec"], 1)
                if live(it, B):
                    dve.wait_ge(ro["l_pe"], it + 1)
                    dve.tensor_tensor(logits[:, bass.ds(it, 1), :].rearrange("l o e -> l (o e)"), bank[2 + par][:, 0:E], bg_bc[:],
                                      ALU.add).then_inc(ro["logits"], 1)

            normalise_all(0, 0, ro, "xT_pe")
            dve.tensor_scalar(rec[:, 0, 0:D], xs[:, 0, :], mean_all[:, 0:1], scale_all[:, 0:1], ALU.subtract, ALU.mult
                              ).then_inc(ro["rec"], 1)
            staged(dve, B, route)

            best, total, first, at = (pick[:, n, :] for n in range(4))
            dve.wait_ge(ro["logits"], B)
            dve.reduce_max(best, logits[:], AX_X).then_inc(ro["v"], 1)
            dve.wait_ge(ro["v"], 1)
            dve.tensor_tensor(route_a[:], logits[:], best.unsqueeze(2).to_broadcast([L, B, E]), ALU.subtract
                              ).then_inc(ro["v"], 1)
            dve.wait_ge(ro["exp"], 1)
            dve.reduce_sum(total, route_b[:], AX_X).then_inc(ro["v"], 1)
            dve.tensor_scalar(route_a[:], route_a[:], 0.0, float(E), ALU.is_lt, ALU.mult).then_inc(ro["v"], 1)
            dve.wait_ge(ro["v"], 4)
            dve.tensor_tensor(route_a[:], route_a[:], experts[:], ALU.add).then_inc(ro["v"], 1)
            dve.wait_ge(ro["v"], 5)
            dve.tensor_reduce(first, route_a[:], AX_X, ALU.min).then_inc(ro["v"], 1)
            dve.wait_ge(ro["v"], 6)
            dve.tensor_tensor(onehot[:], experts[:], first.unsqueeze(2).to_broadcast([L, B, E]), ALU.is_equal
                              ).then_inc(chained, 1)
            dve.wait_ge(chained, 6)
            dve.wait_ge(ro["tables"], 11)
            dve.tensor_copy(before_bf[:], before[:]).then_inc(chained, 1)
            dve.tensor_copy(onehot_bf[:], onehot[:].rearrange("l b e -> l e b")).then_inc(ro["v"], 1)
            dve.wait_ge(chained, 7)
            dve.reciprocal(at, total).then_inc(chained, 1)
            dve.wait_ge(chained, 8)
            dve.tensor_scalar(rec[:, :, GATE:TOKEN], at.unsqueeze(2), tg[:, 3:4], None, ALU.mult).then_inc(ro["rec"], 1)
            dve.wait_ge(ro["pe"], 1)
            dve.tensor_copy(seq_count[:], bank[4][0:B, 0:E]).then_inc(ro["v"], 1)
            dve.wait_ge(ro["v"], 8)
            dve.tensor_tensor(seq_before[:], before[0:B, 0:B].unsqueeze(2).to_broadcast([B, B, E]),
                              seq_count[:].unsqueeze(1).to_broadcast([B, B, E]), ALU.mult).then_inc(ro["v"], 1)
            n_blocks, start, end, base = (blocks_of[:, n, :] for n in range(4))
            dve.wait_ge(ro["pe"], 2)
            dve.tensor_tensor(above[:], bank[6][:, 0:E].unsqueeze(2).to_broadcast([128, E, B]),
                              block_rows[:].unsqueeze(1).to_broadcast([128, E, B]), ALU.is_gt).then_inc(chained, 1)
            dve.wait_ge(chained, 9)
            dve.reduce_sum(n_blocks, above[:], AX_X).then_inc(chained, 1)
            dve.wait_ge(chained, 10)
            dve.tensor_tensor(above[:, :, 0:E], before_e[:], n_blocks.unsqueeze(1).to_broadcast([128, E, E]), ALU.mult
                              ).then_inc(chained, 1)
            dve.wait_ge(chained, 11)
            dve.reduce_sum(start, above[:, :, 0:E], AX_X).then_inc(chained, 1)
            dve.wait_ge(chained, 12)
            dve.tensor_tensor(end, start, n_blocks, ALU.add).then_inc(chained, 1)
            dve.tensor_scalar(base, start, 128.0, None, ALU.mult).then_inc(chained, 1)
            dve.wait_ge(chained, 14)
            dve.tensor_tensor(route_a[:], bank[5][:, 0:B * E].rearrange("p (e b) -> p b e", e=E),
                              base.unsqueeze(1).to_broadcast([L, B, E]), ALU.add).then_inc(chained, 1)
            dve.wait_ge(chained, 15)
            dve.tensor_tensor(route_a[:], route_a[:], onehot[:], ALU.mult).then_inc(chained, 1)
            dve.wait_ge(chained, 16)
            dve.reduce_sum(best, route_a[:], AX_X).then_inc(chained, 1)
            dve.wait_ge(chained, 17)
            dve.tensor_copy(place[:], best).then_inc(ro["place"], 1)
            dve.tensor_tensor(block_cmp[:], block_no[:].unsqueeze(2).to_broadcast([1, BLOCKS, E]),
                              end[0:1, :].unsqueeze(1).to_broadcast([1, BLOCKS, E]), ALU.is_ge).then_inc(chained, 1)
            dve.wait_ge(chained, 18)
            dve.reduce_sum(block_f[:], block_cmp[:], AX_X).then_inc(chained, 1)
            dve.wait_ge(chained, 19)
            dve.tensor_scalar(block_e[:], block_f[:], float(E - 1), None, ALU.min).then_inc(ro["blocks"], 1)

            def expert(it, use, slot):
                old = it - 2
                par = slot % 2
                oslot = (slot + 2) % 4
                if live(it, BLOCKS):
                    e = dve.value_load(block_e[0:1, bass.ds(it, 1)], min_val=0, max_val=E - 1)
                    dve.wait_ge(ex["up_pe"], it + 1)
                    at_least(dve, ex["t_pe"], it - 1)
                    dve.tensor_tensor(hid[:, par, :], bank[par][:, 0:M],
                                      b1_bc[:, bass.ds(e, 1), :].rearrange("p o m -> p (o m)"), ALU.add).then_inc(ex["hid"], 1)
                if live(old, BLOCKS):
                    e = dve.value_load(block_e[0:1, bass.ds(old, 1)], min_val=0, max_val=E - 1)
                    dve.wait_ge(ex["y_pe"], old + 1)
                    at_least(dve, ex["y"], old - 1)
                    dve.tensor_tensor(y2[:, par, :], bank[6 + par][:, 0:D],
                                      b2_bc[:, bass.ds(e, 1), :].rearrange("p o d -> p (o d)"), ALU.add).then_inc(ex["y2"], 1)
                    dve.wait_ge(x_in[oslot], (use + (slot - 2) // 4) * 16 + 16)
                    dve.wait_ge(ex["y2"], old + 1)
                    dve.scalar_tensor_tensor(out=y_out[:, oslot, :], in0=y2[:, par, :], scalar=rows_x[:, oslot, GATE - D:TOKEN - D],
                                             in1=rows_x[:, oslot, 0:D], op0=ALU.mult, op1=ALU.add).then_inc(ex["y"], 1)

            dve.wait_ge(ro["blocks"], 1)
            dve.wait_ge(late_in, 16 * 6)
            staged_slots(dve, BLOCKS, expert)


_INS = ['x', 'ctx_1024', 'fside_Bx16xSxS2_0', 'mask_Bx1xSxS2_ik1', 'g_xattn', 'g_ffn', 'L0_xattn_Wq', 'L0_xattn_bq',
        'L0_xattn_Wk', 'L0_xattn_bk', 'L0_xattn_Wv', 'L0_xattn_bv', 'L0_xattn_Wo', 'L0_xattn_bo', 'L0_ffn_w_up',
        'L0_ffn_w_down', 'L1_xattn_Wq', 'L1_xattn_Wk', 'L1_xattn_Wv', 'L1_xattn_Wo', 'L1_ffn_w_gate', 'L1_ffn_b_gate',
        'L1_ffn_W1', 'L1_ffn_b1', 'L1_ffn_W2', 'L1_ffn_b2']


def kernel(**inputs):
    import numpy as np
    import concourse.bacc as bacc
    from concourse.bass_utils import run_bass_kernel_spmd

    nc = bacc.Bacc("TRN2", target_bir_lowering=False, num_devices=1)
    arrays, args = {}, []
    for name in _INS:
        arr = np.ascontiguousarray(inputs[name])
        arrays[f"in_{name}"] = arr
        args.append(nc.dram_tensor(f"in_{name}", arr.shape, mybir.dt.from_np(arr.dtype), kind="ExternalInput").ap())
    out = nc.dram_tensor("out_x", inputs["x"].shape, F32, kind="ExternalOutput").ap()
    build(nc, *args, out)
    r = run_bass_kernel_spmd(nc, [arrays], core_ids=[0])
    return r.results[0]["out_x"]
```

```python
from contextlib import ExitStack

import concourse.bass as bass
from concourse import mybir

F32 = mybir.dt.float32
F32R = mybir.dt.float32r
BF16 = mybir.dt.bfloat16
I32 = mybir.dt.int32
ALU = mybir.AluOpType
ACT = mybir.ActivationFunctionType
AX_X = mybir.AxisListType.X

H = 16
HB = 4
NB = H // HB
RG = 4
LN_EPS = 1e-5
RMS_EPS = 1e-8
MASKED = -1.0e30


def at_least(eng, sem, value):
    if not isinstance(value, int) or value > 0:
        eng.wait_ge(sem, value)


def live(k, n):
    return not isinstance(k, int) or 0 <= k < n


def staged(eng, n, body, ahead=1):
    end = (n - ahead) // 2
    for it in range(max(-ahead, -2), 4):
        body(it, it // 2, it % 2)
    with eng.Fori(2, end) as pair:
        body(pair * 2, pair, 0)
        body(pair * 2 + 1, pair, 1)
    for it in range(end * 2, n + 2):
        body(it, it // 2, it % 2)


def staged_slots(eng, n, body):
    for it in range(-1, 4):
        body(it, it // 4, it % 4)
    turns = (n - 1) // 4
    with eng.Fori(1, turns) as turn:
        for k in range(4):
            body(turn * 4 + k, turn, k)
    for it in range(4 * turns, n + 2):
        body(it, it // 4, it % 4)


def build(nc, x, ctx_in, bias, mask, g_xattn, g_ffn, Wq0, bq0, Wk0, bk0, Wv0, bv0, Wo0, bo0, w_up, w_down,
          Wq1, Wk1, Wv1, Wo1, w_gate, b_gate, W1, b1, W2, b2, out):
    B, L, D = x.shape
    S = ctx_in.shape[1]
    HD0 = Wq0.shape[1] // H
    HD1 = Wq1.shape[1] // H
    F = w_up.shape[0]
    FC = F // 128
    assert L == 128 and D == 128 and S <= 128 and B % 2 == 0 and HD0 <= 32 and HD1 == 64
    SCALE0 = HD0 ** -0.5
    SCALE1 = HD1 ** -0.5
    C1 = H * HD1 // 128
    E, _, M = W1.shape
    MC = M // 128
    R1 = HB * HD0
    R3 = 3 * R1
    assert R1 == 32
    NT = B * L
    BLOCKS = NT // 128 + E - 1
    GATE, TOKEN, REC = 2 * D, 2 * D + 1, 2 * D + 2

    stack = ExitStack()
    with stack:
        def sb(name, shape, dt=F32):
            return stack.enter_context(nc.sbuf_tensor(name, shape, dt))

        def sem(name):
            return stack.enter_context(nc.semaphore(name))

        bank = [stack.enter_context(nc.psum_tensor(f"bank{i}", [128, 512], F32)) for i in range(8)]

        ident = sb("ident", [128, 128])
        ident_bf = sb("ident_bf", [128, 128], BF16)
        ones = sb("ones", [128, 128])
        gates = sb("gates", [128, 4])
        tg = sb("tg", [128, 4])
        wq0_raw = sb("wq0_raw", [D, H * HD0])
        wk0_raw = sb("wk0_raw", [D, H * HD0])
        wq0_st = sb("wq0_st", [D, NB, 3, HB * HD0])
        wk0_st = sb("wk0_st", [D, NB, 3, HB * HD0])
        own_head = sb("own_head", [128, HB])
        own_part = sb("own_part", [128, 3, HB])
        bq0_col = sb("bq0_col", [128, NB])
        bk0_col = sb("bk0_col", [128, NB])
        wv0 = sb("wv0", [D, H * HD0])
        bv0_row = sb("bv0_row", [1, H * HD0])
        wo0 = sb("wo0", [H * HD0, D])
        bo0_row = sb("bo0_row", [1, D])
        absum = sb("absum", [128, FC, 2])
        thr = sb("thr", [128, 4])
        w2_t = sb("w2_t", [128, E * MC * D])
        assert 4 * H * HD1 <= E * MC * D and 2 * H * S <= E * M and C1 * 128 == H * HD1
        wq1_raw = w2_t[:, 0:H * HD1]
        wk1_raw = w2_t[:, H * HD1:2 * H * HD1]
        wq1T = w2_t[:, 2 * H * HD1:3 * H * HD1].rearrange("p (c d) -> p c d", c=C1)
        wk1T = w2_t[:, 3 * H * HD1:4 * H * HD1].rearrange("p (c d) -> p c d", c=C1)
        kq1_t = sb("kq1_t", [D, H * D])
        kq1 = kq1_t[:].rearrange("p (h d) -> p h d", h=H)
        wo1 = sb("wo1", [128, C1, D])
        vo1_hi = sb("vo1_hi", [D, H, D], F32R)
        vo1_lo = sb("vo1_lo", [D, H, D], F32R)

        rec = sb("rec", [L, B, REC])
        xs = rec[:, :, D:2 * D]
        assert B >= 6 * FC + H * HD1 // D
        up_raw, down_raw, tern_a, tern_b, upT, downT = (rec[:, n * FC:(n + 1) * FC, 0:D] for n in range(6))
        wv1_raw = rec[:, 6 * FC:6 * FC + H * HD1 // D, 0:D]

        ctx_tok = sb("ctx_tok", [S, 2, D])
        mask_i = sb("mask_i", [L, 2, S], I32)
        mask_b = sb("mask_b", [L, 2, S], BF16)
        w1_t = sb("w1_t", [128, E * M])
        bias_t = w1_t[:, 0:2 * H * S].rearrange("l (p h s) -> l p h s", p=2, h=H)
        stats = sb("stats", [128, 6])
        mv = sb("mv", [128, 2, 2])
        stats_all = sb("stats_all", [128, B, 6])
        mean_all = sb("mean_all", [128, B])
        scale_all = sb("scale_all", [128, B])
        tmp_all = sb("tmp_all", [128, 6, B])
        rstd = sb("rstd", [128, 2])
        powers = sb("powers", [128, 3])
        settle = sb("settle", [128, 1])
        xn = sb("xn", [L, 2, D])
        xcT = sb("xcT", [D, 2, L + S])
        proj_t = sb("proj_t", [128, 4 * F])
        q_f32 = proj_t[0:R3, 0:NB * L].rearrange("p (j l) -> p j l", j=NB)
        k_f32 = proj_t[0:R3, NB * L:NB * (L + S)].rearrange("p (j s) -> p j s", j=NB)
        gel = proj_t[:, 0:2 * F].rearrange("p (a f) -> p a f", a=2)
        gelT = proj_t[:, 2 * F:4 * F].rearrange("p (a c l) -> p a c l", a=2, c=FC)
        xcT_hi = sb("xcT_hi", [D, 2, L + S], F32R)
        xcT_lo = sb("xcT_lo", [D, 2, L + S], F32R)
        u_hi = sb("u_hi", [D, 2, H, S], F32R)
        u_lo = sb("u_lo", [D, 2, H, S], F32R)
        k_diag = u_hi[0:R3]
        u_lo_flat = u_lo[:, 0, :, :].rearrange("p h s -> p (h s)")
        q_st = u_lo_flat[0:R3, 0:2 * NB * L].rearrange("p (a j l) -> p a j l", a=2, j=NB)
        k_st = u_lo_flat[0:R3, 2 * NB * L:2 * NB * L + NB * S].rearrange("p (j s) -> p j s", j=NB)
        b1_t = sb("b1_t", [128, E * M])
        sc = b1_t[:, 0:2 * H * S].rearrange("l (p h s) -> l p h s", p=2, h=H)
        wv1T = b1_t[:, 0:H * HD1].rearrange("p (c d) -> p c d", c=C1)
        rowsT = proj_t[:, 0:2 * RG * L].rearrange("p (a n l) -> p a n l", a=2, n=RG)
        mx = sb("mx", [L, 2, H])
        neg_max = sb("neg_max", [L, 2, H])
        WORK = 2 * H * D + H * HD0
        work = sb("work", [128, WORK])
        v0 = work[0:S, 0:2 * H * D].rearrange("s (p h d) -> s p h d", p=2, h=H)
        w_vo = work[0:S, 0:2 * H * D].rearrange("s (p h d) -> s p h d", p=2, h=H)
        gel2 = work[:, 0:F]
        hid = work[:, 0:2 * M].rearrange("l (p m) -> l p m", p=2)
        hidT = work[:, 2 * M:4 * M].rearrange("p (a c l) -> p a c l", a=2, c=MC)
        at0 = 4 * M
        at1, at2 = at0 + 4 * D, at0 + 4 * REC
        rows_n = work[:, at0:at1].rearrange("l (n c) -> l n c", n=4)
        rows_x = work[:, at1:at2].rearrange("l (n c) -> l n c", n=4)
        y_out = work[:, at2:at2 + 4 * D].rearrange("l (n d) -> l n d", n=4)
        assert at2 + 4 * D <= WORK and 2 * H * D + HD0 * H <= WORK
        prT = sb("prT", [S, H, L])
        den = sb("den", [L, 2, H])
        rden = sb("rden", [L, 2, H])
        o0T = sb("o0T", [H * HD0, L])
        ssq = sb("ssq", [L, 2])
        rms = sb("rms", [L, 2])
        rms_eps = sb("rms_eps", [L, 1])
        rrms = sb("rrms", [L, 1])

        w_gate_t = sb("w_gate_t", [D, E])
        bg_bc = sb("bg_bc", [128, E])
        b1_bc = b1_t[:].rearrange("p (e m) -> p e m", e=E)
        b2_bc = sb("b2_bc", [128, E, D])
        blank = sb("blank", [128, REC])
        experts = sb("experts", [128, B, E])
        before = sb("before", [128, 128])
        before_bf = sb("before_bf", [128, 128], BF16)
        ones_bf = sb("ones_bf", [128, 128], BF16)
        before_e = sb("before_e", [128, E, E])
        block_rows = sb("block_rows", [128, B])
        block_no = sb("block_no", [1, BLOCKS])
        logits, route_a, route_b, onehot = (
            kq1_t[:, n * B * E:(n + 1) * B * E].rearrange("l (b e) -> l b e", e=E) for n in range(4))
        above = kq1_t[:, 4 * B * E:5 * B * E].rearrange("p (e b) -> p e b", e=E)
        rowT = kq1_t[:, 5 * B * E:5 * B * E + 2 * D].rearrange("p (a l) -> p a l", a=2)
        y2 = kq1_t[:, 5 * B * E + 2 * D:5 * B * E + 4 * D].rearrange("p (a d) -> p a d", a=2)
        assert 5 * B * E + 4 * D <= H * D
        onehot_bf = sb("onehot_bf", [L, E, B], BF16)
        pick = sb("pick", [L, 4, B])
        seq_count = sb("seq_count", [B, E], BF16)
        seq_before = sb("seq_before", [B, B, E], BF16)
        blocks_of = sb("blocks_of", [128, 4, E])
        block_cmp = sb("block_cmp", [1, BLOCKS, E])
        block_f = sb("block_f", [1, BLOCKS])
        block_e = sb("block_e", [1, BLOCKS], I32)
        place = sb("place", [L, B], I32)
        idle = sb("idle", [128, 1])
        sorted_rows = nc.dram_tensor("sorted_rows", [BLOCKS * 128, REC], F32, kind="Internal").ap()

        wqk0_in = sem("wqk0_in")
        wvo0_in = sem("wvo0_in")
        wqk1_in = sem("wqk1_in")
        wvo1_in = sem("wvo1_in")
        w_in = sem("w_in")
        g_in = sem("g_in")
        x0_in = [sem(f"x0_in{p}") for p in range(2)]
        ctx0_in = [sem(f"ctx0_in{p}") for p in range(2)]
        mask_in = [sem(f"mask_in{p}") for p in range(2)]
        bias_in = [[sem(f"bias_in{p}{j}") for j in range(NB)] for p in range(2)]
        ctx1_in = [sem(f"ctx1_in{p}") for p in range(2)]
        late_in = sem("late_in")
        blanked = sem("blanked")
        ro = {n: sem("r_" + n) for n in (
            "rec", "xT_pe", "xT", "l_pe", "logits", "v", "exp", "pe", "place", "blocks", "placed", "tables",
            "var", "pow", "scale")}
        ex = {n: sem("m_" + n) for n in ("xT_pe", "xT", "up_pe", "hid", "t_pe", "hidT", "y_pe", "y2", "y", "idle")}
        x_in = [sem(f"x_in{n}") for n in range(4)]
        rows_in = [sem(f"rows_in{n}") for n in range(4)]
        rows_out = [sem(f"rows_out{n}") for n in range(4)]
        padded = sem("padded")
        chained = sem("chained")
        tern_set = sem("tern_set")
        consts_set = sem("consts_set")
        powers_set = sem("powers_set")
        tanh_set = sem("tanh_set")
        prep_v = sem("prep_v")
        prep_pe = sem("prep_pe")
        prep_a = sem("prep_a")
        absum_set = sem("absum_set")
        wo1_set = sem("wo1_set")
        weights_set = sem("weights_set")
        a = {n: sem("a_" + n) for n in (
            "ln", "xcT_pe", "xcT", "q_pe", "k_pe", "v_pe", "k_f32", "k_hi", "k_lo", "k_diag", "q_f32",
            "q_hi", "q_lo", "v", "s_pe", "biased", "max", "neg_max", "shifted", "exp",
            "mask", "stats", "rstd", "den", "rden", "normed", "t_pe", "prT", "pv_pe", "oT", "y_pe", "x", "row_stats")}
        f = {n: sem("f_" + n) for n in (
            "ln", "xT_pe", "xT", "up_pe", "gel", "sq", "rms", "eps", "rrms", "t_pe", "gelT", "y_pe", "x", "row_stats",
            "var", "pow", "scale")}
        c = {n: sem("c_" + n) for n in (
            "ln", "xcT_pe", "hi", "lo", "u_pe", "u_hi", "u", "w_pe", "w", "s_pe", "max", "shifted", "exp", "den",
            "rden", "normed", "p_pe", "prT", "y_pe", "x", "row_stats", "var", "pow", "scale")}

        v0_diag = [work[0:S, p * H * D:p * H * D + H * (D + HD0)].rearrange("s (h c) -> s h c", c=D + HD0)[:, :, 0:HD0]
                   for p in range(2)]

        PART_STEP = B - 2
        PARTS = ((0, B - 6), (B - 6, B))

        def bcast(row, n):
            return row.rearrange("(o d) -> o d", o=1).to_broadcast([n, row.shape[0]])

        block = stack.enter_context(nc.Block())

        @block.sync
        def _(sp):
            def load_x(it, par):
                at_least(sp, a["ln"], it - 1)
                sp.dma_start(xs[:, bass.ds(it, 1), :].rearrange("l o d -> l (o d)"),
                             x[bass.ds(it, 1), :, :].rearrange("o l d -> (o l) d")).then_inc(x0_in[par], 16)

            def load_ctx0(it, par):
                at_least(sp, a["xcT_pe"], it - 1)
                sp.dma_start(ctx_tok[:, par, :], ctx_in[bass.ds(it, 1), :, :].rearrange("o s d -> (o s) d")
                             ).then_inc(ctx0_in[par], 16)

            def load_seq(it, par):
                if live(it + 1, B) and not (isinstance(it, int) and it == 0):
                    load_ctx0(it + 1, 1 - par)
                at_least(sp, a["mask"], it - 1)
                sp.dma_start(mask_i[:, par, :], mask[bass.ds(it, 1), 0, :, :].rearrange("o l s -> (o l) s")).then_inc(mask_in[par], 16)
                for j in range(NB):
                    at_least(sp, a["biased"], NB * (it - 2) + j + 1)
                    sp.dma_start(bias_t[:, par, HB * j:HB * j + HB, :],
                                 bias[bass.ds(it, 1), HB * j:HB * j + HB, :, :].rearrange("o h l s -> l (o h) s")
                                 ).then_inc(bias_in[par][j], 16)
                if live(it + 2, B):
                    load_x(it + 2, par)

            load_x(0, 0)
            load_ctx0(0, 0)
            sp.dma_start(wq0_raw[:], Wq0).then_inc(wqk0_in, 16)
            sp.dma_start(wk0_raw[:], Wk0).then_inc(wqk0_in, 16)
            load_x(1, 1)
            load_ctx0(1, 1)
            sp.dma_start(wv0[:], Wv0).then_inc(wvo0_in, 16)
            sp.dma_start(wo0[:], Wo0).then_inc(wvo0_in, 16)
            sp.dma_start(bv0_row[:], bv0.rearrange("(o d) -> o d", o=1)).then_inc(wvo0_in, 16)
            sp.dma_start(bo0_row[:], bo0.rearrange("(o d) -> o d", o=1)).then_inc(wvo0_in, 16)
            sp.dma_start(wq1_raw, Wq1).then_inc(wqk1_in, 16)
            sp.dma_start(wk1_raw, Wk1).then_inc(wqk1_in, 16)
            sp.dma_start(up_raw, w_up.rearrange("(c p) d -> p c d", p=128)).then_inc(w_in, 16)
            sp.dma_start(down_raw, w_down.rearrange("d (c l) -> d c l", c=FC)).then_inc(w_in, 16)
            sp.dma_start(wv1_raw, Wv1.rearrange("d (c l) -> d c l", l=128)).then_inc(wvo1_in, 16)
            sp.dma_start(wo1[:], Wo1.rearrange("(c p) n -> p c n", p=128)).then_inc(wvo1_in, 16)
            load_seq(0, 0)
            load_seq(1, 1)
            sp.wait_ge(ro["tables"], 2)
            sp.dma_start(sorted_rows.rearrange("(j p) c -> p j c", p=128),
                         blank[:].unsqueeze(1).to_broadcast([128, BLOCKS, REC])).then_inc(blanked, 16)
            with sp.Fori(1, B // 2 - 1) as pair:
                load_seq(pair * 2, 0)
                load_seq(pair * 2 + 1, 1)
            load_seq(B - 2, 0)
            load_seq(B - 1, 1)
            sp.dma_start(w_gate_t[:], w_gate).then_inc(late_in, 16)
            sp.dma_start(bg_bc[:], bcast(b_gate, 128)).then_inc(late_in, 16)
            sp.dma_start(b2_bc[:].rearrange("p e d -> p (e d)"), bcast(b2.rearrange("e d -> (e d)"), 128)).then_inc(late_in, 16)
            sp.wait_ge(a["biased"], NB * B)
            sp.dma_start(w1_t[:].rearrange("d (e m) -> d e m", e=E), W1.rearrange("e d m -> d e m")).then_inc(late_in, 16)
            sp.wait_ge(prep_pe, 2)
            sp.dma_start(w2_t[:].rearrange("p (e c d) -> p e c d", e=E, c=MC), W2.rearrange("e (c p) d -> p e c d", p=128)
                         ).then_inc(late_in, 16)

            def load_ctx(it, par):
                at_least(sp, c["xcT_pe"], it - 1)
                sp.dma_start(ctx_tok[:, par, :], ctx_in[bass.ds(it, 1), :, :].rearrange("o s d -> (o s) d")).then_inc(ctx1_in[par], 16)

            sp.wait_ge(a["xcT_pe"], B)
            load_ctx(0, 0)
            load_ctx(1, 1)
            with sp.Fori(1, B // 2) as pair:
                load_ctx(pair * 2, 0)
                load_ctx(pair * 2 + 1, 1)
            sp.wait_ge(c["p_pe"], NB * B)
            sp.dma_start(b1_t[:], bcast(b1.rearrange("e m -> (e m)"), 128)).then_inc(late_in, 16)

            sorted_blocks = sorted_rows.rearrange("(j p) c -> j p c", p=128)

            def load_rows(it, use, slot):
                if live(it, BLOCKS):
                    at_least(sp, ex["xT_pe"], it - 3)
                    sp.wait_ge(ro["placed"], 16 * B)
                    sp.dma_start(rows_n[:, slot, :], sorted_blocks[bass.ds(it, 1), :, 0:D].rearrange("o p c -> (o p) c")
                                 ).then_inc(rows_in[slot], 16)
                late, late_slot = it - 2, (slot + 2) % 4
                if live(late, BLOCKS):
                    at_least(sp, rows_out[late_slot], (use + (slot - 2) // 4) * 16)
                    sp.wait_ge(ro["placed"], 16 * B)
                    sp.dma_start(rows_x[:, late_slot, :], sorted_blocks[bass.ds(late, 1), :, D:REC].rearrange("o p c -> (o p) c")
                                 ).then_inc(x_in[late_slot], 16)

            for it in range(8):
                load_rows(it, it // 4, it % 4)
            with sp.Fori(2, BLOCKS // 4) as turn:
                for k in range(4):
                    load_rows(turn * 4 + k, turn, k)
            for it in range(BLOCKS // 4 * 4, BLOCKS + 2):
                load_rows(it, it // 4, it % 4)

        @block.gpsimd
        def _(pool):
            pool.memset(ones[:], 1.0).then_inc(consts_set, 1)
            pool.memset(ident[:], 1.0).then_inc(consts_set, 1)
            pool.memset(ident_bf[:], 1.0).then_inc(consts_set, 1)
            pool.wait_ge(consts_set, 3)
            pool.affine_select(out=ident[:], in_=ident[:], compare_op=ALU.is_equal, fill=0.0, base=0,
                               pattern=[[-1, 128]], channel_multiplier=1).then_inc(consts_set, 1)
            pool.affine_select(out=ident_bf[:], in_=ident_bf[:], compare_op=ALU.is_equal, fill=0.0, base=0,
                               pattern=[[-1, 128]], channel_multiplier=1).then_inc(consts_set, 1)
            for n, power in enumerate((0.5, -0.5, LN_EPS)):
                pool.memset(powers[:, n:n + 1], power).then_inc(powers_set, 1)
            pool.wait_ge(powers_set, 3)
            pool.memset(work[0:S, :], 0.0).then_inc(consts_set, 1)
            pool.memset(blank[:, 0:TOKEN], 0.0).then_inc(ro["tables"], 1)
            pool.memset(blank[:, TOKEN:REC].bitcast(I32), 1 << 30).then_inc(ro["tables"], 1)
            pool.memset(before[:], 1.0).then_inc(ro["tables"], 1)
            pool.memset(before_e[:], 1.0).then_inc(ro["tables"], 1)
            pool.memset(ones_bf[:], 1.0).then_inc(ro["tables"], 1)
            pool.wait_ge(ro["tables"], 5)
            pool.affine_select(out=before[:], in_=before[:], compare_op=ALU.is_gt, fill=0.0, base=0,
                               pattern=[[1, 128]], channel_multiplier=-1).then_inc(ro["tables"], 1)
            pool.affine_select(out=before_e[:], in_=before_e[:], compare_op=ALU.is_gt, fill=0.0, base=0,
                               pattern=[[1, E], [-1, E]], channel_multiplier=0).then_inc(ro["tables"], 1)
            pool.iota(experts[:], pattern=[[0, B], [1, E]], base=0, channel_multiplier=0,
                      allow_small_or_imprecise_dtypes=True).then_inc(ro["tables"], 1)
            pool.iota(block_rows[:], pattern=[[128, B]], base=0, channel_multiplier=0,
                      allow_small_or_imprecise_dtypes=True).then_inc(ro["tables"], 1)
            pool.iota(block_no[:], pattern=[[1, BLOCKS]], base=0, channel_multiplier=0,
                      allow_small_or_imprecise_dtypes=True).then_inc(ro["tables"], 1)
            pool.iota(rec[:, :, TOKEN:REC].bitcast(I32), pattern=[[128, B]], base=0, channel_multiplier=1
                      ).then_inc(ro["tables"], 1)

            def inv_std(it, par, s):
                pool.wait_ge(s["stats"], 2 * it + 2)
                at_least(pool, s["ln"], it - 1)
                pool.tensor_tensor(rstd[:, par:par + 1], mv[:, par, 1:2], powers[:, 2:3], ALU.add).then_inc(s["rstd"], 1)
                pool.wait_ge(s["rstd"], 2 * it + 1)
                pool.tensor_tensor(rstd[:, par:par + 1], rstd[:, par:par + 1], powers[:, 1:2], ALU.pow
                                   ).then_inc(s["rstd"], 1)

            def powers_of_var(s, part, with_root):
                lo, hi = PARTS[part]
                pool.wait_ge(s["var"], 7 * part + 7)
                pool.tensor_tensor(tmp_all[:, 4, lo:hi], tmp_all[:, 3, lo:hi], powers[:, 1:2].to_broadcast([128, hi - lo]),
                                   ALU.pow).then_inc(s["pow"], 1)
                if with_root:
                    pool.tensor_tensor(tmp_all[:, 5, lo:hi], tmp_all[:, 2, lo:hi], powers[:, 0:1].to_broadcast([128, hi - lo]),
                                       ALU.pow).then_inc(s["pow"], 1)

            def attn0(it, half, par):
                nxt, fur = it + 1, it + 3

                def alone_after_last():
                    if live(it - 1, B):
                        pool.wait_ge(a["normed"], NB * it)
                    else:
                        pool.wait_ge(a["rstd"], 2 * it + 6)

                def shift(j):
                    s = sc[:, par, HB * j:HB * j + HB, :]
                    pool.wait_ge(a["max"], NB * it + j + 1)
                    pool.tensor_tensor(s, s, mx[:, par, HB * j:HB * j + HB].unsqueeze(2).to_broadcast([L, HB, S]),
                                       ALU.subtract).then_inc(a["shifted"], 1)

                if live(nxt, B):
                    k_low = k_st[R1:2 * R1]
                    pool.wait_ge(a["k_hi"], nxt + 1)
                    alone_after_last()
                    pool.tensor_tensor(k_low, k_f32[R1:2 * R1], k_low.bitcast(F32), ALU.subtract).then_inc(a["k_lo"], 1)
                    pool.wait_ge(a["k_lo"], nxt + 1)
                if live(it, B):
                    shift(1)
                if live(fur, B):
                    inv_std(fur, 1 - par, a)
                if live(it, B):
                    shift(2)
                if live(nxt, B):
                    q_low = q_st[2 * R1:R3, 1 - par]
                    pool.wait_ge(a["q_hi"], nxt + 1)
                    pool.wait_ge(a["k_lo"], nxt + 1)
                    if live(it, B):
                        pool.wait_ge(a["shifted"], 2 * it + 2)
                    elif live(fur, B):
                        pool.wait_ge(a["rstd"], 2 * fur + 2)
                    pool.tensor_tensor(q_low, q_f32[2 * R1:R3], q_low.bitcast(F32), ALU.subtract).then_inc(a["q_lo"], 1)
                    pool.wait_ge(a["q_lo"], nxt + 1)
                if live(it, B):
                    for j in range(NB):
                        scale_probs(it, par, j, a)
                if isinstance(it, int) and it == PART_STEP + 1:
                    powers_of_var(f, 0, True)

            def scale_probs(it, par, j, s):
                p = sc[:, par, HB * j:HB * j + HB, :]
                pool.wait_ge(s["rden"], NB * it + j + 1)
                pool.tensor_tensor(p, p, rden[:, par, HB * j:HB * j + HB].unsqueeze(2).to_broadcast([L, HB, S]),
                                   ALU.mult).then_inc(s["normed"], 1)

            inv_std(0, 0, a)
            staged(pool, B, attn0, ahead=3)

            powers_of_var(f, 1, True)

            def ffn_rms(it, half, par):
                if live(it - 1, B):
                    pool.wait_ge(f["sq"], it)
                    at_least(pool, f["eps"], it - 2)
                    pool.tensor_tensor(rms[:, 1 - par:2 - par], ssq[:, 1 - par:2 - par], powers[:, 0:1], ALU.pow
                                       ).then_inc(f["rms"], 1)
                if isinstance(it, int) and it == PART_STEP + 1:
                    powers_of_var(c, 0, False)

            staged(pool, B, ffn_rms)
            powers_of_var(c, 1, False)

            def attn1(it, half, par):
                if live(it, B):
                    for j in range(NB):
                        scale_probs(it, par, j, c)
                if isinstance(it, int) and it == PART_STEP + 1:
                    powers_of_var(ro, 0, False)

            staged(pool, B, attn1)
            powers_of_var(ro, 1, False)

            pool.wait_ge(ro["place"], 1)
            pool.wait_ge(ro["rec"], B + 1)
            pool.wait_ge(blanked, 16)
            for b in range(B):
                pool.indirect_dma_start(out=sorted_rows, out_offset=bass.IndirectOffsetOnAxis(ap=place[:, b:b + 1], axis=0),
                                        in_=rec[:, b, :], in_offset=None, bounds_check=BLOCKS * 128 - 1, oob_is_err=False
                                        ).then_inc(ro["placed"], 16)

            out_rows = out.rearrange("b l d -> (b l) d")

            def store_rows(it, use, slot):
                old = it - 2
                oslot = (slot + 2) % 4
                if live(old, BLOCKS):
                    pool.wait_ge(ex["y"], old + 1)
                    at_least(pool, ex["idle"], old)
                    pool.tensor_tensor(idle[:], powers[:, 0:1], powers[:, 0:1], ALU.add).then_inc(ex["idle"], 1)
                    pool.indirect_dma_start(out=out_rows,
                                            out_offset=bass.IndirectOffsetOnAxis(
                                                ap=rows_x[:, oslot, TOKEN - D:REC - D].bitcast(I32), axis=0),
                                            in_=y_out[:, oslot, :], in_offset=None, bounds_check=NT - 1, oob_is_err=False
                                            ).then_inc(rows_out[oslot], 16)

            staged_slots(pool, BLOCKS, store_rows)
            for n in range(4):
                pool.wait_ge(rows_out[n], 16 * ((BLOCKS - n + 3) // 4))

        @block.tensor
        def _(pe):
            pe.wait_ge(consts_set, 6)
            pe.wait_ge(wqk1_in, 32)
            wq1_chunks, wk1_chunks = (w.rearrange("d (c l) -> d c l", l=128) for w in (wq1_raw, wk1_raw))
            for w, b_ in ((wq1_chunks, 1), (wk1_chunks, 3)):
                for n in range(C1):
                    mm = pe.transpose(bank[b_ + n // 4][:, n % 4 * 128:n % 4 * 128 + 128], w[:, n, :], ident[:])
            mm.then_inc(prep_pe, 1)
            pe.wait_ge(prep_a, 4)
            for n in range(C1):
                for r in range(2):
                    mm = pe.matmul(bank[3 + 2 * r + n // 4][:, n % 4 * 128:n % 4 * 128 + 128],
                                   wk1T[64 * r:64 * r + 64, n, :], wq1T[64 * r:64 * r + 64, n, :],
                                   start=(n % 4 == 0), stop=(n % 4 == 3), skip_group_check=True)
            mm.then_inc(prep_pe, 1)
            pe.wait_ge(wvo1_in, 32)
            for n in range(C1):
                mm = pe.transpose(bank[1 + n // 4][:, n % 4 * 128:n % 4 * 128 + 128], wv1_raw[:, n, :], ident[:])
            mm.then_inc(prep_pe, 1)
            pe.wait_ge(absum_set, 2)
            for n in range(FC):
                mm = pe.matmul(bank[0][:, 0:2], ones[:], absum[:, n, :], start=(n == 0), stop=(n == FC - 1))
            mm.then_inc(prep_pe, 1)
            pe.wait_ge(prep_a, 10)
            pe.wait_ge(weights_set, 3)
            pe.wait_ge(wo1_set, 1)
            for n in range(C1):
                for r in range(2):
                    mm = pe.matmul(bank[(1 + n // 4, (7, 0)[n // 4])[r]][:, n % 4 * 128:n % 4 * 128 + 128],
                                   wv1T[64 * r:64 * r + 64, n, :], wo1[64 * r:64 * r + 64, n, :],
                                   start=(n % 4 == 0), stop=(n % 4 == 3), skip_group_check=True)
            mm.then_inc(prep_pe, 1)
            pe.wait_ge(prep_v, 2)
            pe.wait_ge(prep_a, 10)
            for n in range(FC):
                pe.transpose(bank[3][:, n * 128:n * 128 + 128], tern_a[:, n, :], ident[:])
            for n in range(FC):
                mm = pe.transpose(bank[4][:, n * 128:n * 128 + 128], tern_b[:, n, :], ident[:])
            mm.then_inc(prep_pe, 1)
            pe.wait_ge(prep_a, 16)
            pe.wait_ge(prep_v, 6)

            def attn0(it, half, par):
                nxt, far, prv, old = it + 1, it + 2, it - 1, it - 2
                npar = 1 - par
                xT = xcT[:, npar, 0:L]
                cT = xcT[:, npar, L:L + S]

                def transpose_probs(j):
                    if live(prv, B):
                        pe.wait_ge(a["normed"], NB * prv + j + 1)
                        at_least(pe, a["prT"], NB * prv + j - 1)
                        for n in range(HB):
                            mm = pe.transpose(bank[4 + j % 2][0:S, n * L:n * L + L], sc[:, npar, HB * j + n, :], ident[:])
                        mm.then_inc(a["t_pe"], 1)

                def scores(j):
                    if live(it, B):
                        b_ = bank[j % 2][:, 0:HB * S].rearrange("p (h s) -> p h s", h=HB)
                        at_least(pe, a["biased"], NB * it + j - 1)
                        if j == 0:
                            pe.wait_ge(a["mask"], it + 1)
                            pe.wait_ge(a["q_lo"], it + 1)
                            pe.wait_ge(a["k_diag"], HB * it + HB)
                        pe.matmul(b_, ident_bf[:], mask_b[:, par, :].unsqueeze(1).to_broadcast([L, HB, S]),
                                  start=True, stop=False)
                        pe.matmul(b_, q_st[:, par, j, :], k_diag[:, par, HB * j:HB * j + HB, :], start=False, stop=True
                                  ).then_inc(a["s_pe"], 1)

                scores(0)
                transpose_probs(0)
                if live(nxt, B):
                    at_least(pe, a["v"], nxt)
                    for j in range(NB):
                        mm = pe.matmul(bank[3][0:R3, j * L:j * L + L], wq0_st[:, j, :, :].rearrange("p t r -> p (t r)"), xT,
                                       start=(j == 0), stop=(j == NB - 1), skip_group_check=True)
                    mm.then_inc(a["q_pe"], 1)
                scores(1)
                transpose_probs(1)
                scores(2)
                transpose_probs(2)
                scores(3)
                transpose_probs(3)
                if live(far, B):
                    pe.wait_ge(a["ln"], far + 1)
                    pe.wait_ge(ctx0_in[par], half * 16 + 32)
                    at_least(pe, a["k_f32"], far)
                    pe.transpose(bank[2][:, 0:L], xn[:, par, :], ident[:])
                    pe.transpose(bank[2][:, L:L + S], ctx_tok[:, par, :], ident[0:S, 0:S]).then_inc(a["xcT_pe"], 1)
                if live(nxt, B):
                    pe.wait_ge(a["q_f32"], nxt + 1)
                    pe.matmul(bank[3][0:S, 0:H * HD0], cT, wv0[:], start=True, stop=False)
                    pe.matmul(bank[3][0:S, 0:H * HD0], ones[0:1, 0:S], bv0_row[:], start=False, stop=True
                              ).then_inc(a["v_pe"], 1)
                if live(old, B):
                    pe.wait_ge(a["oT"], old + 1)
                    at_least(pe, a["x"], old)
                    pe.matmul(bank[7][:, 0:D], o0T[:], wo0[:], start=True, stop=False)
                    pe.matmul(bank[7][:, 0:D], ones[0:1, 0:L], bo0_row[:], start=False, stop=True).then_inc(a["y_pe"], 1)
                if live(far, B):
                    pe.wait_ge(a["xcT"], far + 1)
                    for j in range(NB):
                        mm = pe.matmul(bank[2][0:R3, j * S:j * S + S], wk0_st[:, j, :, :].rearrange("p t r -> p (t r)"),
                                       xcT[:, par, L:L + S], start=(j == 0), stop=(j == NB - 1), skip_group_check=True)
                    mm.then_inc(a["k_pe"], 1)
                if live(prv, B):
                    pe.wait_ge(a["prT"], NB * prv + NB)
                    pe.wait_ge(a["v"], prv + 1)
                    at_least(pe, a["oT"], prv)
                    for h in range(H):
                        mm = pe.matmul(bank[6][:, 0:L], v0[:, npar, h, :], prT[:, h, :], start=(h == 0), stop=(h == H - 1))
                    mm.then_inc(a["pv_pe"], 1)

            pe.wait_ge(wvo0_in, 64)
            pe.wait_ge(weights_set, 1)
            staged(pe, B, attn0, ahead=3)

            pe.wait_ge(a["x"], B)

            def ffn0(it, half, par):
                nxt, prv, old = it + 1, it - 1, it - 2
                npar = 1 - par
                if live(it, B):
                    pe.wait_ge(f["xT"], it + 1)
                    at_least(pe, f["gel"], it - 1)
                    pe.matmul(bank[par][:, 0:F].rearrange("l (c f) -> l c f", c=FC), xcT[:, par, 0:L], upT, start=True, stop=True).then_inc(f["up_pe"], 1)
                if live(nxt, B):
                    pe.wait_ge(f["ln"], nxt + 1)
                    at_least(pe, f["xT"], nxt - 1)
                    pe.transpose(bank[4 + npar][:, 0:L], xn[:, npar, :], ident[:]).then_inc(f["xT_pe"], 1)
                if live(old, B):
                    pe.wait_ge(f["gelT"], old + 1)
                    at_least(pe, f["x"], old - 1)
                    for n in range(FC):
                        mm = pe.matmul(bank[6 + par][:, 0:D], gelT[:, par, n, :], downT[:, n, :],
                                       start=(n == 0), stop=(n == FC - 1))
                    mm.then_inc(f["y_pe"], 1)
                if live(prv, B):
                    pe.wait_ge(f["gel"], prv + 1)
                    at_least(pe, f["gelT"], prv - 1)
                    for n in range(FC):
                        mm = pe.transpose(bank[2 + npar][:, n * 128:n * 128 + 128],
                                          gel[:, npar, n * 128:n * 128 + 128], ident[:])
                    mm.then_inc(f["t_pe"], 1)

            staged(pe, B, ffn0)

            def attn1(it, half, par):
                nxt, far, prv = it + 1, it + 2, it - 1
                npar = 1 - par

                def transpose_probs(j):
                    pe.wait_ge(c["normed"], NB * prv + j + 1)
                    at_least(pe, c["prT"], NB * prv + j - 1)
                    for n in range(HB):
                        mm = pe.transpose(bank[2 + j % 2][0:S, n * L:n * L + L], sc[:, npar, HB * j + n, :], ident[:])
                    mm.then_inc(c["p_pe"], 1)

                def scores(j):
                    pe.wait_ge(c["u"], NB * it + j + 1)
                    at_least(pe, c["shifted"], NB * it + j - 1)
                    hi, lo = xcT_hi[:, par, 0:L], xcT_lo[:, par, 0:L]
                    uh = u_hi[:, par, HB * j:HB * j + HB, :].rearrange("p h s -> p (h s)")
                    ul = u_lo[:, par, HB * j:HB * j + HB, :].rearrange("p h s -> p (h s)")
                    b_ = bank[j % 2][:, 0:HB * S]
                    pe.matmul(b_, hi, uh, start=True, stop=False)
                    pe.matmul(b_, hi, ul, start=False, stop=False)
                    pe.matmul(b_, lo, uh, start=False, stop=True).then_inc(c["s_pe"], 1)

                def project_u(j):
                    at_least(pe, c["u"], NB * nxt + j)
                    for n in range(HB):
                        mm = pe.matmul(bank[4][:, n * S:n * S + S], kq1[:, HB * j + n, :], xcT[:, npar, L:L + S],
                                       start=(n == 0), stop=(n == HB - 1), skip_group_check=True)
                    mm.then_inc(c["u_pe"], 1)

                def project_w(j):
                    at_least(pe, c["w"], NB * it + j)
                    hi, lo = xcT_hi[:, par, L:L + S], xcT_lo[:, par, L:L + S]
                    vh = vo1_hi[:, HB * j:HB * j + HB, :].rearrange("p h n -> p (h n)")
                    vl = vo1_lo[:, HB * j:HB * j + HB, :].rearrange("p h n -> p (h n)")
                    b_ = bank[5][0:S, :]
                    pe.matmul(b_, hi, vh, start=True, stop=False)
                    pe.matmul(b_, hi, vl, start=False, stop=False)
                    pe.matmul(b_, lo, vh, start=False, stop=True).then_inc(c["w_pe"], 1)

                if live(nxt, B):
                    pe.wait_ge(c["hi"], 2 * nxt + 2)
                    pe.wait_ge(c["lo"], nxt + 1)
                for j in range(NB):
                    if live(it, B):
                        scores(j)
                    if live(prv, B):
                        transpose_probs(j)
                    if live(nxt, B):
                        project_u(j)
                    if live(it, B):
                        project_w(j)
                if live(far, B):
                    pe.wait_ge(c["ln"], far + 1)
                    pe.wait_ge(ctx1_in[par], half * 16 + 32)
                    at_least(pe, c["hi"], 2 * far)
                    at_least(pe, c["lo"], far)
                    pe.transpose(bank[6][:, 0:L], xn[:, par, :], ident[:])
                    pe.transpose(bank[6][:, L:L + S], ctx_tok[:, par, :], ident[0:S, 0:S]).then_inc(c["xcT_pe"], 1)
                if live(prv, B):
                    pe.wait_ge(c["prT"], NB * prv + NB)
                    pe.wait_ge(c["w"], NB * prv + NB)
                    at_least(pe, c["x"], prv)
                    for h in range(H):
                        mm = pe.matmul(bank[7][:, 0:D], prT[:, h, :], w_vo[:, npar, h, :], start=(h == 0), stop=(h == H - 1))
                    mm.then_inc(c["y_pe"], 1)

            pe.wait_ge(f["x"], B)
            staged(pe, B, attn1, ahead=2)

            pe.wait_ge(late_in, 16 * 6)
            for g in range(B // RG + 1):
                if live(g, B // RG):
                    pe.wait_ge(ro["rec"], RG * g + RG)
                    at_least(pe, ro["xT"], g - 1)
                    for n in range(RG):
                        mm = pe.transpose(bank[g % 2][:, n * L:n * L + L], rec[:, RG * g + n, 0:D], ident[:])
                    mm.then_inc(ro["xT_pe"], 1)
                if g:
                    pe.wait_ge(ro["xT"], g)
                    at_least(pe, ro["logits"], g - 2)
                    for n in range(RG):
                        mm = pe.matmul(bank[3 - g % 2][:, n * E:n * E + E], rowsT[:, 1 - g % 2, n, :], w_gate_t[:],
                                       start=(n == 0), stop=(n == RG - 1), skip_group_check=True)
                    mm.then_inc(ro["l_pe"], 1)
            pe.wait_ge(ro["v"], 7)
            for e in range(E):
                mm = pe.matmul(bank[4][0:B, e:e + 1], onehot_bf[:, e, :], ones_bf[:, 0:1], start=(e == 0), stop=(e == E - 1),
                               skip_group_check=True)
            mm.then_inc(ro["pe"], 1)
            pe.wait_ge(ro["v"], 9)
            pe.matmul(bank[5][:, 0:B * E].rearrange("p (e b) -> p e b", e=E), before_bf[:], onehot_bf[:], start=True, stop=False)
            pe.matmul(bank[5][:, 0:B * E].rearrange("p (e b) -> p b e", e=E), ones_bf[0:B, :], seq_before[:], start=False, stop=True)
            pe.matmul(bank[6][:, 0:E], ones_bf[0:B, :], seq_count[:], start=True, stop=True).then_inc(ro["pe"], 1)

            def expert(it, use, slot):
                nxt, prv, old = it + 1, it - 1, it - 2
                par = slot % 2
                npar = 1 - par
                nslot = (slot + 1) % 4
                if live(it, BLOCKS):
                    e = pe.value_load(block_e[0:1, bass.ds(it, 1)], min_val=0, max_val=E - 1)
                    pe.wait_ge(ex["xT"], it + 1)
                    at_least(pe, ex["hid"], it - 1)
                    pe.matmul(bank[par][:, 0:M], rowT[:, par, :], w1_t[:, bass.ds(e * M, M)], start=True, stop=True
                              ).then_inc(ex["up_pe"], 1)
                if live(nxt, BLOCKS):
                    pe.wait_ge(rows_in[nslot], (use + (slot + 1) // 4) * 16 + 16)
                    at_least(pe, ex["xT"], nxt - 1)
                    pe.transpose(bank[4 + npar][:, 0:128], rows_n[:, nslot, :], ident[:]).then_inc(ex["xT_pe"], 1)
                if live(old, BLOCKS):
                    e = pe.value_load(block_e[0:1, bass.ds(old, 1)], min_val=0, max_val=E - 1)
                    pe.wait_ge(ex["hidT"], old + 1)
                    at_least(pe, ex["y2"], old - 1)
                    for n in range(MC):
                        mm = pe.matmul(bank[6 + par][:, 0:D], hidT[:, par, n, :], w2_t[:, bass.ds(e * (MC * D) + n * D, D)],
                                       start=(n == 0), stop=(n == MC - 1))
                    mm.then_inc(ex["y_pe"], 1)
                if live(prv, BLOCKS):
                    pe.wait_ge(ex["hid"], prv + 1)
                    at_least(pe, ex["hidT"], prv - 1)
                    for n in range(MC):
                        mm = pe.transpose(bank[2 + npar][:, n * 128:n * 128 + 128], hid[:, npar, n * 128:n * 128 + 128],
                                          ident[:])
                    mm.then_inc(ex["t_pe"], 1)

            pe.wait_ge(ro["blocks"], 1)
            staged_slots(pe, BLOCKS, expert)

        @block.scalar
        def _(act):
            with nc.allow_non_contiguous_dma(reason="two 512-byte vectors laid along partitions"):
                for t in range(3):
                    act.dma_start(bq0_col[R1 * t:R1 * t + R1, :], bq0.rearrange("(j r) -> r j", r=R1)).then_inc(g_in, 16)
                    act.dma_start(bk0_col[R1 * t:R1 * t + R1, :], bk0.rearrange("(j r) -> r j", r=R1)).then_inc(g_in, 16)
            act.dma_start(gates[:, 0:2], bcast(g_xattn, 128)).then_inc(g_in, 16)
            act.dma_start(gates[:, 2:4], bcast(g_ffn, 128)).then_inc(g_in, 16)
            act.wait_ge(g_in, 16 * 8)
            act.activation(tg[:], gates[:], ACT.Tanh).then_inc(tanh_set, 1)

            act.wait_ge(prep_pe, 1)
            for w, b_ in ((wq1T, 1), (wk1T, 3)):
                for n in range(2):
                    act.copy(w[:, 4 * n:4 * n + 4, :].rearrange("p c d -> p (c d)"), bank[b_ + n][:]).then_inc(prep_a, 1)
            act.wait_ge(prep_pe, 2)
            for r in range(2):
                for n in range(2):
                    act.mul(kq1[:, 8 * n + r:8 * n + r + 7:2, :],
                            bank[3 + 2 * r + n][:].rearrange("p (h e) -> p h e", h=4), SCALE1).then_inc(prep_a, 1)
            act.wait_ge(prep_pe, 3)
            for n in range(2):
                act.copy(wv1T[:, 4 * n:4 * n + 4, :].rearrange("p c d -> p (c d)"), bank[1 + n][:]).then_inc(prep_a, 1)
            act.wait_ge(prep_pe, 5)
            for r in range(2):
                for n in range(2):
                    act.copy(vo1_hi[:, 8 * n + r:8 * n + r + 7:2, :],
                             bank[(1 + n, (7, 0)[n])[r]][:].rearrange("p (h e) -> p h e", h=4)).then_inc(prep_a, 1)
            act.wait_ge(prep_pe, 6)
            act.copy(upT, bank[3][:].rearrange("p (c d) -> p c d", c=FC)).then_inc(prep_a, 1)
            act.mul(downT, bank[4][:].rearrange("p (c d) -> p c d", c=FC), tg[:, 2:3]).then_inc(prep_a, 1)

            def attn0(it, half, par):
                nxt, far, prv = it + 1, it + 2, it - 1
                npar = 1 - par

                def copy_probs(j):
                    act.wait_ge(a["t_pe"], NB * prv + j + 1)
                    at_least(act, a["pv_pe"], prv)
                    act.copy(prT[:, HB * j:HB * j + HB, :].rearrange("p h l -> p (h l)"), bank[4 + j % 2][0:S, :]
                             ).then_inc(a["prT"], 1)

                def exponent(j):
                    if j in (1, 2):
                        p = sc[:, par, HB * j:HB * j + HB, :]
                        act.wait_ge(a["shifted"], 2 * it + j)
                        act.activation(p, p, ACT.Exp).then_inc(a["exp"], 1)
                    else:
                        act.wait_ge(a["neg_max"], 2 * it + 1 + j // 3)
                        for h in range(HB * j, HB * j + HB):
                            p = sc[:, par, h, :]
                            e = act.activation(p, p, ACT.Exp, bias=neg_max[:, par, h:h + 1],
                                               accum_out=den[:, par, h:h + 1])
                        e.then_inc(a["exp"], 1)

                def spread_k(n):
                    act.wait_ge(a["k_lo"], nxt + 1)
                    at_least(act, a["s_pe"], NB * (nxt - 1))
                    act.mul(k_diag[:, npar].rearrange("p (j n) s -> p n j s", n=HB)[:, n], k_st.bitcast(F32),
                            own_head[0:R3, n:n + 1]).then_inc(a["k_diag"], 1)

                if live(prv, B):
                    copy_probs(0)
                if live(it, B):
                    exponent(0)
                if live(prv, B):
                    copy_probs(1)
                if live(nxt, B):
                    act.wait_ge(a["q_f32"], nxt + 1)
                    at_least(act, a["s_pe"], NB * (nxt - 1))
                    act.copy(q_st[:, npar], q_f32).then_inc(a["q_hi"], 1)
                if live(prv, B):
                    copy_probs(2)
                    copy_probs(3)
                if live(far, B):
                    act.wait_ge(a["xcT_pe"], far + 1)
                    at_least(act, a["v_pe"], far - 1)
                    act.copy(xcT[:, par, :], bank[2][:, 0:L + S]).then_inc(a["xcT"], 1)
                if live(it, B):
                    exponent(1)
                if live(nxt, B):
                    spread_k(0)
                if live(it, B):
                    exponent(2)
                if live(nxt, B):
                    spread_k(1)
                    spread_k(2)
                    spread_k(3)
                if live(it, B):
                    exponent(3)
                if live(far, B):
                    act.wait_ge(a["k_f32"], far + 1)
                    at_least(act, a["k_diag"], HB * far)
                    act.copy(k_st, k_f32).then_inc(a["k_hi"], 1)
                if live(prv, B):
                    act.wait_ge(a["pv_pe"], prv + 1)
                    at_least(act, a["y_pe"], prv)
                    act.copy(o0T[:], bank[6][:, 0:L]).then_inc(a["oT"], 1)
                if live(nxt, B):
                    act.wait_ge(a["v_pe"], nxt + 1)
                    at_least(act, a["pv_pe"], nxt - 1)
                    act.copy(v0_diag[npar], bank[3][0:S, 0:H * HD0].rearrange("s (h d) -> s h d", h=H)
                             ).then_inc(a["v"], 1)

            act.wait_ge(consts_set, 6)
            act.wait_ge(padded, 2)
            staged(act, B, attn0, ahead=3)

            def ffn0(it, half, par):
                nxt, prv = it + 1, it - 1
                npar = 1 - par
                if live(nxt, B):
                    act.wait_ge(f["xT_pe"], nxt + 1)
                    at_least(act, f["up_pe"], nxt - 1)
                    act.copy(xcT[:, npar, 0:L], bank[4 + npar][:, 0:L]).then_inc(f["xT"], 1)
                if live(it, B):
                    act.wait_ge(f["up_pe"], it + 1)
                    at_least(act, f["t_pe"], it - 1)
                    at_least(act, f["sq"], it - 1)
                    act.activation(gel[:, par, :], bank[par][:, 0:F], ACT.Gelu).then_inc(f["gel"], 1)
                if live(prv, B):
                    act.wait_ge(f["t_pe"], prv + 1)
                    at_least(act, f["y_pe"], prv - 1)
                    act.copy(gelT[:, npar, :, :].rearrange("p c l -> p (c l)"), bank[2 + npar][:]).then_inc(f["gelT"], 1)

            staged(act, B, ffn0)

            def attn1(it, half, par):
                nxt, far, prv = it + 1, it + 2, it - 1
                npar = 1 - par

                def copy_probs(j):
                    act.wait_ge(c["p_pe"], NB * prv + j + 1)
                    at_least(act, c["y_pe"], prv)
                    act.copy(prT[:, HB * j:HB * j + HB, :].rearrange("p h l -> p (h l)"), bank[2 + j % 2][0:S, :]
                             ).then_inc(c["prT"], 1)

                def exponent(j):
                    p = sc[:, par, HB * j:HB * j + HB, :]
                    act.wait_ge(c["shifted"], NB * it + j + 1)
                    act.activation(p, p, ACT.Exp).then_inc(c["exp"], 1)

                def high_u(j):
                    act.wait_ge(c["u_pe"], NB * nxt + j + 1)
                    at_least(act, c["s_pe"], NB * (nxt - 2) + j + 1)
                    act.copy(u_hi[:, npar, HB * j:HB * j + HB, :].rearrange("p h s -> p (h s)"),
                             bank[4][:, 0:HB * S]).then_inc(c["u_hi"], 1)

                for j in range(NB):
                    if live(prv, B):
                        copy_probs(j)
                    if live(nxt, B):
                        high_u(j)
                    if live(it, B):
                        exponent(j)
                        act.wait_ge(c["w_pe"], NB * it + j + 1)
                        at_least(act, c["y_pe"], it - 1)
                        act.copy(w_vo[:, par, HB * j:HB * j + HB, :].rearrange("p h n -> p (h n)"), bank[5][0:S, :]
                                 ).then_inc(c["w"], 1)
                if live(far, B):
                    act.wait_ge(c["xcT_pe"], far + 1)
                    act.copy(xcT_hi[:, par, :], bank[6][:, 0:L + S]).then_inc(c["hi"], 1)
                    act.copy(xcT[:, par, L:L + S], bank[6][:, L:L + S]).then_inc(c["hi"], 1)

            staged(act, B, attn1, ahead=2)

            for g in range(B // RG):
                act.wait_ge(ro["xT_pe"], g + 1)
                at_least(act, ro["l_pe"], g - 1)
                act.copy(rowsT[:, g % 2], bank[g % 2][:].rearrange("p (n l) -> p n l", n=RG)).then_inc(ro["xT"], 1)
            act.wait_ge(ro["v"], 2)
            act.activation(route_b[:], route_a[:], ACT.Exp).then_inc(ro["exp"], 1)

            def expert(it, use, slot):
                nxt, prv = it + 1, it - 1
                par = slot % 2
                npar = 1 - par
                if live(nxt, BLOCKS):
                    act.wait_ge(ex["xT_pe"], nxt + 1)
                    at_least(act, ex["up_pe"], nxt - 1)
                    act.copy(rowT[:, npar, :], bank[4 + npar][:, 0:128]).then_inc(ex["xT"], 1)
                if live(prv, BLOCKS):
                    act.wait_ge(ex["t_pe"], prv + 1)
                    at_least(act, ex["y_pe"], prv - 1)
                    act.activation(hidT[:, npar, :, :].rearrange("p c l -> p (c l)"), bank[2 + npar][:], ACT.Relu
                                   ).then_inc(ex["hidT"], 1)

            staged_slots(act, BLOCKS, expert)

        @block.vector
        def _(dve):
            dve.wait_ge(wqk0_in, 32)
            dve.tensor_scalar(wq0_st[:], wq0_raw[:].rearrange("p (j r) -> p j r", j=NB).unsqueeze(2).to_broadcast([D, NB, 3, R1]),
                              SCALE0, None, ALU.mult).then_inc(chained, 1)
            dve.tensor_copy(wk0_st[:], wk0_raw[:].rearrange("p (j r) -> p j r", j=NB).unsqueeze(2).to_broadcast([D, NB, 3, R1])
                            ).then_inc(chained, 1)
            dve.wait_ge(g_in, 16 * 8)
            dve.tensor_scalar(bq0_col[0:R3, :], bq0_col[0:R3, :], SCALE0, None, ALU.mult).then_inc(chained, 1)
            dve.wait_ge(consts_set, 5)
            dve.reduce_sum(own_part[0:R3], ident[0:R3, 0:R3].rearrange("p (t n d) -> p t n d", t=3, n=HB), AX_X
                           ).then_inc(padded, 1)
            dve.wait_ge(padded, 1)
            dve.reduce_sum(own_head[0:R3], own_part[0:R3].rearrange("p t n -> p n t"), AX_X).then_inc(padded, 1)
            dve.wait_ge(tanh_set, 1)
            dve.wait_ge(wvo0_in, 64)
            dve.tensor_scalar(wo0[:], wo0[:], tg[:, 0:1], None, ALU.mult).then_inc(chained, 1)
            dve.tensor_scalar(bo0_row[:], bo0_row[:], tg[0:1, 0:1], None, ALU.mult).then_inc(chained, 1)
            dve.wait_ge(chained, 5)
            dve.sem_inc(weights_set, 1)

            def scales(s, part, rows_done, with_rms):
                lo, hi = PARTS[part]
                me, mo, ve, vo = (stats_all[:, lo:hi, n] for n in (1, 4, 2, 5))
                t = [tmp_all[:, n, lo:hi] for n in range(6)]
                v0_ = 7 * part
                dve.wait_ge(rows_done, hi)
                dve.tensor_tensor(t[0], me, mo, ALU.add).then_inc(s["var"], 1)
                dve.tensor_tensor(t[1], me, mo, ALU.subtract).then_inc(s["var"], 1)
                dve.tensor_tensor(t[2], ve, vo, ALU.add).then_inc(s["var"], 1)
                dve.wait_ge(s["var"], v0_ + 3)
                dve.tensor_scalar(mean_all[:, lo:hi], t[0], 0.5, None, ALU.mult).then_inc(s["var"], 1)
                dve.scalar_tensor_tensor(out=t[1], in0=t[1], scalar=0.25, in1=t[1], op0=ALU.mult, op1=ALU.mult
                                         ).then_inc(s["var"], 1)
                dve.wait_ge(s["var"], v0_ + 5)
                dve.scalar_tensor_tensor(out=t[2], in0=t[2], scalar=1.0 / D, in1=t[1], op0=ALU.mult, op1=ALU.add
                                         ).then_inc(s["var"], 1)
                dve.wait_ge(s["var"], v0_ + 6)
                dve.tensor_scalar(t[3], t[2], LN_EPS, None, ALU.add).then_inc(s["var"], 1)
                if part == 1:
                    t = [tmp_all[:, n, :] for n in range(6)]
                    if not with_rms:
                        dve.wait_ge(s["pow"], 2)
                        dve.tensor_copy(scale_all[:], t[4]).then_inc(s["scale"], 1)
                    else:
                        dve.wait_ge(s["pow"], 4)
                        dve.tensor_tensor(t[0], t[5], t[4], ALU.mult).then_inc(s["scale"], 1)
                        dve.wait_ge(s["scale"], 1)
                        dve.tensor_scalar(t[1], t[0], RMS_EPS, None, ALU.add).then_inc(s["scale"], 1)
                        dve.wait_ge(s["scale"], 2)
                        dve.reciprocal(t[0], t[1]).then_inc(s["scale"], 1)
                        dve.wait_ge(s["scale"], 3)
                        dve.tensor_tensor(scale_all[:], t[0], t[4], ALU.mult).then_inc(s["scale"], 1)

            def seq_rows(k):
                return xs[:, bass.ds(k, 1), :].rearrange("l o d -> l (o d)")

            def normalise_all(k, par, s, transposed):
                at_least(dve, s[transposed], k - 1)
                dve.wait_ge(s["scale"], 4 if s is f else 1)
                dve.tensor_scalar(xn[:, par, :], seq_rows(k), mean_all[:, bass.ds(k, 1)], scale_all[:, bass.ds(k, 1)],
                                  ALU.subtract, ALU.mult).then_inc(s["ln"], 1)

            def stats_of(k, s):
                dve.wait_ge(s["x"], k + 1)
                dve.bn_stats(stats_all[:, bass.ds(k, 1), :].rearrange("l o n -> l (o n)"), seq_rows(k)
                             ).then_inc(s["row_stats"], 1)

            def denominators(it, par, j, s):
                cols = slice(HB * j, HB * j + HB)
                dve.wait_ge(s["exp"], NB * it + j + 1)
                dve.reduce_sum(den[:, par, cols], sc[:, par, cols, :], AX_X).then_inc(s["den"], 1)

            def reciprocals(it, par, j, s, ready):
                cols = slice(HB * j, HB * j + HB)
                dve.wait_ge(*ready)
                dve.reciprocal(rden[:, par, cols], den[:, par, cols]).then_inc(s["rden"], 1)

            def row_stats(it, par, s):
                dve.bn_stats(stats[:], xs[:, bass.ds(it, 1), :].rearrange("l o d -> l (o d)")).then_inc(s["stats"], 1)
                dve.wait_ge(s["stats"], 2 * it + 1)
                dve.memset(settle[:], 0.0)
                dve.bn_aggr(mv[:, par, :], stats[:]).then_inc(s["stats"], 1)

            def normalise(it, par, s, transposed, ready, scale):
                at_least(dve, s[transposed], it - 1)
                dve.wait_ge(s["stats"], 2 * it + 2)
                dve.wait_ge(ready[0], ready[1] * it + ready[1])
                dve.tensor_scalar(xn[:, par, :], xs[:, bass.ds(it, 1), :].rearrange("l o d -> l (o d)"),
                                  mv[:, par, 0:1], scale[:, par:par + 1], ALU.subtract, ALU.mult).then_inc(s["ln"], 1)

            def attn0(it, half, par):
                nxt, far, fur, old = it + 1, it + 2, it + 3, it - 2
                npar = 1 - par

                def add_bias(j):
                    if live(it, B):
                        s = sc[:, par, HB * j:HB * j + HB, :]
                        dve.wait_ge(bias_in[par][j], half * 16 + 16)
                        at_least(dve, a["t_pe"], NB * (it - 2) + j + 1)
                        dve.wait_ge(a["s_pe"], NB * it + j + 1)
                        dve.tensor_tensor(s, bank[j % 2][:, 0:HB * S].rearrange("p (h s) -> p h s", h=HB),
                                          bias_t[:, par, HB * j:HB * j + HB, :], ALU.add).then_inc(a["biased"], 1)
                        dve.wait_ge(a["biased"], NB * it + j + 1)
                        dve.reduce_max(mx[:, par, HB * j:HB * j + HB], s, AX_X).then_inc(a["max"], 1)
                        if j not in (1, 2):
                            cols = slice(HB * j, HB * j + HB)
                            at_least(dve, a["exp"], NB * (it - 2) + j + 1)
                            dve.wait_ge(a["max"], NB * it + j + 1)
                            dve.tensor_scalar(neg_max[:, par, cols], mx[:, par, cols], -1.0, None, ALU.mult
                                              ).then_inc(a["neg_max"], 1)

                def sums(j):
                    if live(it, B):
                        denominators(it, par, j, a)

                def inverses(j):
                    if live(it, B):
                        reciprocals(it, par, j, a, (a["den"], 2 * it + j) if j in (1, 2) else (a["exp"], NB * it + j + 1))

                add_bias(0)
                if live(nxt, B):
                    dve.wait_ge(a["q_pe"], nxt + 1)
                    at_least(dve, a["q_lo"], nxt)
                    dve.tensor_tensor(q_f32, bank[3][0:R3, :].rearrange("p (j l) -> p j l", j=NB),
                                      bq0_col[0:R3, :].unsqueeze(2).to_broadcast([R3, NB, L]), ALU.add).then_inc(a["q_f32"], 1)
                add_bias(1)
                if live(fur, B):
                    dve.wait_ge(x0_in[npar], half * 16 + (32 + 16 * par))
                    row_stats(fur, npar, a)
                add_bias(2)
                add_bias(3)
                inverses(0)
                sums(1)
                if live(nxt, B):
                    additive_mask(nxt, half + par, npar)
                inverses(1)
                sums(2)
                if live(fur, B):
                    normalise(fur, npar, a, "xcT_pe", (a["rstd"], 2), rstd)
                inverses(2)
                if live(old, B):
                    dve.wait_ge(a["y_pe"], old + 1)
                    dve.tensor_tensor(seq_rows(old), bank[7][:, 0:D], seq_rows(old), ALU.add).then_inc(a["x"], 1)
                if live(far, B):
                    dve.wait_ge(a["k_pe"], far + 1)
                    at_least(dve, a["k_lo"], far)
                    dve.tensor_tensor(k_f32, bank[2][0:R3, 0:NB * S].rearrange("p (j s) -> p j s", j=NB),
                                      bk0_col[0:R3, :].unsqueeze(2).to_broadcast([R3, NB, S]), ALU.add).then_inc(a["k_f32"], 1)
                if live(old, B):
                    stats_of(old, a)
                inverses(3)
                if isinstance(it, int) and it == PART_STEP:
                    scales(f, 0, a["row_stats"], True)

            def additive_mask(it, half, par):
                at_least(dve, a["s_pe"], NB * (it - 1))
                dve.wait_ge(mask_in[par], half * 16 + 16)
                dve.tensor_scalar(mask_b[:, par, :], mask_i[:, par, :], 0.0, MASKED, ALU.is_equal, ALU.mult
                                  ).then_inc(a["mask"], 1)

            dve.wait_ge(x0_in[0], 16)
            row_stats(0, 0, a)
            normalise(0, 0, a, "xcT_pe", (a["rstd"], 2), rstd)

            dve.wait_ge(w_in, 32)
            for m, (w, t) in enumerate(((up_raw, tern_a), (down_raw, tern_b))):
                dve.scalar_tensor_tensor(out=t, in0=w, scalar=-1.0, in1=w, op0=ALU.mult, op1=ALU.max
                                         ).then_inc(padded, 1)
                dve.wait_ge(padded, 3 + m)
                dve.reduce_sum(absum[:, :, m], t, AX_X).then_inc(absum_set, 1)
            dve.wait_ge(wvo1_in, 32)
            dve.tensor_scalar(wo1[:], wo1[:], tg[:, 1:2], None, ALU.mult).then_inc(wo1_set, 1)
            dve.wait_ge(prep_pe, 4)
            dve.tensor_scalar(thr[:, 0:2], bank[0][:, 0:2], 0.5 / (F * D), None, ALU.mult).then_inc(weights_set, 1)
            dve.tensor_scalar(thr[:, 2:4], bank[0][:, 0:2], -0.5 / (F * D), None, ALU.mult).then_inc(weights_set, 1)
            dve.wait_ge(weights_set, 3)
            for m, (w, t) in enumerate(((up_raw, tern_a), (down_raw, tern_b))):
                below = gelT[:, m, :, :]
                dve.tensor_scalar(t, w, thr[:, m:m + 1], None, ALU.is_gt).then_inc(tern_set, 1)
                dve.tensor_scalar(below, w, thr[:, 2 + m:3 + m], None, ALU.is_lt).then_inc(tern_set, 1)
                dve.wait_ge(tern_set, 2 + 4 * m)
                dve.tensor_tensor(t, t, below, ALU.subtract).then_inc(tern_set, 1)
                dve.wait_ge(tern_set, 3 + 4 * m)
                dve.tensor_tensor(t, t, w, ALU.subtract).then_inc(tern_set, 1)
                dve.wait_ge(tern_set, 4 + 4 * m)
                dve.tensor_tensor(t, t, w, ALU.add).then_inc(prep_v, 1)
            for k, (r, n) in enumerate(((0, 0), (0, 1), (1, 0), (1, 1))):
                dve.wait_ge(prep_a, 11 + k)
                cols = slice(8 * n + r, 8 * n + r + 7, 2)
                dve.tensor_tensor(vo1_lo[:, cols, :], bank[(1 + n, (7, 0)[n])[r]][:].rearrange("p (h e) -> p h e", h=4),
                                  vo1_hi[:, cols, :].bitcast(F32), ALU.subtract).then_inc(prep_v, 1)

            staged(dve, B, attn0, ahead=3)

            scales(f, 1, a["row_stats"], True)

            def ffn0(it, half, par):
                far, prv, old = it + 2, it - 1, it - 2
                npar = 1 - par
                if live(far, B):
                    normalise_all(far, par, f, "xT_pe")
                if live(old, B):
                    dve.wait_ge(f["rms"], old + 1)
                    at_least(dve, f["rrms"], old)
                    dve.tensor_scalar(rms_eps[:], rms[:, par:par + 1], RMS_EPS, None, ALU.add).then_inc(f["eps"], 1)
                    dve.wait_ge(f["eps"], old + 1)
                    at_least(dve, f["x"], old)
                    dve.reciprocal(rrms[:], rms_eps[:]).then_inc(f["rrms"], 1)
                if live(prv, B):
                    dve.wait_ge(f["gel"], prv + 1)
                    at_least(dve, f["rms"], prv - 1)
                    dve.tensor_tensor_reduce(out=gel2[:], in0=gel[:, npar, :], in1=gel[:, npar, :], scale=1.0 / F, scalar=0.0,
                                             op0=ALU.mult, op1=ALU.add, accum_out=ssq[:, npar:npar + 1]).then_inc(f["sq"], 1)
                if live(old, B):
                    dve.wait_ge(f["rrms"], old + 1)
                    dve.wait_ge(f["y_pe"], old + 1)
                    dve.scalar_tensor_tensor(out=seq_rows(old), in0=bank[6 + par][:, 0:D], scalar=rrms[:],
                                             in1=seq_rows(old), op0=ALU.mult, op1=ALU.add).then_inc(f["x"], 1)
                    stats_of(old, f)
                if isinstance(it, int) and it == PART_STEP:
                    scales(c, 0, f["row_stats"], False)

            normalise_all(0, 0, f, "xT_pe")
            staged(dve, B, ffn0)

            scales(c, 1, f["row_stats"], False)

            def attn1(it, half, par):
                nxt, far, old = it + 1, it + 2, it - 2
                npar = 1 - par

                def shift(j):
                    s = bank[j % 2][:, 0:HB * S].rearrange("p (h s) -> p h s", h=HB)
                    m = mx[:, par, HB * j:HB * j + HB]
                    dve.wait_ge(c["s_pe"], NB * it + j + 1)
                    dve.reduce_max(m, s, AX_X).then_inc(c["max"], 1)
                    at_least(dve, c["p_pe"], NB * (it - 2) + j + 1)
                    dve.wait_ge(c["max"], NB * it + j + 1)
                    dve.tensor_tensor(sc[:, par, HB * j:HB * j + HB, :], s, m.unsqueeze(2).to_broadcast([L, HB, S]),
                                      ALU.subtract).then_inc(c["shifted"], 1)

                def low_u(j):
                    cols = slice(HB * j, HB * j + HB)
                    dve.wait_ge(c["u_hi"], NB * nxt + j + 1)
                    dve.tensor_tensor(u_lo[:, npar, cols, :].rearrange("p h s -> p (h s)"), bank[4][:, 0:HB * S],
                                      u_hi[:, npar, cols, :].rearrange("p h s -> p (h s)").bitcast(F32), ALU.subtract
                                      ).then_inc(c["u"], 1)

                if live(far, B):
                    normalise_all(far, par, c, "xcT_pe")
                for j in range(NB):
                    if live(it, B):
                        shift(j)
                        if j:
                            denominators(it, par, j - 1, c)
                    if live(nxt, B):
                        low_u(j)
                    if live(it, B) and j:
                        reciprocals(it, par, j - 1, c, (c["den"], NB * it + j))
                    if j == 0 and live(old, B):
                        dve.wait_ge(c["y_pe"], old + 1)
                        dve.tensor_tensor(seq_rows(old), bank[7][:, 0:D], seq_rows(old), ALU.add).then_inc(c["x"], 1)
                    if j == 1 and live(old, B):
                        stats_of(old, c)
                if live(it, B):
                    denominators(it, par, NB - 1, c)
                    reciprocals(it, par, NB - 1, c, (c["den"], NB * it + NB))
                if live(far, B):
                    dve.wait_ge(c["hi"], 2 * far + 2)
                    dve.tensor_tensor(xcT_lo[:, par, :], bank[6][:, 0:L + S], xcT_hi[:, par, :].bitcast(F32),
                                      ALU.subtract).then_inc(c["lo"], 1)
                if isinstance(it, int) and it == PART_STEP:
                    scales(ro, 0, c["row_stats"], False)

            staged(dve, B, attn1, ahead=2)

            scales(ro, 1, c["row_stats"], False)

            dve.wait_ge(ro["scale"], 1)
            for g in range(B // RG + 2):
                if live(g, B // RG):
                    for b in range(RG * g, RG * g + RG):
                        dve.tensor_scalar(rec[:, b, 0:D], xs[:, b, :], mean_all[:, b:b + 1], scale_all[:, b:b + 1],
                                          ALU.subtract, ALU.mult).then_inc(ro["rec"], 1)
                if g >= 2:
                    dve.wait_ge(ro["l_pe"], g - 1)
                    dve.tensor_tensor(logits[:, RG * (g - 2):RG * (g - 1), :],
                                      bank[2 + g % 2][:, 0:RG * E].rearrange("l (n e) -> l n e", n=RG),
                                      bg_bc[:].unsqueeze(1).to_broadcast([L, RG, E]), ALU.add).then_inc(ro["logits"], 1)

            best, total, first, at = (pick[:, n, :] for n in range(4))
            dve.wait_ge(ro["logits"], B // RG)
            dve.reduce_max(best, logits[:], AX_X).then_inc(ro["v"], 1)
            dve.wait_ge(ro["v"], 1)
            dve.tensor_tensor(route_a[:], logits[:], best.unsqueeze(2).to_broadcast([L, B, E]), ALU.subtract
                              ).then_inc(ro["v"], 1)
            dve.wait_ge(ro["exp"], 1)
            dve.reduce_sum(total, route_b[:], AX_X).then_inc(ro["v"], 1)
            dve.tensor_scalar(route_a[:], route_a[:], 0.0, float(E), ALU.is_lt, ALU.mult).then_inc(ro["v"], 1)
            dve.wait_ge(ro["v"], 4)
            dve.tensor_tensor(route_a[:], route_a[:], experts[:], ALU.add).then_inc(ro["v"], 1)
            dve.wait_ge(ro["v"], 5)
            dve.tensor_reduce(first, route_a[:], AX_X, ALU.min).then_inc(ro["v"], 1)
            dve.wait_ge(ro["v"], 6)
            dve.tensor_tensor(onehot[:], experts[:], first.unsqueeze(2).to_broadcast([L, B, E]), ALU.is_equal
                              ).then_inc(chained, 1)
            dve.wait_ge(chained, 6)
            dve.wait_ge(ro["tables"], 11)
            dve.tensor_copy(before_bf[:], before[:]).then_inc(chained, 1)
            dve.tensor_copy(onehot_bf[:], onehot[:].rearrange("l b e -> l e b")).then_inc(ro["v"], 1)
            dve.wait_ge(chained, 7)
            dve.reciprocal(at, total).then_inc(chained, 1)
            dve.wait_ge(chained, 8)
            dve.tensor_scalar(rec[:, :, GATE:TOKEN], at.unsqueeze(2), tg[:, 3:4], None, ALU.mult).then_inc(ro["rec"], 1)
            dve.wait_ge(ro["pe"], 1)
            dve.tensor_copy(seq_count[:], bank[4][0:B, 0:E]).then_inc(ro["v"], 1)
            dve.wait_ge(ro["v"], 8)
            dve.tensor_tensor(seq_before[:], before[0:B, 0:B].unsqueeze(2).to_broadcast([B, B, E]),
                              seq_count[:].unsqueeze(1).to_broadcast([B, B, E]), ALU.mult).then_inc(ro["v"], 1)
            n_blocks, start, end, base = (blocks_of[:, n, :] for n in range(4))
            dve.wait_ge(ro["pe"], 2)
            dve.tensor_tensor(above[:], bank[6][:, 0:E].unsqueeze(2).to_broadcast([128, E, B]),
                              block_rows[:].unsqueeze(1).to_broadcast([128, E, B]), ALU.is_gt).then_inc(chained, 1)
            dve.wait_ge(chained, 9)
            dve.reduce_sum(n_blocks, above[:], AX_X).then_inc(chained, 1)
            dve.wait_ge(chained, 10)
            dve.tensor_tensor(above[:, :, 0:E], before_e[:], n_blocks.unsqueeze(1).to_broadcast([128, E, E]), ALU.mult
                              ).then_inc(chained, 1)
            dve.wait_ge(chained, 11)
            dve.reduce_sum(start, above[:, :, 0:E], AX_X).then_inc(chained, 1)
            dve.wait_ge(chained, 12)
            dve.tensor_tensor(end, start, n_blocks, ALU.add).then_inc(chained, 1)
            dve.tensor_scalar(base, start, 128.0, None, ALU.mult).then_inc(chained, 1)
            dve.wait_ge(chained, 14)
            dve.tensor_tensor(route_a[:], bank[5][:, 0:B * E].rearrange("p (e b) -> p b e", e=E),
                              base.unsqueeze(1).to_broadcast([L, B, E]), ALU.add).then_inc(chained, 1)
            dve.wait_ge(chained, 15)
            dve.tensor_tensor(route_a[:], route_a[:], onehot[:], ALU.mult).then_inc(chained, 1)
            dve.wait_ge(chained, 16)
            dve.reduce_sum(best, route_a[:], AX_X).then_inc(chained, 1)
            dve.wait_ge(chained, 17)
            dve.tensor_copy(place[:], best).then_inc(ro["place"], 1)
            dve.tensor_tensor(block_cmp[:], block_no[:].unsqueeze(2).to_broadcast([1, BLOCKS, E]),
                              end[0:1, :].unsqueeze(1).to_broadcast([1, BLOCKS, E]), ALU.is_ge).then_inc(chained, 1)
            dve.wait_ge(chained, 18)
            dve.reduce_sum(block_f[:], block_cmp[:], AX_X).then_inc(chained, 1)
            dve.wait_ge(chained, 19)
            dve.tensor_scalar(block_e[:], block_f[:], float(E - 1), None, ALU.min).then_inc(ro["blocks"], 1)

            def expert(it, use, slot):
                old = it - 2
                par = slot % 2
                oslot = (slot + 2) % 4
                if live(it, BLOCKS):
                    e = dve.value_load(block_e[0:1, bass.ds(it, 1)], min_val=0, max_val=E - 1)
                    dve.wait_ge(ex["up_pe"], it + 1)
                    at_least(dve, ex["t_pe"], it - 1)
                    dve.tensor_tensor(hid[:, par, :], bank[par][:, 0:M],
                                      b1_bc[:, bass.ds(e, 1), :].rearrange("p o m -> p (o m)"), ALU.add).then_inc(ex["hid"], 1)
                if live(old, BLOCKS):
                    e = dve.value_load(block_e[0:1, bass.ds(old, 1)], min_val=0, max_val=E - 1)
                    dve.wait_ge(ex["y_pe"], old + 1)
                    at_least(dve, ex["y"], old - 1)
                    dve.tensor_tensor(y2[:, par, :], bank[6 + par][:, 0:D],
                                      b2_bc[:, bass.ds(e, 1), :].rearrange("p o d -> p (o d)"), ALU.add).then_inc(ex["y2"], 1)
                    dve.wait_ge(x_in[oslot], (use + (slot - 2) // 4) * 16 + 16)
                    dve.wait_ge(ex["y2"], old + 1)
                    dve.scalar_tensor_tensor(out=y_out[:, oslot, :], in0=y2[:, par, :], scalar=rows_x[:, oslot, GATE - D:TOKEN - D],
                                             in1=rows_x[:, oslot, 0:D], op0=ALU.mult, op1=ALU.add).then_inc(ex["y"], 1)

            dve.wait_ge(ro["blocks"], 1)
            dve.wait_ge(late_in, 16 * 6)
            staged_slots(dve, BLOCKS, expert)


_INS = ['x', 'ctx_1024', 'fside_Bx16xSxS2_0', 'mask_Bx1xSxS2_ik1', 'g_xattn', 'g_ffn', 'L0_xattn_Wq', 'L0_xattn_bq',
        'L0_xattn_Wk', 'L0_xattn_bk', 'L0_xattn_Wv', 'L0_xattn_bv', 'L0_xattn_Wo', 'L0_xattn_bo', 'L0_ffn_w_up',
        'L0_ffn_w_down', 'L1_xattn_Wq', 'L1_xattn_Wk', 'L1_xattn_Wv', 'L1_xattn_Wo', 'L1_ffn_w_gate', 'L1_ffn_b_gate',
        'L1_ffn_W1', 'L1_ffn_b1', 'L1_ffn_W2', 'L1_ffn_b2']


def kernel(**inputs):
    import numpy as np
    import concourse.bacc as bacc
    from concourse.bass_utils import run_bass_kernel_spmd

    nc = bacc.Bacc("TRN2", target_bir_lowering=False, num_devices=1)
    arrays, args = {}, []
    for name in _INS:
        arr = np.ascontiguousarray(inputs[name])
        arrays[f"in_{name}"] = arr
        args.append(nc.dram_tensor(f"in_{name}", arr.shape, mybir.dt.from_np(arr.dtype), kind="ExternalInput").ap())
    out = nc.dram_tensor("out_x", inputs["x"].shape, F32, kind="ExternalOutput").ap()
    build(nc, *args, out)
    r = run_bass_kernel_spmd(nc, [arrays], core_ids=[0])
    return r.results[0]["out_x"]
```
